# Optimizing a Trainium2 kernel written in Bass

```python
import numpy as np
import jax
import jax.numpy as jnp

def _softmax(x, axis=-1):
    return jax.nn.softmax(x, axis=axis)

def _gelu(x):
    return jax.nn.gelu(x, approximate=True)

def _silu(x):
    return jax.nn.silu(x)

def _sigmoid(x):
    return jax.nn.sigmoid(x)

def _layernorm(x, axis=-1, eps=1e-05):
    m = jnp.mean(x, axis=axis, keepdims=True)
    v = jnp.var(x, axis=axis, keepdims=True)
    return (x - m) / jnp.sqrt(v + eps)

def _scatter_add(tgt, idx, src, axis=0):
    return tgt.at[idx].add(src)

def _segment_sum(src, seg, n):
    return jax.ops.segment_sum(src, seg, n)
kernel_name = 'mk_prb_d2_jaxref_r4_e73904'

def setup_inputs(seed: int=0):
    np.random.seed(seed)
    _w = jnp.asarray

    def _L0_attn_setup():
        import jax, jax.numpy as jnp
        import numpy as np
        DIMS, HEAD = (256, 16)
        HD = DIMS // HEAD
        MAX_ITER = 3
        B, T = (4, 512)

        def _ln(x, w, eps=1e-05):
            m = jnp.mean(x, axis=-1, keepdims=True)
            v = jnp.var(x, axis=-1, keepdims=True)
            return (x - m) * jax.lax.rsqrt(v + eps) * w
        key = jax.random.key(seed)
        ks = jax.random.split(key, 10)
        n = lambda k, s: jax.random.normal(k, s, jnp.float32) * 0.02
        z = lambda s: jnp.zeros(s, jnp.float32)
        o = lambda s: jnp.ones(s, jnp.float32)
        return {'x': jax.random.normal(ks[0], (B, T, DIMS), jnp.float32), 'Wq': n(ks[1], (DIMS, DIMS)), 'bq': z((DIMS,)), 'Wk': n(ks[2], (DIMS, DIMS)), 'Wv': n(ks[3], (DIMS, DIMS)), 'bv': z((DIMS,)), 'Wo': n(ks[4], (DIMS, DIMS)), 'bo': z((DIMS,)), 'lna_w': o((DIMS,)), 'lnc_w': o((HD,)), 'lnd_w': o((HD,)), 'Wlq': n(ks[5], (HD, HD)), 'blq': z((HD,)), 'Wlk': n(ks[6], (HD, HD)), 'blk': z((HD,)), 'Wlv': n(ks[7], (HD, HD)), 'blv': z((HD,)), 'temp': jnp.float32(1.0), 'threshold': jnp.float32(0.01), 'factor': jnp.float32(0.1)}
    _L0_attn_in = _L0_attn_setup()

    def _L0_ffn_setup():
        import jax, jax.numpy as jnp
        import numpy as np
        ALPHA = 1.0
        key = jax.random.key(seed)
        ks = jax.random.split(key, 7)
        B, S, IN, OUT = (8, 2048, 256, 256)
        RANK, DDIM, UDIM = (4, 100, 50)
        return {'hidden_states': jax.random.normal(ks[0], (B, S, IN), dtype=jnp.float32), 'W': jax.random.normal(ks[1], (OUT, IN), dtype=jnp.float32) * 0.02, 'b': jax.random.normal(ks[2], (OUT,), dtype=jnp.float32) * 0.02, 'lora_down': jax.random.normal(ks[3], (RANK, DDIM), dtype=jnp.float32) * 0.1, 'lora_up': jax.random.normal(ks[4], (UDIM, RANK), dtype=jnp.float32) * 0.1, 'down_aux': jax.random.normal(ks[5], (DDIM, IN), dtype=jnp.float32) * 0.03, 'up_aux': jax.random.normal(ks[6], (OUT, UDIM), dtype=jnp.float32) * 0.03}
    _L0_ffn_in = _L0_ffn_setup()

    def _L1_attn_setup():
        import jax, jax.numpy as jnp
        import numpy as np
        B, T, C = (2, 512, 256)
        NH = 16
        HD = C // NH

        def build_alibi_bias(n_head, max_len):
            slopes = jnp.arange(1, n_head + 1, dtype=jnp.float32) / n_head
            ar = jnp.arange(max_len, dtype=jnp.float32)
            return slopes[:, None, None] * (ar[None, None, :] - ar[None, :, None])
        key = jax.random.key(seed)
        ks = jax.random.split(key, 7)
        s = 0.02
        return {'x': jax.random.normal(ks[0], (B, T, C), dtype=jnp.float32), 'q_w': jax.random.normal(ks[1], (C, C), dtype=jnp.float32) * s, 'q_b': jnp.zeros((C,), dtype=jnp.float32), 'kv_w': jax.random.normal(ks[2], (C, 2 * C), dtype=jnp.float32) * s, 'kv_b': jnp.zeros((2 * C,), dtype=jnp.float32), 'o_w': jax.random.normal(ks[3], (C, C), dtype=jnp.float32) * s, 'o_b': jnp.zeros((C,), dtype=jnp.float32)}
    _L1_attn_in = _L1_attn_setup()

    def _L1_ffn_setup():
        import jax, jax.numpy as jnp
        import numpy as np
        DIM = 256

        def _reference_tuple_inner(x, W_r, W_k, W_v, mu_r, mu_k):
            B, T, C = x.shape
            x_prev = jnp.concatenate([jnp.zeros((B, 1, C), x.dtype), x[:, :-1, :]], axis=1)
            xr = mu_r * x + (1.0 - mu_r) * x_prev
            xk = mu_k * x + (1.0 - mu_k) * x_prev
            r = jax.nn.sigmoid(jnp.einsum('btc,dc->btd', xr, W_r))
            k = jnp.einsum('btc,dc->btd', xk, W_k)
            k_act = jnp.square(jax.nn.relu(k))
            out = r * jnp.einsum('btc,dc->btd', k_act, W_v)
            new_state = x[:, -1, :]
            return (out, new_state)
        key = jax.random.key(seed)
        ks = jax.random.split(key, 6)
        B, T, C = (8, 512, DIM)
        x = jax.random.normal(ks[0], (B, T, C), dtype=jnp.float32)
        s = 1.0 / np.sqrt(C)
        W_r = jax.random.uniform(ks[1], (C, C), jnp.float32, -s, s)
        W_k = jax.random.uniform(ks[2], (C, C), jnp.float32, -s, s)
        W_v = jax.random.uniform(ks[3], (C, C), jnp.float32, -s, s)
        mu_r = jax.random.uniform(ks[4], (C,), jnp.float32)
        mu_k = jax.random.uniform(ks[5], (C,), jnp.float32)
        return {'x': x, 'W_r': W_r, 'W_k': W_k, 'W_v': W_v, 'mu_r': mu_r, 'mu_k': mu_k}
    _L1_ffn_in = _L1_ffn_setup()
    _d = {'L0_attn_x': _L0_attn_in['x'], 'L0_attn_Wq': _L0_attn_in['Wq'], 'L0_attn_bq': _L0_attn_in['bq'], 'L0_attn_Wk': _L0_attn_in['Wk'], 'L0_attn_Wv': _L0_attn_in['Wv'], 'L0_attn_bv': _L0_attn_in['bv'], 'L0_attn_Wo': _L0_attn_in['Wo'], 'L0_attn_bo': _L0_attn_in['bo'], 'L0_attn_lna_w': _L0_attn_in['lna_w'], 'L0_attn_lnc_w': _L0_attn_in['lnc_w'], 'L0_attn_lnd_w': _L0_attn_in['lnd_w'], 'L0_attn_Wlq': _L0_attn_in['Wlq'], 'L0_attn_blq': _L0_attn_in['blq'], 'L0_attn_Wlk': _L0_attn_in['Wlk'], 'L0_attn_blk': _L0_attn_in['blk'], 'L0_attn_Wlv': _L0_attn_in['Wlv'], 'L0_attn_blv': _L0_attn_in['blv'], 'L0_attn_temp': _L0_attn_in['temp'], 'L0_attn_threshold': _L0_attn_in['threshold'], 'L0_attn_factor': _L0_attn_in['factor'], 'L0_ffn_W': _L0_ffn_in['W'], 'L0_ffn_b': _L0_ffn_in['b'], 'L0_ffn_lora_down': _L0_ffn_in['lora_down'], 'L0_ffn_lora_up': _L0_ffn_in['lora_up'], 'L0_ffn_down_aux': _L0_ffn_in['down_aux'], 'L0_ffn_up_aux': _L0_ffn_in['up_aux'], 'L1_attn_q_w': _L1_attn_in['q_w'], 'L1_attn_q_b': _L1_attn_in['q_b'], 'L1_attn_kv_w': _L1_attn_in['kv_w'], 'L1_attn_kv_b': _L1_attn_in['kv_b'], 'L1_attn_o_w': _L1_attn_in['o_w'], 'L1_attn_o_b': _L1_attn_in['o_b'], 'L1_ffn_W_r': _L1_ffn_in['W_r'], 'L1_ffn_W_k': _L1_ffn_in['W_k'], 'L1_ffn_W_v': _L1_ffn_in['W_v'], 'L1_ffn_mu_r': _L1_ffn_in['mu_r'], 'L1_ffn_mu_k': _L1_ffn_in['mu_k']}
    _x0 = _d['L0_attn_x']
    _d['L0_attn_x'] = jax.random.normal(jax.random.fold_in(jax.random.key(seed), 1), (16, 1024, 256), dtype=_x0.dtype)
    del _x0
    return _d

def reference(L0_attn_x, L0_attn_Wq, L0_attn_bq, L0_attn_Wk, L0_attn_Wv, L0_attn_bv, L0_attn_Wo, L0_attn_bo, L0_attn_lna_w, L0_attn_lnc_w, L0_attn_lnd_w, L0_attn_Wlq, L0_attn_blq, L0_attn_Wlk, L0_attn_blk, L0_attn_Wlv, L0_attn_blv, L0_attn_temp, L0_attn_threshold, L0_attn_factor, L0_ffn_W, L0_ffn_b, L0_ffn_lora_down, L0_ffn_lora_up, L0_ffn_down_aux, L0_ffn_up_aux, L1_attn_q_w, L1_attn_q_b, L1_attn_kv_w, L1_attn_kv_b, L1_attn_o_w, L1_attn_o_b, L1_ffn_W_r, L1_ffn_W_k, L1_ffn_W_v, L1_ffn_mu_r, L1_ffn_mu_k):

    def _L0_attn_ref(x, Wq, bq, Wk, Wv, bv, Wo, bo, lna_w, lnc_w, lnd_w, Wlq, blq, Wlk, blk, Wlv, blv, temp, threshold, factor):
        import jax, jax.numpy as jnp
        import numpy as np
        DIMS, HEAD = (256, 16)
        HD = DIMS // HEAD
        MAX_ITER = 3
        B, T = (4, 512)

        def _ln(x, w, eps=1e-05):
            m = jnp.mean(x, axis=-1, keepdims=True)
            v = jnp.var(x, axis=-1, keepdims=True)
            return (x - m) * jax.lax.rsqrt(v + eps) * w
        Bn, Tn, D = x.shape
        H, hd = (HEAD, HD)
        temp0 = jax.lax.stop_gradient(temp)
        thr = jax.lax.stop_gradient(threshold)
        fac = jax.lax.stop_gradient(factor)
        scale = hd ** (-0.25)
        xn = _ln(x, lna_w)
        q = (xn @ Wq.T + bq) * scale
        k = xn @ Wk.T * scale
        v = xn @ Wv.T + bv
        shp = lambda t: t.reshape(Bn, Tn, H, hd).transpose(0, 2, 1, 3)
        q, k, v = (shp(q), shp(k), shp(v))
        E = H
        sm_scale = 1.0 / float(np.sqrt(hd))
        qcur, kcur, vcur = (q, k, v)
        prev = jnp.zeros_like(q)
        attn_out = jnp.zeros_like(q)
        done = jnp.asarray(False)
        for it in range(MAX_ITER):
            ql = qcur[:, :, :E] @ Wlq.T + blq
            kl = kcur[:, :, :E] @ Wlk.T + blk
            vl = vcur[:, :, :E] @ Wlv.T + blv
            t_it = temp0 + 0.005 * it
            tscale = jnp.where((t_it != 1.0) & (t_it > 0), jax.lax.rsqrt(t_it), 1.0)
            qs = _ln(ql, lnc_w) * tscale
            ks_ = _ln(kl, lnd_w)
            logits = jnp.einsum('bhqd,bhkd->bhqk', qs, ks_) * sm_scale
            ai = jnp.einsum('bhqk,bhkd->bhqd', jax.nn.softmax(logits, axis=-1), vl)
            iter_out = jnp.zeros_like(qcur).at[:, :, :E].set(ai)
            diff = jnp.mean(jnp.abs(iter_out - prev))
            attn_out = jnp.where(done, attn_out, iter_out)
            done = done | (diff < thr + fac * diff) & (it > 0)
            prev = iter_out
            qcur = qcur + iter_out
            kcur, vcur = (kl, vl)
        out = attn_out.transpose(0, 2, 1, 3).reshape(Bn, Tn, D)
        return out @ Wo.T + bo

    def _L0_ffn_ref(hidden_states, W, b, lora_down, lora_up, down_aux, up_aux):
        import jax, jax.numpy as jnp
        import numpy as np
        ALPHA = 1.0
        lilora_weight = up_aux @ (lora_up @ (lora_down @ down_aux))
        base = jnp.einsum('bsi,oi->bso', hidden_states, W) + b
        delta = jnp.einsum('bsi,oi->bso', hidden_states, lilora_weight)
        return base + ALPHA * delta

    def _L1_attn_ref(x, q_w, q_b, kv_w, kv_b, o_w, o_b):
        import jax, jax.numpy as jnp
        import numpy as np
        B, T, C = (2, 512, 256)
        NH = 16
        HD = C // NH

        def build_alibi_bias(n_head, max_len):
            slopes = jnp.arange(1, n_head + 1, dtype=jnp.float32) / n_head
            ar = jnp.arange(max_len, dtype=jnp.float32)
            return slopes[:, None, None] * (ar[None, None, :] - ar[None, :, None])
        Bx, Tx, Cx = x.shape
        q = (x @ q_w + q_b).reshape(Bx, Tx, NH, HD).transpose(0, 2, 1, 3)
        kv = (x @ kv_w + kv_b).reshape(Bx, Tx, 2, NH, HD).transpose(2, 0, 3, 1, 4)
        k, v = (kv[0], kv[1])
        att = jnp.einsum('bhqd,bhkd->bhqk', q, k) * (1.0 / np.sqrt(HD))
        att = att + build_alibi_bias(NH, Tx)[None]
        causal = jnp.tril(jnp.ones((Tx, Tx), dtype=bool))
        att = jnp.where(causal[None, None], att, -jnp.inf)
        att = jax.nn.softmax(att, axis=-1)
        y = jnp.einsum('bhqk,bhkd->bhqd', att, v)
        y = y.transpose(0, 2, 1, 3).reshape(Bx, Tx, Cx)
        return y @ o_w + o_b

    def _L1_ffn_ref(x, W_r, W_k, W_v, mu_r, mu_k):
        import jax, jax.numpy as jnp
        import numpy as np
        DIM = 256

        def _reference_tuple_inner(x, W_r, W_k, W_v, mu_r, mu_k):
            B, T, C = x.shape
            x_prev = jnp.concatenate([jnp.zeros((B, 1, C), x.dtype), x[:, :-1, :]], axis=1)
            xr = mu_r * x + (1.0 - mu_r) * x_prev
            xk = mu_k * x + (1.0 - mu_k) * x_prev
            r = jax.nn.sigmoid(jnp.einsum('btc,dc->btd', xr, W_r))
            k = jnp.einsum('btc,dc->btd', xk, W_k)
            k_act = jnp.square(jax.nn.relu(k))
            out = r * jnp.einsum('btc,dc->btd', k_act, W_v)
            new_state = x[:, -1, :]
            return (out, new_state)
        return _reference_tuple_inner(x, W_r, W_k, W_v, mu_r, mu_k)[0]
    x = L0_attn_x
    xn = _layernorm(x, axis=-1)
    x = x + _L0_attn_ref(xn, L0_attn_Wq, L0_attn_bq, L0_attn_Wk, L0_attn_Wv, L0_attn_bv, L0_attn_Wo, L0_attn_bo, L0_attn_lna_w, L0_attn_lnc_w, L0_attn_lnd_w, L0_attn_Wlq, L0_attn_blq, L0_attn_Wlk, L0_attn_blk, L0_attn_Wlv, L0_attn_blv, L0_attn_temp, L0_attn_threshold, L0_attn_factor) + _L0_ffn_ref(xn, L0_ffn_W, L0_ffn_b, L0_ffn_lora_down, L0_ffn_lora_up, L0_ffn_down_aux, L0_ffn_up_aux)
    xn = _layernorm(x, axis=-1)
    x = x + _L1_attn_ref(xn, L1_attn_q_w, L1_attn_q_b, L1_attn_kv_w, L1_attn_kv_b, L1_attn_o_w, L1_attn_o_b) + _L1_ffn_ref(xn, L1_ffn_W_r, L1_ffn_W_k, L1_ffn_W_v, L1_ffn_mu_r, L1_ffn_mu_k)
    return x

_drawn_inputs = setup_inputs


def setup_inputs(seed=0):
    import zlib

    import numpy as np

    out = dict(_drawn_inputs(seed))
    spreads = {'L0_attn_bq': (0.0, 2.0),
     'L0_attn_bv': (0.0, 2.0),
     'L0_attn_bo': (0.0, 0.1),
     'L0_attn_lna_w': (1.0, 0.6),
     'L0_attn_lnc_w': (1.0, 0.6),
     'L0_attn_lnd_w': (1.0, 0.6),
     'L0_attn_blq': (0.0, 2.0),
     'L0_attn_blk': (0.0, 0.8),
     'L0_attn_blv': (0.0, 0.8),
     'L1_attn_q_b': (0.0, 2.0),
     'L1_attn_kv_b': (0.0, 0.489),
     'L1_attn_o_b': (0.0, 0.1)}
    factors = {'L0_attn_Wq': 21.485,
     'L0_attn_Wk': 8.0,
     'L0_attn_Wv': 8.0,
     'L0_attn_Wo': 8.0,
     'L0_attn_Wlq': 8.0,
     'L0_attn_Wlk': 8.0,
     'L0_attn_Wlv': 8.0,
     'L0_ffn_b': 2.912,
     'L0_ffn_lora_down': 2.996,
     'L0_ffn_lora_up': 3.357,
     'L0_ffn_down_aux': 3.134,
     'L0_ffn_up_aux': 3.105,
     'L1_attn_q_w': 32.129,
     'L1_ffn_W_r': 3.331,
     'L1_ffn_mu_r': 6.759}
    for name, (base, spread) in spreads.items():
        noise = np.random.default_rng([zlib.crc32(name.encode()), seed]).standard_normal(out[name].shape)
        drawn = base * np.exp(spread * noise) if base else spread * noise
        out[name] = jnp.asarray(drawn.astype(out[name].dtype))
    for name, factor in factors.items():
        out[name] = (out[name] * factor).astype(out[name].dtype)
    return out
```

```python
import concourse.bass as bass
from concourse import mybir
from contextlib import ExitStack

FP32 = mybir.dt.float32
BF16 = mybir.dt.bfloat16
ALU = mybir.AluOpType
ACT = mybir.ActivationFunctionType
AX = mybir.AxisListType

P = 128
B, T, D = 16, 1024, 256
NH, HD = 16, 16
DC = D // P
E0 = 16
RT = B * E0 // P
BPT = P // E0
HPC = P // HD
MS = 512
TPM = MS // P
STEPS = B * T // MS
GH = 4
NG = NH // GH
QT = T // P
VW = HD + 1
VPAD = GH * VW + 32 - VW
NPOS = 3
NSLOT = 6
KA = NPOS + NSLOT * HD
KB = KA + 3
Q_PART = [0, 0, 0, 1, 1, 2]
K_PART = [0, 1, 2, 0, 1, 0]
EPS = 1e-5
BIG = -1e30
LEAD = 5


class Chain:

    def __init__(self, eng, sem, base=0):
        self.eng, self.sem, self.base, self.n = eng, sem, base, 0

    def __call__(self, ins):
        self.n += 1
        ins.then_inc(self.sem, 1)
        self.eng.wait_ge(self.sem, self.base + self.n)


def prepare(nc, a, scr):
    ctx = ExitStack()
    with ctx:
        def sb(name, shape, dt=FP32):
            return ctx.enter_context(nc.sbuf_tensor(name, shape, dt))

        def pb(name, shape, dt=FP32):
            return ctx.enter_context(nc.psum_tensor(name, shape, dt))

        def sem(name):
            return ctx.enter_context(nc.semaphore(name))

        ident = sb("p_ident", [P, P])
        ones = sb("p_ones", [P, P])
        ldT = sb("p_ldT", [100, 4])
        da = sb("p_da", [100, D])
        luT = sb("p_luT", [4, 50])
        uaT = sb("p_uaT", [50, D])
        t1 = sb("p_t1", [4, D])
        t2 = sb("p_t2", [50, D])
        wt = sb("p_wt", [P, DC, D])
        x = sb("p_x", [P, RT, D])
        xn = sb("p_xn", [P, RT, D])
        lna = sb("p_lna", [P, D])
        stats = sb("p_stats", [P, RT, 6])
        mv = sb("p_mv", [P, RT, 2])
        ve = sb("p_ve", [P, 32])
        rstd = sb("p_rstd", [P, 32])
        neghalf = sb("p_neghalf", [P, 32])
        xT = sb("p_xT", [P, DC, RT * P])
        wqkv = sb("p_wqkv", [P, 3, DC, D])
        wo = sb("p_wo", [P, DC, D])
        bqv = sb("p_bqv", [P, 2, D])
        bd = sb("p_bd", [P, 3, P])
        bl = sb("p_bl", [P, 3, HD])
        lnw = sb("p_lnw", [P, 2, HD])
        cur = [sb(f"p_cur{i}", [P, RT, D]) for i in range(3)]
        curT = [sb(f"p_curT{i}", [P, DC, RT * P]) for i in range(3)]
        lat = [sb(f"p_lat{i}", [P, RT, D]) for i in range(3)]
        nrm = [sb(f"p_nrm{i}", [P, RT, D]) for i in range(2)]
        nrmT = [sb(f"p_nrmT{i}", [P, DC, RT * P]) for i in range(2)]
        sq = sb("p_sq", [P, RT, D])
        mean = sb("p_mean", [P, RT * NH])
        hmask = sb("p_hmask", [P, HPC])
        bmask = sb("p_bmask", [P, P])
        kx = sb("p_kx", [P, 2, HPC, P])
        s = sb("p_s", [P, 2, HPC, P])
        smax = sb("p_smax", [P, 2, HPC])
        ssum = sb("p_ssum", [P, 2, HPC])
        pT = sb("p_pT", [P, 2, HPC, P])
        ai = [sb(f"p_ai{i}", [P, RT, D]) for i in range(3)]
        dsum = sb("p_dsum", [P, 8])
        sc = sb("p_sc", [P, 3])
        tsc = sb("p_tsc", [P, 4])
        pbank = [pb(f"p_b{i}", [P, 1024]) for i in range(4)]

        s_in = sem("p_loaded")
        s_const = sem("p_const")
        s_lora_pe = sem("p_lora_pe")
        s_lora = sem("p_lora")
        s_var = sem("p_var")
        s_rstd = sem("p_rstd")
        s_xn = sem("p_xn")
        s_xT_pe = sem("p_xT_pe")
        s_xT = sem("p_xT")
        s_qkv_pe = sem("p_qkv_pe")
        s_cur = sem("p_cur")
        s_curT_pe = sem("p_curT_pe")
        s_curT = sem("p_curT")
        s_lat_pe = sem("p_lat_pe")
        s_nrm = sem("p_nrm")
        s_nrmT_pe = sem("p_nrmT_pe")
        s_nrmT = sem("p_nrmT")
        s_kx = sem("p_kx")
        s_sc_pe = sem("p_scores_pe")
        s_sub = sem("p_sub")
        s_exp = sem("p_exp")
        s_turn_pe = sem("p_turn_pe")
        s_pT = sem("p_pT")
        s_pv_pe = sem("p_pv_pe")
        s_ai = sem("p_ai")
        s_dif = sem("p_dif")
        s_dif_pe = sem("p_dif_pe")
        s_sel = sem("p_sel")
        s_oT_pe = sem("p_oT_pe")
        s_oT = sem("p_oT")
        s_o_pe = sem("p_o_pe")
        s_o = sem("p_o")
        s_out = sem("p_stored")
        s_link = sem("p_dve_link")

        UN = DC * RT
        flat = lambda t: t.rearrange("p h n -> p (h n)")
        heads = lambda t: t[:, :, :].rearrange("p r (h d) -> p (r h) d", d=HD)
        whole = lambda bank: bank[:, 0:RT * D].rearrange("p (r n) -> p r n", r=RT)
        col = lambda t: t.rearrange("p (h o) -> p h o", o=1)

        block = ctx.enter_context(nc.Block())
        lo = [(ident[:, :], a["ident"]), (ldT[:, :], a["ldT"]), (da[:, :], a["down_aux"]),
              (luT[:, :], a["luT"]), (uaT[:, :], a["uaT"]),
              (wt[:, :, :], a["W0T"].rearrange("(k p) n -> p k n", p=P)),
              (lna[:, :], a["lna_w"].partition_broadcast(P)),
              (wo[:, :, :], a["WoT"].rearrange("(k p) n -> p k n", p=P)),
              (bqv[:, 0, :], a["bq"].partition_broadcast(P)),
              (bqv[:, 1, :], a["bv"].partition_broadcast(P)),
              (lnw[:, 0, :], a["lnc_w"].partition_broadcast(P)),
              (lnw[:, 1, :], a["lnd_w"].partition_broadcast(P)),
              (hmask[:, :], a["headmask"]), (bmask[:, :], a["batchmask"]),
              (sc[:, 0:1], a["temp"].partition_broadcast(P)),
              (sc[:, 1:2], a["threshold"].partition_broadcast(P)),
              (sc[:, 2:3], a["factor"].partition_broadcast(P))]
        for n, w in enumerate(("WqT", "WkT", "WvT")):
            lo.append((wqkv[:, n, :, :], a[w].rearrange("(k p) n -> p k n", p=P)))
        for n, w in enumerate(("blq", "blk", "blv")):
            lo.append((bl[:, n, :], a[w].partition_broadcast(P)))
        for b in range(B):
            at = b % BPT * E0
            lo.append((x[at:at + E0, b // BPT, :], a["x"][b, 0:E0, :]))
        n_loads = 16 * (len(lo) + 3 * HPC)

        @block.sync
        def _(sp):
            for dst, src in lo:
                sp.dma_start(dst, src).then_inc(s_in, 16)
            sp.wait_ge(s_const, 3)
            for n, w in enumerate(("WlqT", "WlkT", "WlvT")):
                for h in range(HPC):
                    sp.dma_start(bd[h * HD:(h + 1) * HD, n, h * HD:(h + 1) * HD], a[w]).then_inc(s_in, 16)
            sp.wait_ge(s_lora, 3)
            sp.dma_start(scr["w0"].rearrange("(k p) n -> p k n", p=P), wt[:, :, :]).then_inc(s_out, 16)
            sp.wait_ge(s_o, 1)
            sp.dma_start(scr["attn0"].rearrange("(r p) n -> p r n", p=P), xn[:, :, :]).then_inc(s_out, 16)
            sp.wait_ge(s_out, 32)

        @block.gpsimd
        def _(pool):
            pool.memset(ones[:, :], 1.0).then_inc(s_const, 1)
            pool.memset(bd[:, :, :], 0.0).then_inc(s_const, 1)
            pool.memset(neghalf[:, :], -0.5).then_inc(s_const, 1)
            pool.wait_ge(s_const, 3)
            for n in range(2):
                pool.wait_ge(s_var, n + 1)
                pool.tensor_tensor(rstd[:, 0:RT], ve[:, 0:RT], neghalf[:, 0:RT], ALU.pow).then_inc(s_rstd, 1)
            for it in range(3):
                pool.wait_ge(s_var, 3 * it + 3)
                pool.tensor_tensor(tsc[:, 0:1], tsc[:, 3:4], neghalf[:, 0:1], ALU.pow).then_inc(s_rstd, 1)
                for n in range(2):
                    pool.wait_ge(s_var, 3 * it + 4 + n)
                    pool.tensor_tensor(rstd[:, :], ve[:, :], neghalf[:, :], ALU.pow).then_inc(s_rstd, 1)

        @block.tensor
        def _(pe):
            def turn_rows(bank, src):
                for k in range(DC):
                    for r in range(RT):
                        at = (k * RT + r) * P
                        mm = pe.transpose(bank[:, at:at + P], src[:, r, k * P:(k + 1) * P], ident[:, :])
                return mm

            pe.wait_ge(s_in, n_loads)
            pe.wait_ge(s_const, 3)
            pe.matmul(pbank[0][0:4, 0:D], ldT[:, :], da[:, :], start=True, stop=True).then_inc(s_lora_pe, 1)
            pe.wait_ge(s_lora, 1)
            pe.matmul(pbank[0][0:50, 0:D], luT[:, :], t1[:, :], start=True, stop=True).then_inc(s_lora_pe, 1)
            pe.wait_ge(s_lora, 2)
            for k in range(DC):
                mm = pe.matmul(pbank[0][:, k * D:(k + 1) * D], t2[:, k * P:(k + 1) * P], uaT[:, :],
                               start=True, stop=True)
            mm.then_inc(s_lora_pe, 1)
            pe.wait_ge(s_xn, 1)
            turn_rows(pbank[1], xn).then_inc(s_xT_pe, 1)
            pe.wait_ge(s_xT, 1)
            pe.wait_ge(s_lora, 3)
            for n in range(3):
                for r in range(RT):
                    for k in range(DC):
                        mm = pe.matmul(pbank[n][:, r * D:(r + 1) * D], xT[:, k, r * P:(r + 1) * P],
                                       wqkv[:, n, k, :], start=(k == 0), stop=(k == DC - 1))
                mm.then_inc(s_qkv_pe, 1)
            for it in range(3):
                pe.wait_ge(s_cur, it + 1)
                for n in range(3):
                    src = cur[n] if n == 0 or it == 0 else lat[n]
                    turn_rows(pbank[n], src).then_inc(s_curT_pe, 1)
                for n in range(3):
                    pe.wait_ge(s_curT, 3 * it + n + 1)
                    for r in range(RT):
                        for k in range(DC):
                            at = r * D + k * P
                            mm = pe.matmul(pbank[n][:, at:at + P], curT[n][:, k, r * P:(r + 1) * P],
                                           bd[:, n, :], start=True, stop=True)
                    mm.then_inc(s_lat_pe, 1)
                for n in range(2):
                    pe.wait_ge(s_nrm, 2 * it + n + 1)
                    turn_rows(pbank[n], nrm[n]).then_inc(s_nrmT_pe, 1)
                pe.wait_ge(s_nrmT, 2 * it + 2)

                def scores(u):
                    g, k, r, z = UN * it + u, u // RT, u % RT, u % 2
                    pe.wait_ge(s_kx, g + 1)
                    if g >= 2:
                        pe.wait_ge(s_pT, g - 1)
                    for c in range(2):
                        mm = pe.matmul(pbank[2 + z][:, c * 512:(c + 1) * 512], nrmT[0][:, k, r * P:(r + 1) * P],
                                       flat(kx[:, z, c * 4:(c + 1) * 4, :]), start=True, stop=True)
                    mm.then_inc(s_sc_pe, 1)

                def weigh(u):
                    g, k, r, z = UN * it + u, u // RT, u % RT, u % 2
                    pe.wait_ge(s_exp, g + 1)
                    for h in range(HPC):
                        mm = pe.transpose(pbank[2 + z][:, h * P:(h + 1) * P], s[:, z, h, :], ident[:, :])
                    mm.then_inc(s_turn_pe, 1)
                    pe.wait_ge(s_pT, g + 1)
                    if g >= 2:
                        pe.wait_ge(s_ai, g - 1)
                    for h in range(HPC):
                        at = k * P + h * HD
                        mm = pe.matmul(pbank[z][:, h * HD:(h + 1) * HD], pT[:, z, h, :],
                                       lat[2][:, r, at:at + HD], start=True, stop=True)
                    mm.then_inc(s_pv_pe, 1)

                scores(0)
                for u in range(1, UN):
                    scores(u)
                    weigh(u - 1)
                weigh(UN - 1)
                if it == 1:
                    pe.wait_ge(s_dif, 1)
                    pe.matmul(pbank[0][:, 512:513], ones[:, :], dsum[:, 0:1], start=True, stop=True).then_inc(s_dif_pe, 1)
            pe.wait_ge(s_sel, 1)
            turn_rows(pbank[0], ai[2]).then_inc(s_oT_pe, 1)
            pe.wait_ge(s_oT, 1)
            for r in range(RT):
                for k in range(DC):
                    mm = pe.matmul(pbank[1][:, r * D:(r + 1) * D], xT[:, k, r * P:(r + 1) * P], wo[:, k, :],
                                   start=(k == 0), stop=(k == DC - 1))
            mm.then_inc(s_o_pe, 1)

        @block.scalar
        def _(act):
            for it in range(3):
                for n in range(3):
                    act.wait_ge(s_curT_pe, 3 * it + n + 1)
                    nc.scalar.copy(curT[n][:, :, :], whole(pbank[n])).then_inc(s_curT, 1)
                for n in range(2):
                    act.wait_ge(s_nrmT_pe, 2 * it + n + 1)
                    nc.scalar.copy(nrmT[n][:, :, :], whole(pbank[n])).then_inc(s_nrmT, 1)

                def exps(u):
                    g, z = UN * it + u, u % 2
                    act.wait_ge(s_sub, g + 1)
                    nc.scalar.activation(flat(s[:, z, :, :]), flat(s[:, z, :, :]), ACT.Exp).then_inc(s_exp, 1)

                def copies(u):
                    g, z = UN * it + u, u % 2
                    act.wait_ge(s_turn_pe, g + 1)
                    if g >= 2:
                        act.wait_ge(s_pv_pe, g - 1)
                    nc.scalar.copy(flat(pT[:, z, :, :]), pbank[2 + z][:, :]).then_inc(s_pT, 1)

                exps(0)
                for u in range(1, UN):
                    copies(u - 1)
                    exps(u)
                copies(UN - 1)

        @block.vector
        def _(dve):
            V = nc.vector
            link = Chain(dve, s_link)
            dve.wait_ge(s_in, n_loads)
            dve.wait_ge(s_const, 3)
            dve.wait_ge(s_lora_pe, 1)
            V.tensor_copy(t1[:, :], pbank[0][0:4, 0:D]).then_inc(s_lora, 1)
            dve.wait_ge(s_lora_pe, 2)
            V.tensor_copy(t2[:, :], pbank[0][0:50, 0:D]).then_inc(s_lora, 1)
            dve.wait_ge(s_lora_pe, 3)
            V.tensor_tensor(wt[:, :, :], wt[:, :, :], pbank[0][:, 0:DC * D].rearrange("p (k n) -> p k n", k=DC),
                            ALU.add).then_inc(s_lora, 1)
            for n in range(2):
                src = x if n == 0 else xn
                for r in range(RT):
                    link(V.bn_stats(stats[:, r, :], src[:, r, :]))
                    link(V.bn_aggr(mv[:, r, :], stats[:, r, :]))
                V.tensor_scalar(ve[:, 0:RT], mv[:, :, 1], EPS, None, ALU.add).then_inc(s_var, 1)
                dve.wait_ge(s_rstd, n + 1)
                for r in range(RT):
                    link(V.tensor_scalar(xn[:, r, :], src[:, r, :], mv[:, r, 0:1], rstd[:, r:r + 1],
                                         ALU.subtract, ALU.mult))
            V.tensor_tensor(xn[:, :, :], xn[:, :, :],
                            lna[:, :].rearrange("p (o n) -> p o n", o=1).to_broadcast([P, RT, D]),
                            ALU.mult).then_inc(s_xn, 1)
            dve.wait_ge(s_xT_pe, 1)
            V.tensor_copy(xT[:, :, :], whole(pbank[1])).then_inc(s_xT, 1)
            scale = HD ** -0.25
            dve.wait_ge(s_qkv_pe, 1)
            link(V.tensor_tensor(cur[0][:, :, :], whole(pbank[0]), bqv[:, 0:1, :].to_broadcast([P, RT, D]), ALU.add))
            link(V.tensor_scalar(cur[0][:, :, :], cur[0][:, :, :], scale, None, ALU.mult))
            dve.wait_ge(s_qkv_pe, 2)
            link(V.tensor_scalar(cur[1][:, :, :], whole(pbank[1]), scale, None, ALU.mult))
            dve.wait_ge(s_qkv_pe, 3)
            V.tensor_tensor(cur[2][:, :, :], whole(pbank[2]), bqv[:, 1:2, :].to_broadcast([P, RT, D]),
                            ALU.add).then_inc(s_cur, 1)
            for it in range(3):
                for n in range(3):
                    dve.wait_ge(s_lat_pe, 3 * it + n + 1)
                    link(V.tensor_tensor(heads(lat[n]), pbank[n][:, 0:RT * D].rearrange("p (h d) -> p h d", d=HD),
                                         bl[:, n:n + 1, :].to_broadcast([P, RT * NH, HD]), ALU.add))
                link(V.tensor_scalar(tsc[:, 1:2], sc[:, 0:1], 0.005 * it, None, ALU.add))
                link(V.tensor_scalar(tsc[:, 2:3], tsc[:, 1:2], 0.0, None, ALU.is_gt))
                link(V.tensor_scalar(tsc[:, 1:2], tsc[:, 1:2], tsc[:, 2:3], None, ALU.mult))
                link(V.tensor_scalar(tsc[:, 2:3], tsc[:, 2:3], -1.0, 1.0, ALU.mult, ALU.add))
                V.tensor_tensor(tsc[:, 3:4], tsc[:, 1:2], tsc[:, 2:3], ALU.add).then_inc(s_var, 1)
                for n in range(2):
                    link(V.tensor_reduce(mean[:, :], heads(lat[n]), AX.X, ALU.add))
                    link(V.tensor_scalar(mean[:, :], mean[:, :], 1.0 / HD, None, ALU.mult))
                    link(V.tensor_tensor(heads(nrm[n]), heads(lat[n]),
                                         col(mean[:, :]).to_broadcast([P, RT * NH, HD]), ALU.subtract))
                    link(V.tensor_tensor(sq[:, :, :], nrm[n][:, :, :], nrm[n][:, :, :], ALU.mult))
                    link(V.tensor_reduce(ve[:, :], heads(sq), AX.X, ALU.add))
                    V.tensor_scalar(ve[:, :], ve[:, :], 1.0 / HD, EPS, ALU.mult, ALU.add).then_inc(s_var, 1)
                    link(V.tensor_tensor(heads(nrm[n]), heads(nrm[n]),
                                         lnw[:, n:n + 1, :].to_broadcast([P, RT * NH, HD]), ALU.mult))
                    dve.wait_ge(s_rstd, 3 * it + 4 + n)
                    norm = V.tensor_tensor(heads(nrm[n]), heads(nrm[n]),
                                           col(rstd[:, :]).to_broadcast([P, RT * NH, HD]), ALU.mult)
                    if n == 1:
                        norm.then_inc(s_nrm, 1)
                    else:
                        link(norm)
                        V.tensor_scalar(nrm[0][:, :, :], nrm[0][:, :, :], tsc[:, 0:1], None,
                                        ALU.mult).then_inc(s_nrm, 1)
                dve.wait_ge(s_nrmT, 2 * it + 2)

                def keys(u):
                    g, k, r, z = UN * it + u, u // RT, u % RT, u % 2
                    if g >= 2:
                        dve.wait_ge(s_sc_pe, g - 1)
                    V.tensor_tensor(kx[:, z, :, :],
                                    nrmT[1][:, k:k + 1, r * P:(r + 1) * P].to_broadcast([P, HPC, P]),
                                    col(hmask[:, :]).to_broadcast([P, HPC, P]), ALU.mult).then_inc(s_kx, 1)

                def shifted(u):
                    g, z = UN * it + u, u % 2
                    dve.wait_ge(s_sc_pe, g + 1)
                    if g >= 2:
                        dve.wait_ge(s_turn_pe, g - 1)
                    link(V.scalar_tensor_tensor(
                        s[:, z, :, :], pbank[2 + z][:, :].rearrange("p (h n) -> p h n", n=P), HD ** -0.5,
                        bmask[:, :].rearrange("p (o n) -> p o n", o=1).to_broadcast([P, HPC, P]),
                        ALU.mult, ALU.add))
                    link(V.tensor_reduce(smax[:, z, :], s[:, z, :, :], AX.X, ALU.max))
                    V.tensor_tensor(s[:, z, :, :], s[:, z, :, :], col(smax[:, z, :]).to_broadcast([P, HPC, P]),
                                    ALU.subtract).then_inc(s_sub, 1)

                def result(u):
                    g, k, r, z = UN * it + u, u // RT, u % RT, u % 2
                    dve.wait_ge(s_exp, g + 1)
                    link(V.tensor_reduce(ssum[:, z, :], s[:, z, :, :], AX.X, ALU.add))
                    link(V.reciprocal(ssum[:, z, :], ssum[:, z, :]))
                    dve.wait_ge(s_pv_pe, g + 1)
                    V.tensor_tensor(ai[it][:, r, k * P:(k + 1) * P].rearrange("p (h d) -> p h d", d=HD),
                                    pbank[z][:, 0:P].rearrange("p (h d) -> p h d", d=HD),
                                    col(ssum[:, z, :]).to_broadcast([P, HPC, HD]), ALU.mult).then_inc(s_ai, 1)

                keys(0)
                keys(1)
                shifted(0)
                for u in range(1, UN):
                    shifted(u)
                    if u + 1 < UN:
                        keys(u + 1)
                    result(u - 1)
                result(UN - 1)
                dve.wait_ge(s_ai, UN * (it + 1))
                if it == 1:
                    link(V.tensor_tensor(sq[:, :, :], ai[1][:, :, :], ai[0][:, :, :], ALU.subtract))
                    V.tensor_reduce(dsum[:, 0:1], sq[:, :, :], AX.XY, ALU.add,
                                    apply_absolute_value=True).then_inc(s_dif, 1)
                    dve.wait_ge(s_dif_pe, 1)
                    link(V.tensor_scalar(dsum[:, 1:2], pbank[0][:, 512:513], 1.0 / (B * T * D), None, ALU.mult))
                    link(V.tensor_scalar(dsum[:, 2:3], dsum[:, 1:2], sc[:, 2:3], sc[:, 1:2], ALU.mult, ALU.add))
                    link(V.tensor_tensor(dsum[:, 3:4], dsum[:, 1:2], dsum[:, 2:3], ALU.is_lt))
                    link(V.tensor_scalar(dsum[:, 4:5], dsum[:, 3:4], -1.0, 1.0, ALU.mult, ALU.add))
                if it < 2:
                    V.tensor_tensor(cur[0][:, :, :], cur[0][:, :, :], ai[it][:, :, :], ALU.add).then_inc(s_cur, 1)
            link(V.tensor_scalar(ai[1][:, :, :], ai[1][:, :, :], dsum[:, 3:4], None, ALU.mult))
            V.scalar_tensor_tensor(flat(ai[2][:, :, :]), flat(ai[2][:, :, :]), dsum[:, 4:5], flat(ai[1][:, :, :]),
                                   ALU.mult, ALU.add).then_inc(s_sel, 1)
            dve.wait_ge(s_oT_pe, 1)
            V.tensor_copy(xT[:, :, :], whole(pbank[0])).then_inc(s_oT, 1)
            dve.wait_ge(s_o_pe, 1)
            V.tensor_copy(xn[:, :, :], whole(pbank[1])).then_inc(s_o, 1)


def project(nc, a, scr):
    ctx = ExitStack()
    with ctx:
        def sb(name, shape, dt=FP32):
            return ctx.enter_context(nc.sbuf_tensor(name, shape, dt))

        def sem(name):
            return ctx.enter_context(nc.semaphore(name))

        ident = sb("j_ident", [P, P])
        w = {n: sb(f"j_{n}", [P, DC, D]) for n in ("w0", "wq", "wk", "wv", "wr", "wkk", "wvv")}
        bias0 = sb("j_bias0", [P, 2, D])
        vbias = sb("j_vbias", [P, D])
        obias = sb("j_obias", [P, D])
        qbias = sb("j_qbias", [P, DC])
        kbias = sb("j_kbias", [P, DC])
        mu = sb("j_mu", [P, 2, DC])
        omu = sb("j_omu", [P, 2, DC])
        neghalf = sb("j_neghalf", [P, TPM])
        x = sb("j_x", [P, 2, TPM, D])
        att = sb("j_att", [E0, D])
        xn = sb("j_xn", [P, TPM, D])
        xT = sb("j_xT", [P, DC, MS])
        x1 = sb("j_x1", [P, 2, TPM, D])
        x1n = sb("j_x1n", [P, TPM, D])
        x1T = sb("j_x1T", [P, 2, DC, MS + 1])
        stats = sb("j_stats", [P, 2, TPM, 6])
        mv = sb("j_mv", [P, 2, TPM, 2])
        ve = sb("j_ve", [P, 2, TPM])
        hold = sb("j_hold", [P, 1])
        rstd = sb("j_rstd", [P, 2, TPM])
        xmu = sb("j_xmu", [P, 2, DC, MS])
        mix = sb("j_mix", [P, 2, DC, MS])
        full = sb("j_full", [P, 2, DC, MS])
        rest = sb("j_rest", [P, 2, DC, MS])
        part = sb("j_part", [P, 2, 3, DC, MS], BF16)
        v = sb("j_v", [P, 2, TPM, NH, VW])
        kact = sb("j_kact", [P, DC, MS])
        ksq = sb("j_ksq", [P, DC, MS])
        gate = sb("j_gate", [P, TPM, D])
        ffn = sb("j_ffn", [P, TPM, D])
        res = sb("j_res", [P, 2, TPM, D])
        bank = [ctx.enter_context(nc.psum_tensor(f"j_b{i}", [P, 2 * 512], FP32)) for i in range(4)]

        s_w = sem("j_weights")
        s_set = sem("j_set")
        s_x = [sem(f"j_x_in{i}") for i in range(2)]
        s_att = sem("j_att_in")
        s_var0, s_rs0, s_xn = sem("j_var0"), sem("j_rs0"), sem("j_xn_ready")
        s_var1, s_rs1, s_x1n = sem("j_var1"), sem("j_rs1"), sem("j_x1n_ready")
        s_t1, s_xT = sem("j_t1_pe"), sem("j_xT_ready")
        s_f0, s_xb, s_x1 = sem("j_f0_pe"), sem("j_xb_ready"), sem("j_x1_ready")
        s_t2, s_x1T = sem("j_t2_pe"), sem("j_x1T_ready")
        s_xmu, s_mixk, s_mixr = sem("j_xmu_ready"), sem("j_mixk_ready"), sem("j_mixr_ready")
        s_q, s_full = sem("j_q_pe"), [sem("j_q_full"), sem("j_k_full")]
        s_k = sem("j_k_pe")
        s_hi, s_res1 = [sem("j_q_hi"), sem("j_k_hi")], [sem("j_q_res1"), sem("j_k_res1")]
        s_mid, s_lo = [sem("j_q_mid"), sem("j_k_mid")], [sem("j_q_lo"), sem("j_k_lo")]
        s_v, s_vb = sem("j_v_pe"), sem("j_v_ready")
        s_kk, s_relu, s_ksq = sem("j_kk_pe"), sem("j_relu"), sem("j_ksq")
        s_r, s_tanh = sem("j_r_pe"), sem("j_tanh")
        s_kv, s_ffn, s_xo, s_res = sem("j_kv_pe"), sem("j_ffn_ready"), sem("j_xo_ready"), sem("j_res_ready")
        s_qk_out = [sem("j_q_stored"), sem("j_k_stored")]
        s_v_out = [sem(f"j_v_stored{i}") for i in range(2)]
        s_res_out = [sem(f"j_res_stored{i}") for i in range(2)]
        s_link = sem("j_dve_link")
        s_xbias = sem("j_xbias")

        xt = a["x"].rearrange("b (h t p) c -> (b h) p t c", p=P, t=TPM)
        res_d = scr["res"].rearrange("b (h t p) c -> (b h) p t c", p=P, t=TPM)
        v_d = scr["v"].rearrange("b (h t p) c -> (b h) p t c", p=P, t=TPM)
        part_d = [scr[n].rearrange("s b (k p) t -> b s p k t", p=P) for n in ("qs", "ks")]
        att_d = scr["attn0"].rearrange("(b t) n -> b t n", t=E0)
        rows = lambda bk: bk[:, :].rearrange("p (t n) -> p t n", t=TPM)
        chunks = lambda bk: bk[:, :].rearrange("p (k n) -> p k n", k=DC)
        every = lambda t, n=TPM: t.rearrange("p (o n) -> p o n", o=1).to_broadcast([P, n, D])

        block = ctx.enter_context(nc.Block())
        lo = [(ident[:, :], a["ident"])]
        lo += [(w[n][:, :, :], src.rearrange("(k p) n -> p k n", p=P)) for n, src in (
            ("w0", scr["w0"]), ("wq", a["q_w"]), ("wk", a["kv_w"][:, 0:D]), ("wv", a["kv_w"][:, D:2 * D]),
            ("wr", a["WrT"]), ("wkk", a["WkkT"]), ("wvv", a["WvvT"]))]
        lo += [(bias0[:, 0, :], a["b0"].partition_broadcast(P)), (bias0[:, 1, :], a["bo"].partition_broadcast(P)),
               (vbias[:, :], a["kv_b"][D:2 * D].partition_broadcast(P)),
               (obias[:, :], a["o_b"].partition_broadcast(P)),
               (mu[:, 0, :], a["mu_r_col"]), (mu[:, 1, :], a["mu_k_col"]),
               (qbias[:, :], a["q_b_col"]), (kbias[:, :], a["k_b_col"])]
        n_w = 16 * len(lo)
        N_SET = 6

        @block.sync
        def _(sp):
            for dst, src in lo:
                sp.dma_start(dst, src).then_inc(s_w, 16)
            for i in range(2):
                sp.dma_start(x[:, i, :, :], xt[i]).then_inc(s_x[i], 16)
            sp.dma_start(att[:, :], att_d[0]).then_inc(s_att, 16)

            def step(b, half, more):
                m = 2 * b + half
                if half == 0 and more:
                    sp.wait_ge(s_xb, 2 * b + 1)
                    sp.dma_start(att[:, :], att_d[b + 1]).then_inc(s_att, 16)
                if more:
                    sp.wait_ge(s_x1, m + 1)
                    sp.dma_start(x[:, half, :, :], xt[m + 2]).then_inc(s_x[half], 16)
                for n in range(2):
                    sp.wait_ge(s_lo[n], m + 1)
                    for s in range(3):
                        sp.dma_start(part_d[n][b, s][:, :, half * MS:(half + 1) * MS],
                                     part[:, n, s, :, :]).then_inc(s_qk_out[n], 16)
                sp.wait_ge(s_vb, m + 1)
                sp.dma_start(v_d[m], v[:, half, :, :, :].rearrange("p t h d -> p t (h d)")).then_inc(s_v_out[half], 16)
                sp.wait_ge(s_res, m + 1)
                sp.dma_start(res_d[m], res[:, half, :, :]).then_inc(s_res_out[half], 16)

            with sp.Fori(0, B - 1) as b:
                for half in range(2):
                    step(b, half, True)
            for half in range(2):
                step(B - 1, half, False)
            for n in range(2):
                sp.wait_ge(s_qk_out[n], 48 * STEPS)
                sp.wait_ge(s_v_out[n], 16 * B)
                sp.wait_ge(s_res_out[n], 16 * B)

        @block.tensor
        def _(pe):
            def turn(bk, src):
                for k in range(DC):
                    for t in range(TPM):
                        at = k * MS + t * P
                        mm = pe.transpose(bk[:, at:at + P], src[:, t, k * P:(k + 1) * P], ident[:, :])
                return mm

            def by_token(bk, src, weight):
                for t in range(TPM):
                    for k in range(DC):
                        mm = pe.matmul(bk[:, t * D:(t + 1) * D], src[:, k, t * P:(t + 1) * P], weight[:, k, :],
                                       start=(k == 0), stop=(k == DC - 1))
                return mm

            def by_dim(bk, src, weight):
                for n in range(DC):
                    for k in range(DC):
                        mm = pe.matmul(bk[:, n * MS:(n + 1) * MS], weight[:, k, n * P:(n + 1) * P], src[:, k, :],
                                       start=(k == 0), stop=(k == DC - 1))
                return mm

            def step(m, half, first, more):
                new = x1T[:, half, :, 1:MS + 1]
                pe.wait_ge(s_x1n, m + 1)
                if not first:
                    pe.wait_ge(s_full[1], m)
                turn(bank[0], x1n).then_inc(s_t2, 1)
                if more:
                    pe.wait_ge(s_xn, m + 2)
                    if not first:
                        pe.wait_ge(s_vb, m)
                    turn(bank[1], xn).then_inc(s_t1, 1)
                pe.wait_ge(s_x1T, m + 1)
                if not first:
                    pe.wait_ge(s_ffn, m)
                by_dim(bank[2], new, w["wq"]).then_inc(s_q, 1)
                if more:
                    pe.wait_ge(s_xT, m + 2)
                    if not first:
                        pe.wait_ge(s_tanh, m)
                    by_token(bank[3], xT, w["w0"]).then_inc(s_f0, 1)
                by_dim(bank[0], new, w["wk"]).then_inc(s_k, 1)
                if not more:
                    pe.wait_ge(s_vb, m)
                by_token(bank[1], new, w["wv"]).then_inc(s_v, 1)
                pe.wait_ge(s_mixk, m + 1)
                pe.wait_ge(s_full[0], m + 1)
                by_dim(bank[2], mix[:, 1, :, :], w["wkk"]).then_inc(s_kk, 1)
                pe.wait_ge(s_mixr, m + 1)
                if more:
                    pe.wait_ge(s_x1, m + 2)
                else:
                    pe.wait_ge(s_tanh, m)
                by_token(bank[3], mix[:, 0, :, :], w["wr"]).then_inc(s_r, 1)
                pe.wait_ge(s_ksq, m + 1)
                by_token(bank[2], ksq, w["wvv"]).then_inc(s_kv, 1)

            pe.wait_ge(s_w, n_w)
            pe.wait_ge(s_xn, 1)
            turn(bank[1], xn).then_inc(s_t1, 1)
            pe.wait_ge(s_xT, 1)
            by_token(bank[3], xT, w["w0"]).then_inc(s_f0, 1)
            pe.wait_ge(s_x1, 1)
            step(0, 0, True, True)
            step(1, 1, False, True)
            with pe.Fori(1, B - 1) as b:
                for half in range(2):
                    step(2 * b + half, half, False, True)
            step(STEPS - 2, 0, False, True)
            step(STEPS - 1, 1, False, False)

        @block.scalar
        def _(act):
            def step(m, half, first, more):
                act.wait_ge(s_t2, m + 1)
                nc.scalar.copy(x1T[:, half, :, 1:MS + 1], chunks(bank[0])).then_inc(s_x1T, 1)
                if more:
                    act.wait_ge(s_t1, m + 2)
                    act.wait_ge(s_f0, m + 1)
                    nc.scalar.copy(xT[:, :, :], chunks(bank[1])).then_inc(s_xT, 1)
                act.wait_ge(s_x1T, m + 1)
                if half == 1:
                    nc.scalar.copy(x1T[:, 1, :, 0:1], x1T[:, 0, :, MS:MS + 1]).then_inc(s_xmu, 1)
                if not first:
                    act.wait_ge(s_mixr, m)
                for i in (1, 0):
                    for k in range(DC):
                        nc.scalar.activation(xmu[:, i, k, :], x1T[:, half, k, 1:MS + 1], ACT.Copy,
                                             scale=mu[:, i, k:k + 1]).then_inc(s_xmu, 1)
                act.wait_ge(s_q, m + 1)
                if not first:
                    act.wait_ge(s_res1[0], m)
                    act.wait_ge(s_hi[0], m)
                for k in range(DC):
                    i = nc.scalar.activation(full[:, 0, k, :], bank[2][:, k * MS:(k + 1) * MS], ACT.Identity,
                                             bias=qbias[:, k:k + 1], scale=HD ** -0.5)
                i.then_inc(s_full[0], 1)
                act.wait_ge(s_k, m + 1)
                if not first:
                    act.wait_ge(s_res1[1], m)
                    act.wait_ge(s_hi[1], m)
                for k in range(DC):
                    i = nc.scalar.activation(full[:, 1, k, :], bank[0][:, k * MS:(k + 1) * MS], ACT.Identity,
                                             bias=kbias[:, k:k + 1])
                i.then_inc(s_full[1], 1)
                act.wait_ge(s_kk, m + 1)
                if not first:
                    act.wait_ge(s_ksq, m)
                nc.scalar.activation(kact[:, :, :], chunks(bank[2]), ACT.Relu).then_inc(s_relu, 1)
                for n in range(2):
                    act.wait_ge(s_res1[n], m + 1)
                    if not first:
                        act.wait_ge(s_qk_out[n], 48 * m)
                    nc.scalar.copy(part[:, n, 1, :, :], rest[:, n, :, :]).then_inc(s_mid[n], 1)
                act.wait_ge(s_r, m + 1)
                if not first:
                    act.wait_ge(s_ffn, m)
                nc.scalar.activation(gate[:, :, :], rows(bank[3]), ACT.Tanh, scale=0.5).then_inc(s_tanh, 1)

            act.wait_ge(s_w, n_w)
            act.wait_ge(s_set, N_SET)
            act.wait_ge(s_t1, 1)
            nc.scalar.copy(xT[:, :, :], chunks(bank[1])).then_inc(s_xT, 1)
            step(0, 0, True, True)
            step(1, 1, False, True)
            with act.Fori(1, B - 1) as b:
                for half in range(2):
                    step(2 * b + half, half, False, True)
            step(STEPS - 2, 0, False, True)
            step(STEPS - 1, 1, False, False)

        @block.vector
        def _(dve):
            V = nc.vector
            STEP_LINKS, PRO_LINKS = 5, 6

            def norm_stats(z, src, link, s_var):
                for t in range(TPM):
                    i = V.bn_stats(stats[:, z, t, :], src[:, t, :])
                link(i)
                V.memset(hold[:, :], 0.0)
                for t in range(TPM):
                    i = V.bn_aggr(mv[:, z, t, :], stats[:, z, t, :])
                link(i)
                V.tensor_scalar(ve[:, z, :], mv[:, z, :, 1], EPS, None, ALU.add).then_inc(s_var, 1)

            def normalise(z, src, dst, s_done):
                for t in range(TPM):
                    i = V.tensor_scalar(dst[:, t, :], src[:, t, :], mv[:, z, t, 0:1], rstd[:, z, t:t + 1],
                                        ALU.subtract, ALU.mult)
                i.then_inc(s_done, 1)

            def layer0(m, half, link, first=False):
                dve.wait_ge(s_f0, m + 1)
                dve.wait_ge(s_xb, m + 1)
                if not first:
                    dve.wait_ge(s_xo, m - 1)
                V.tensor_tensor(x1[:, half, :, :], rows(bank[3]), x[:, half, :, :], ALU.add).then_inc(s_x1, 1)
                dve.wait_ge(s_x1, m + 1)
                norm_stats(1, x1[:, half, :, :], link, s_var1)
                dve.wait_ge(s_rs1, m + 1)
                if not first:
                    dve.wait_ge(s_t2, m)
                normalise(1, x1[:, half, :, :], x1n, s_x1n)

            def norm0(m, half, count, link, first=False):
                dve.wait_ge(s_x[half], 16 * count)
                norm_stats(0, x[:, half, :, :], link, s_var0)
                dve.wait_ge(s_rs0, m + 1)
                if not first:
                    dve.wait_ge(s_t1, m)
                normalise(0, x[:, half, :, :], xn, s_xn)

            def split(n, m, first):
                dve.wait_ge(s_full[n], m + 1)
                if not first:
                    dve.wait_ge(s_qk_out[n], 48 * m)
                V.tensor_copy(part[:, n, 0, :, :], full[:, n, :, :]).then_inc(s_hi[n], 1)

            def step(m, b, half, base, first, more, norm):
                link = Chain(dve, s_link, base)
                for i, s_done in ((1, s_mixk), (0, s_mixr)):
                    dve.wait_ge(s_xmu, 4 * m + (b + half) + (4 if i == 0 else 2))
                    if not first:
                        dve.wait_ge(s_kk if i == 1 else s_r, m)
                    for k in range(DC):
                        j = V.scalar_tensor_tensor(mix[:, i, k, :], x1T[:, half, k, 0:MS], omu[:, i, k:k + 1],
                                                   xmu[:, i, k, :], ALU.mult, ALU.add)
                    j.then_inc(s_done, 1)
                if more:
                    layer0(m + 1, 1 - half, link)
                split(0, m, first)
                split(1, m, first)
                dve.wait_ge(s_hi[1], m + 1)
                V.tensor_tensor(rest[:, 1, :, :], full[:, 1, :, :], part[:, 1, 0, :, :],
                                ALU.subtract).then_inc(s_res1[1], 1)
                dve.wait_ge(s_v, m + 1)
                if not (isinstance(b, int) and b == 0):
                    dve.wait_ge(s_v_out[half], 16 * b)
                for t in range(TPM):
                    i = V.tensor_tensor(v[:, half, t, :, 0:HD], bank[1][:, t * D:(t + 1) * D].rearrange("p (h d) -> p h d", d=HD),
                                        vbias[:, :].rearrange("p (h d) -> p h d", d=HD), ALU.add)
                i.then_inc(s_vb, 1)
                if norm:
                    norm0(m + 2, half, b + 2, link)
                dve.wait_ge(s_mid[1], m + 1)
                V.tensor_tensor(part[:, 1, 2, :, :], rest[:, 1, :, :], part[:, 1, 1, :, :],
                                ALU.subtract).then_inc(s_lo[1], 1)
                dve.wait_ge(s_tanh, m + 1)
                link(V.tensor_scalar(gate[:, :, :], gate[:, :, :], 0.5, 0.5, ALU.mult, ALU.add))
                dve.wait_ge(s_kv, m + 1)
                if not first:
                    dve.wait_ge(s_res, m)
                V.tensor_tensor(ffn[:, :, :], rows(bank[2]), gate[:, :, :], ALU.mult).then_inc(s_ffn, 1)

            dve.wait_ge(s_w, n_w)
            pro = Chain(dve, s_link)
            V.tensor_scalar(qbias[:, :], qbias[:, :], HD ** -0.5, None, ALU.mult).then_inc(s_set, 1)
            V.tensor_scalar(omu[:, :, :], mu[:, :, :], -1.0, 1.0, ALU.mult, ALU.add).then_inc(s_set, 1)
            V.tensor_tensor(bias0[:, 0, :], bias0[:, 0, :], bias0[:, 1, :], ALU.add).then_inc(s_set, 1)
            dve.wait_ge(s_set, N_SET)
            norm0(0, 0, 1, pro, True)
            norm0(1, 1, 1, pro)
            layer0(0, 0, pro, True)
            assert pro.n == PRO_LINKS
            step(0, 0, 0, PRO_LINKS, True, True, True)
            step(1, 0, 1, PRO_LINKS + STEP_LINKS, False, True, True)
            with dve.Fori(1, B - 1) as b:
                for half in range(2):
                    step(2 * b + half, b, half, PRO_LINKS + STEP_LINKS * (2 * b + half), False, True, True)
            step(STEPS - 2, B - 1, 0, PRO_LINKS + STEP_LINKS * (STEPS - 2), False, True, False)
            step(STEPS - 1, B - 1, 1, PRO_LINKS + STEP_LINKS * (STEPS - 2) + 3, False, False, False)

        @block.gpsimd
        def _(pool):
            pool.memset(neghalf[:, :], -0.5).then_inc(s_set, 1)
            pool.memset(v[:, :, :, :, HD:VW], 1.0).then_inc(s_set, 1)
            pool.memset(x1T[:, 0, :, 0:1], 0.0).then_inc(s_set, 1)
            pool.wait_ge(s_set, N_SET)

            def rs0(m):
                pool.wait_ge(s_var0, m + 1)
                pool.tensor_tensor(rstd[:, 0, :], ve[:, 0, :], neghalf[:, :], ALU.pow).then_inc(s_rs0, 1)

            def rs1(m):
                pool.wait_ge(s_var1, m + 1)
                pool.tensor_tensor(rstd[:, 1, :], ve[:, 1, :], neghalf[:, :], ALU.pow).then_inc(s_rs1, 1)

            def with_bias(m, b, half):
                pool.wait_ge(s_xn, m + 1)
                if half == 0:
                    pool.tensor_tensor(x[:, half, :, :], x[:, half, :, :], every(bias0[:, 0, :]), ALU.add).then_inc(s_xbias, 1)
                    pool.wait_ge(s_xbias, b + 1)
                    pool.wait_ge(s_att, 16 * (b + 1))
                    pool.tensor_tensor(x[0:E0, half, 0, :], x[0:E0, half, 0, :], att[:, :], ALU.add).then_inc(s_xb, 1)
                else:
                    pool.tensor_tensor(x[:, half, :, :], x[:, half, :, :], every(bias0[:, 0, :]), ALU.add).then_inc(s_xb, 1)

            def step(m, b, half, first, more, norm):
                if more:
                    rs1(m + 1)
                pool.wait_ge(s_hi[0], m + 1)
                pool.tensor_tensor(rest[:, 0, :, :], full[:, 0, :, :], part[:, 0, 0, :, :],
                                   ALU.subtract).then_inc(s_res1[0], 1)
                if norm:
                    rs0(m + 2)
                pool.wait_ge(s_relu, m + 1)
                if not first:
                    pool.wait_ge(s_kv, m)
                pool.tensor_tensor(ksq[:, :, :], kact[:, :, :], kact[:, :, :], ALU.mult).then_inc(s_ksq, 1)
                pool.wait_ge(s_mid[0], m + 1)
                pool.tensor_tensor(part[:, 0, 2, :, :], rest[:, 0, :, :], part[:, 0, 1, :, :],
                                   ALU.subtract).then_inc(s_lo[0], 1)
                if not (isinstance(b, int) and b == 0):
                    pool.wait_ge(s_res_out[half], 16 * b)
                pool.tensor_tensor(res[:, half, :, :], x1[:, half, :, :], every(obias[:, :]), ALU.add).then_inc(s_xo, 1)
                if norm:
                    with_bias(m + 2, b + 1, half)
                pool.wait_ge(s_xo, m + 1)
                pool.wait_ge(s_ffn, m + 1)
                pool.tensor_tensor(res[:, half, :, :], res[:, half, :, :], ffn[:, :, :], ALU.add).then_inc(s_res, 1)

            rs0(0)
            with_bias(0, 0, 0)
            rs0(1)
            with_bias(1, 0, 1)
            rs1(0)
            step(0, 0, 0, True, True, True)
            step(1, 0, 1, False, True, True)
            with pool.Fori(1, B - 1) as b:
                for half in range(2):
                    step(2 * b + half, b, half, False, True, True)
            step(STEPS - 2, B - 1, 0, False, True, False)
            step(STEPS - 1, B - 1, 1, False, False, False)


def quads():
    half = T // 2
    key_side = [(j, 0, P * j, half - P * j) for j in range(QT // 2)]
    key_side += [(j, 1, max(half, P * j), T - max(half, P * j)) for j in range(QT)]
    query_side = [(i, 0, P * (i + 1)) for i in reversed(range(QT // 2))]
    query_side += [(i, 0, half) for i in range(QT // 2, QT)]
    query_side += [(i, half, P * (i + 1) - half) for i in reversed(range(QT // 2, QT))]
    assert [q[3] for q in key_side] == [q[2] for q in query_side]
    return key_side, query_side


KEY_QUADS, QUERY_QUADS = quads()
NQ = len(KEY_QUADS)


def per_bank(n):
    return 512 // n if n in (128, 256) else 1


def body_units(kind):
    at = {}
    for g in range(NG):
        for r in range(NQ):
            todo = []
            ahead, q = divmod(r + LEAD, NQ)
            to = g + 1 + ahead
            if not (kind == "last" and to >= NG):
                for h in range(0, GH, per_bank(QUERY_QUADS[q][2])):
                    todo.append(("max", to, (q, h)))
            if r == 2 and not (kind == "first" and g == 0):
                todo.append(("norm", g - 1, 1))
            if r == 6:
                todo.append(("norm", g, 0))
            if r == 8 and not (kind == "last" and g == NG - 1):
                todo.append(("rows", g + 1, None))
            if g == 0 and kind != "first":
                if r in (4, 5):
                    todo += [("turn", -1, 2 * (r - 4) + u) for u in range(2)]
                if r in (7, 8):
                    todo += [("out", -1, 2 * (r - 7) + u) for u in range(2)]
            at[g, r] = todo
    return at


def attend(nc, a, scr, out):
    ctx = ExitStack()
    with ctx:
        def sb(name, shape, dt=FP32):
            return ctx.enter_context(nc.sbuf_tensor(name, shape, dt))

        def sem(name):
            return ctx.enter_context(nc.semaphore(name))

        ident = sb("t_ident", [P, P])
        identb = sb("t_identb", [P, P], BF16)
        amask = sb("t_amask", [P, P], BF16)
        bmask = sb("t_bmask", [P, P], BF16)
        ow = sb("t_ow", [P, DC, D])
        q_op = [sb(f"t_q{g}", [P, GH, T], BF16) for g in range(NG)]
        k_op = [sb(f"t_k{g}", [P, GH, T], BF16) for g in range(NG)]
        v = [sb(f"t_v{g}", [P, QT, VPAD], FP32) for g in range(NG)]
        prob = sb("t_prob", [P, 2, GH, 512])
        mx = sb("t_mx", [P, 2, GH, QT])
        mx2 = sb("t_mx2", [P, 2, 2, GH, QT // 2])
        mrest = sb("t_mrest", [P, GH * QT])
        mpart = sb("t_mpart", [P, 3, GH * QT], BF16)
        mrows = sb("t_mrows", [3 * GH * QT, P], BF16)
        yu = sb("t_yu", [P, 2, 512])
        rec = sb("t_rec", [P, 2, GH, GH])
        y = sb("t_y", [P, QT, D])
        yT = sb("t_yT", [P, DC, T])
        res = sb("t_res", [P, QT, D])
        o = sb("t_o", [P, QT, D])
        abank = [ctx.enter_context(nc.psum_tensor(f"t_a{i}", [P, 512], FP32)) for i in range(3)]
        abf = [t[:, :].bitcast(BF16) for t in abank]
        bbank = [ctx.enter_context(nc.psum_tensor(f"t_b{i}", [P, 512], FP32)) for i in range(3)]
        ybank = [ctx.enter_context(nc.psum_tensor(f"t_y{i}", [P, 512], FP32)) for i in range(2)]

        s_c = sem("t_const_in")
        s_set = sem("t_set")
        s_qk = [sem(f"t_qk_in{g}") for g in range(NG)]
        s_vin = [sem(f"t_v_in{g}") for g in range(NG)]
        s_a = sem("t_a_pe")
        s_au = sem("t_a_used")
        s_b = sem("t_b_pe")
        s_e = sem("t_exp")
        s_pv = sem("t_pv_pe")
        s_yu = sem("t_yu_copied")
        s_mp = sem("t_mpart_ready")
        s_mw = sem("t_mrows_written")
        s_m = [sem(f"t_m_in{g}") for g in range(NG)]
        s_res = sem("t_res_in")
        s_out = sem("t_out_stored")
        s_link = sem("t_dve_link")

        kinds = {k: body_units(k) for k in ("first", "mid", "last")}
        count = {k: sum(map(len, at.values())) for k, at in kinds.items()}
        PRO = [("max", 0, (q, h)) for q in range(NQ) for h in range(0, GH, per_bank(QUERY_QUADS[q][2]))]
        PRO += [("rows", 0, None)]
        PRO += [("max", 1, (q, h)) for q in range(LEAD) for h in range(0, GH, per_bank(QUERY_QUADS[q][2]))]
        TAIL = [("norm", -1, 1)] + [("turn", -1, u) for u in range(4)] + [("out", -1, u) for u in range(4)]
        B_UNITS = NG * sum(GH // per_bank(q[3]) for q in KEY_QUADS)

        def base(kind, b):
            if kind == "first":
                return len(PRO)
            return len(PRO) + count["first"] + count["mid"] * (b - 1)

        TAIL_BASE = len(PRO) + count["first"] + count["mid"] * (B - 2) + count["last"]
        LOADS = 2 * NSLOT

        qs = scr["qs"].rearrange("s b (h d) t -> s b d h t", d=HD)
        ks = scr["ks"].rearrange("s b (h d) t -> s b d h t", d=HD)
        vs = scr["v"].rearrange("b (j p) (g c) -> b g p j c", p=P, g=NG)
        resd = scr["res"].rearrange("b (t p) c -> b p t c", p=P)
        outd = out.rearrange("b (t p) c -> b p t c", p=P)

        block = ctx.enter_context(nc.Block())

        @block.sync
        def _(sp):
            lo = [(ident[:, :], a["ident"]), (identb[:, :], a["identb"]), (amask[:, :], a["amask"]),
                  (bmask[:, :], a["bmask"]), (ow[:, :, :], a["o_w"].rearrange("(k p) n -> p k n", p=P))]
            for g in range(NG):
                lo += [(q_op[g][0:NPOS, :, :], a["q_pos"][:, g * GH:(g + 1) * GH, :]),
                       (k_op[g][0:NPOS, :, :], a["k_pos"]), (k_op[g][KA:KB, :, :], a["k_one"])]
            for dst, src in lo:
                sp.dma_start(dst, src).then_inc(s_c, 16)

            def load(b, g):
                for s in range(NSLOT):
                    at = NPOS + s * HD
                    heads = slice(g * GH, (g + 1) * GH)
                    sp.dma_start(q_op[g][at:at + HD, :, :], qs[Q_PART[s], b][:, heads, :]).then_inc(s_qk[g], 16)
                    sp.dma_start(k_op[g][at:at + HD, :, :], ks[K_PART[s], b][:, heads, :]).then_inc(s_qk[g], 16)
                sp.dma_start(v[g][:, :, 0:GH * VW], vs[b, g]).then_inc(s_vin[g], 16)

            def rows(b, g):
                t = NG * b + g
                if isinstance(b, int) and b == 0 and g == 0:
                    sp.wait_ge(s_au, PRO.index(("rows", 0, None)) + 1)
                sp.dma_start(scr["m"][g], mrows[:, :]).then_inc(s_mw, 16)
                sp.wait_ge(s_mw, 16 * (t + 1))
                sp.dma_start(q_op[g][KA:KB, :, :].rearrange("p h t -> p (h t)"),
                             scr["m"][g].rearrange("(s n) q -> s (n q)", s=3)).then_inc(s_m[g], 16)

            def body(kind, b):
                seen = base(kind, b)
                for g in range(NG):
                    for r in range(NQ):
                        for what, to, detail in kinds[kind][g, r]:
                            seen = seen + 1
                            if what == "rows":
                                sp.wait_ge(s_au, seen)
                                rows(b + to // NG, to % NG)
                        if r == 1 and not (kind == "first" and g == 0):
                            done = NG * NQ * b + NQ * g
                            if g > 0 and kind != "last":
                                sp.wait_ge(s_pv, done)
                                load(b + 1, g - 1)
                            if g == 0:
                                sp.wait_ge(s_pv, done)
                                load(b, NG - 1)

            for g in range(NG):
                load(0, g)
            rows(0, 0)
            body("first", 0)
            with sp.Fori(1, B - 1) as b:
                body("mid", b)
            body("last", B - 1)

        @block.tensor
        def _(pe):
            def a_unit(what, to, detail, n, seen, b, seen_norm):
                bk = abank[n]
                if what == "max":
                    g = to % NG
                    q, h0 = detail
                    i, k0, w = QUERY_QUADS[q]
                    for s in range(per_bank(w)):
                        h = h0 + s
                        piece = bk[:, s * w:(s + 1) * w]
                        diagonal = k0 + w == (i + 1) * P
                        mm = pe.matmul(piece, q_op[g][0:KA, h, i * P:(i + 1) * P], k_op[g][0:KA, h, k0:k0 + w],
                                       start=True, stop=not diagonal)
                        if diagonal:
                            mm = pe.matmul(piece[:, w - P:w], identb[:, :], amask[:, :], start=False, stop=True)
                elif what == "rows":
                    pe.wait_ge(s_mp, NG * b + to + 1)
                    mm = pe.transpose(abf[n][0:3 * GH * QT, 0:P], mpart[:, :, :].rearrange("p s n -> p (s n)"), identb[:, :])
                elif what == "norm":
                    pe.wait_ge(s_yu, 2 * (NG * b + to) + detail + 1)
                    for t in range(4):
                        mm = pe.transpose(bk[:, t * P:(t + 1) * P], yu[:, detail, t * P:(t + 1) * P], ident[:, :])
                elif what == "turn":
                    pe.wait_ge(s_au, seen_norm)
                    k, half = divmod(detail, 2)
                    for t in range(4):
                        mm = pe.transpose(bk[:, t * P:(t + 1) * P], y[:, half * 4 + t, k * P:(k + 1) * P], ident[:, :])
                else:
                    pe.wait_ge(s_au, seen_norm)
                    for s in range(2):
                        t = 2 * detail + s
                        for k in range(DC):
                            mm = pe.matmul(bk[:, s * D:(s + 1) * D], yT[:, k, t * P:(t + 1) * P], ow[:, k, :],
                                           start=(k == 0), stop=(k == DC - 1))
                mm.then_inc(s_a, 1)

            def run(units, start, n0, b, last_of):
                for n, (what, to, detail) in enumerate(units, n0):
                    pe.wait_ge(s_au, start + max(n - 2, 0))
                    if what == "max" and detail == (0, 0):
                        pe.wait_ge(s_qk[to % NG], 16 * LOADS * (b + to // NG + 1))
                    if what == "norm":
                        last_of["norm"] = start + n + 1
                    if what == "turn":
                        last_of["turn"] = start + n + 1
                    a_unit(what, to, detail, n % 3, start + n, b,
                           last_of.get("norm" if what == "turn" else "turn"))

            def body(kind, b):
                at, start, n0, u0, last_of = kinds[kind], base(kind, b), 0, 0, {}
                for g in range(NG):
                    t = NG * b + g
                    for r in range(NQ):
                        j, c, q0, w = KEY_QUADS[r]
                        todo = list(at[g, r])
                        maxes = [u for u in todo if u[0] == "max"]
                        if r == 0:
                            pe.wait_ge(s_m[g], 16 * (b + 1))
                            pe.wait_ge(s_vin[g], 16 * (b + 1))
                        pieces = list(range(0, GH, per_bank(w)))
                        for x, h0 in enumerate(pieces):
                            if maxes:
                                run([maxes.pop(0)], start, n0, b, last_of)
                                n0 += 1
                            pe.wait_ge(s_e, B_UNITS * b + max(u0 - 2, 0))
                            for s in range(per_bank(w)):
                                h = h0 + s
                                piece = bbank[u0 % 3][:, s * w:(s + 1) * w]
                                diagonal = q0 == j * P
                                mm = pe.matmul(piece, k_op[g][0:KB, h, j * P:(j + 1) * P], q_op[g][0:KB, h, q0:q0 + w],
                                               start=True, stop=not diagonal)
                                if diagonal:
                                    mm = pe.matmul(piece[:, 0:P], identb[:, :], bmask[:, :], start=False, stop=True)
                            mm.then_inc(s_b, 1)
                            u0 += 1
                            if x == min(2, len(pieces) - 1):
                                weigh(kind, b, g, r - 1, u0 - x - 1)
                        rest = maxes + [u for u in todo if u[0] != "max"]
                        run(rest, start, n0, b, last_of)
                        n0 += len(rest)
                if kind == "last":
                    weigh(kind, b, NG, -1, u0)
                assert n0 == count[kind] and u0 == B_UNITS

            def weigh(kind, b, g, r, units):
                if r < 0:
                    if kind == "first" and g == 0:
                        return
                    r, g = NQ - 1, g - 1
                j, c, q0, w = KEY_QUADS[r]
                pe.wait_ge(s_e, B_UNITS * b + units)
                if j == 0 and not (kind == "first" and g == 0):
                    pe.wait_ge(s_yu, 2 * (NG * b + g - 1) + c + 1)
                for h in range(GH):
                    mm = pe.matmul(ybank[c][32 * h:32 * h + 32, q0 - 512 * c:q0 - 512 * c + w],
                                   v[g % NG][:, j, h * VW:h * VW + 32], prob[:, r % 2, h, 0:w],
                                   start=(j == 0), stop=(j == (QT // 2 if c == 0 else QT) - 1))
                mm.then_inc(s_pv, 1)

            pe.wait_ge(s_c, 16 * (5 + 3 * NG))
            pe.wait_ge(s_set, 1)
            run(PRO, 0, 0, 0, {})
            body("first", 0)
            with pe.Fori(1, B - 1) as b:
                body("mid", b)
            body("last", B - 1)
            run(TAIL, TAIL_BASE, 0, B, {})

        @block.scalar
        def _(act):
            LAST_OUT = {k: 1 + max(n for n, u in enumerate(u for g in range(NG) for r in range(NQ) for u in at[g, r])
                                   if u[0] == "out") for k, at in kinds.items() if k != "first"}

            def copy_y(b, g, c):
                t = NG * b + g
                act.wait_ge(s_pv, NQ * t + (4 if c == 0 else NQ))
                nc.scalar.copy(yu[:, c, :], ybank[c][:, :]).then_inc(s_yu, 1)

            def body(kind, b):
                seen, u0 = base(kind, b), 0
                used = {} if kind == "first" else {0: seen, 1: seen}
                for g in range(NG):
                    if g == 0 and kind != "first":
                        act.wait_ge(s_au, base(kind, b))
                        act.dma_start(res[:, :, :], resd[b - 1]).then_inc(s_res, 16)
                    if g == 1 and kind != "first":
                        act.wait_ge(s_au, base(kind, b) + LAST_OUT[kind])
                        act.dma_start(outd[b - 1], o[:, :, :]).then_inc(s_out, 16)
                    for r in range(NQ):
                        j, c, q0, w = KEY_QUADS[r]
                        if not (kind == "first" and g == 0 and r < 2):
                            act.wait_ge(s_pv, NG * NQ * b + NQ * g + r - 1)
                        for h0 in range(0, GH, per_bank(w)):
                            act.wait_ge(s_b, B_UNITS * b + u0 + 1)
                            m = per_bank(w)
                            nc.scalar.activation(prob[:, r % 2, h0:h0 + m, 0:w],
                                                 bbank[u0 % 3][:, 0:m * w].rearrange("p (h n) -> p h n", h=m),
                                                 ACT.Exp).then_inc(s_e, 1)
                            u0 += 1
                        for what, to, detail in kinds[kind][g, r]:
                            seen = seen + 1
                            if what == "norm":
                                used[detail] = seen
                        if r == 0 and not (kind == "first" and g == 0):
                            if used.get(1) is not None:
                                act.wait_ge(s_au, used[1])
                            copy_y(b, g - 1, 1)
                        if r == 4:
                            if used.get(0) is not None:
                                act.wait_ge(s_au, used[0])
                            copy_y(b, g, 0)

            act.wait_ge(s_set, 1)
            body("first", 0)
            with act.Fori(1, B - 1) as b:
                body("mid", b)
            body("last", B - 1)
            act.wait_ge(s_au, TAIL_BASE)
            act.dma_start(res[:, :, :], resd[B - 1]).then_inc(s_res, 16)
            copy_y(B - 1, NG - 1, 1)
            act.wait_ge(s_au, TAIL_BASE + len(TAIL))
            act.dma_start(outd[B - 1], o[:, :, :]).then_inc(s_out, 16)
            act.wait_ge(s_out, 16 * B)

        @block.vector
        def _(dve):
            V = nc.vector

            def unit(what, to, detail, n, seen, b, link):
                bk = abank[n]
                dve.wait_ge(s_a, seen + 1)
                if what == "max":
                    z = to % 2
                    q, h0 = detail
                    i, k0, w = QUERY_QUADS[q]
                    m = per_bank(w)
                    dst = mx[:, z, h0:h0 + m, i] if i < QT // 2 else mx2[:, z, k0 // 512, h0:h0 + m, i - QT // 2]
                    V.tensor_reduce(dst, bk[:, 0:m * w].rearrange("p (h n) -> p h n", h=m), AX.X,
                                    ALU.max).then_inc(s_au, 1)
                    if q == NQ - 1 and h0 + m == GH:
                        parts(to, seen + 1, link, b)
                elif what == "rows":
                    if not (isinstance(b, int) and b == 0 and to == 0):
                        dve.wait_ge(s_mw, 16 * (NG * b + to))
                    V.tensor_copy(mrows[:, :], abf[n][0:3 * GH * QT, 0:P]).then_inc(s_au, 1)
                elif what == "norm":
                    piece = bk[:, :].rearrange("p (t h n) -> p t h n", t=4, h=GH)
                    link(V.reciprocal(rec[:, detail, :, :], piece[:, :, :, HD]))
                    g = to % NG
                    for t in range(4):
                        i = V.tensor_tensor(
                            y[:, 4 * detail + t, g * GH * HD:(g + 1) * GH * HD].rearrange("p (h d) -> p h d", d=HD),
                            piece[:, t, :, 0:HD],
                            rec[:, detail, t, :].rearrange("p (h o) -> p h o", o=1).to_broadcast([P, GH, HD]), ALU.mult)
                    i.then_inc(s_au, 1)
                elif what == "turn":
                    k, half = divmod(detail, 2)
                    V.tensor_copy(yT[:, k, half * 512:(half + 1) * 512], bk[:, :]).then_inc(s_au, 1)
                else:
                    if detail == 0:
                        dve.wait_ge(s_res, 16 * b)
                        if not (isinstance(b, int) and b == 1):
                            dve.wait_ge(s_out, 16 * (b - 1))
                    V.tensor_tensor(o[:, 2 * detail:2 * detail + 2, :], bk[:, :].rearrange("p (t n) -> p t n", t=2),
                                    res[:, 2 * detail:2 * detail + 2, :], ALU.add).then_inc(s_au, 1)

            def parts(to, seen, link, b):
                z = to % 2
                dve.wait_ge(s_au, seen)
                link(V.tensor_tensor(mx[:, z, :, QT // 2:QT], mx2[:, z, 0, :, :], mx2[:, z, 1, :, :], ALU.max))
                flat = mx[:, z, :, :].rearrange("p h i -> p (h i)")
                link(V.tensor_scalar(mpart[:, 0, :], flat, -1.0, None, ALU.mult))
                link(V.scalar_tensor_tensor(mrest[:, :], flat, -1.0, mpart[:, 0, :], ALU.mult, ALU.subtract))
                link(V.tensor_copy(mpart[:, 1, :], mrest[:, :]))
                V.tensor_tensor(mpart[:, 2, :], mrest[:, :], mpart[:, 1, :], ALU.subtract).then_inc(s_mp, 1)

            def links_of(units):
                return sum(4 if (w == "max" and d[0] == NQ - 1 and d[1] + per_bank(QUERY_QUADS[d[0]][2]) == GH)
                           else 1 if w == "norm" else 0 for w, _, d in units)

            in_body = {k: [u for g in range(NG) for r in range(NQ) for u in at[g, r]] for k, at in kinds.items()}
            n_links = {k: links_of(u) for k, u in in_body.items()}

            def body(kind, b):
                start = base(kind, b)
                lb = links_of(PRO) if kind == "first" else links_of(PRO) + n_links["first"] + n_links["mid"] * (b - 1)
                link = Chain(dve, s_link, lb)
                for n, (what, to, detail) in enumerate(in_body[kind]):
                    unit(what, to, detail, n % 3, start + n, b, link)
                assert link.n == n_links[kind]

            for g in range(NG):
                i = V.memset(v[g][:, :, GH * VW:VPAD], 0.0)
            i.then_inc(s_set, 1)
            dve.wait_ge(s_set, 1)
            pro = Chain(dve, s_link)
            for n, (what, to, detail) in enumerate(PRO):
                unit(what, to, detail, n % 3, n, 0, pro)
            body("first", 0)
            with dve.Fori(1, B - 1) as b:
                body("mid", b)
            body("last", B - 1)
            link = Chain(dve, s_link, links_of(PRO) + n_links["first"] + n_links["mid"] * (B - 2) + n_links["last"])
            for n, (what, to, detail) in enumerate(TAIL):
                unit(what, to, detail, n % 3, TAIL_BASE + n, B, link)


def kernel(**inputs):
    import numpy as np
    import concourse.bacc as bacc
    from concourse.bass_utils import run_bass_kernel_spmd as run

    nc = bacc.Bacc("TRN2", target_bir_lowering=False, num_devices=1)
    arrays, a = {}, {}

    def give(name, array):
        array = np.ascontiguousarray(array)
        arrays[f"in_{name}"] = array
        a[name] = nc.dram_tensor(f"in_{name}", array.shape, mybir.dt.from_np(array.dtype), kind="ExternalInput").ap()

    turned = {"WqT": "L0_attn_Wq", "WkT": "L0_attn_Wk", "WvT": "L0_attn_Wv", "WoT": "L0_attn_Wo",
              "WlqT": "L0_attn_Wlq", "WlkT": "L0_attn_Wlk", "WlvT": "L0_attn_Wlv", "W0T": "L0_ffn_W",
              "ldT": "L0_ffn_lora_down", "luT": "L0_ffn_lora_up", "uaT": "L0_ffn_up_aux",
              "WrT": "L1_ffn_W_r", "WkkT": "L1_ffn_W_k", "WvvT": "L1_ffn_W_v"}
    plain = {"x": "L0_attn_x", "bq": "L0_attn_bq", "bv": "L0_attn_bv", "bo": "L0_attn_bo",
             "lna_w": "L0_attn_lna_w", "lnc_w": "L0_attn_lnc_w", "lnd_w": "L0_attn_lnd_w",
             "blq": "L0_attn_blq", "blk": "L0_attn_blk", "blv": "L0_attn_blv",
             "down_aux": "L0_ffn_down_aux", "b0": "L0_ffn_b", "q_w": "L1_attn_q_w",
             "kv_w": "L1_attn_kv_w", "kv_b": "L1_attn_kv_b", "o_w": "L1_attn_o_w", "o_b": "L1_attn_o_b"}
    for name, of in turned.items():
        give(name, np.asarray(inputs[of]).T)
    for name, of in plain.items():
        give(name, inputs[of])
    for name in ("temp", "threshold", "factor"):
        give(name, np.asarray(inputs["L0_attn_" + name]).reshape(1))

    for name, vec in (("mu_r_col", inputs["L1_ffn_mu_r"]), ("mu_k_col", inputs["L1_ffn_mu_k"]),
                      ("q_b_col", inputs["L1_attn_q_b"]), ("k_b_col", np.asarray(inputs["L1_attn_kv_b"])[0:D])):
        give(name, np.asarray(vec).reshape(DC, P).T)

    bf16 = np.dtype("bfloat16")
    p = np.arange(P)
    t = np.arange(T)
    head = np.arange(1, NH + 1)
    later = np.where(p[None, :] > p[:, None], BIG, 0.0)
    give("ident", np.eye(P, dtype=np.float32))
    give("identb", np.eye(P).astype(bf16))
    give("amask", later.astype(bf16))
    give("bmask", later.T.astype(bf16))
    give("headmask", (p[:, None] // HD == np.arange(HPC)[None, :]).astype(np.float32))
    give("batchmask", np.where(p[:, None] // E0 == p[None, :] // E0, 0.0, BIG).astype(np.float32))
    k_pos = np.stack([t - t % 8, t % 8, np.full(T, 8)]).astype(bf16)
    slope = np.broadcast_to(head[:, None] / NH, (NH, T))
    q_pos = np.stack([slope, slope, -head[:, None] * (t // P)[None, :]]).astype(bf16)
    give("k_pos", np.broadcast_to(k_pos[:, None, :], (NPOS, GH, T)))
    give("k_one", np.ones((3, GH, T)).astype(bf16))
    give("q_pos", q_pos)

    def scratch(name, shape, dt=FP32):
        return nc.dram_tensor(name, shape, dt, kind="Internal").ap()

    scr = {"w0": scratch("scr_w0", (D, D)), "attn0": scratch("scr_attn0", (B * E0, D)),
           "qs": scratch("scr_q", (3, B, D, T), BF16), "ks": scratch("scr_k", (3, B, D, T), BF16),
           "v": scratch("scr_v", (B, T, NH * VW)), "res": scratch("scr_res", (B, T, D)),
           "m": scratch("scr_m", (NG, 3 * GH * QT, P), BF16)}
    out = nc.dram_tensor("out", (B, T, D), FP32, kind="ExternalOutput").ap()
    prepare(nc, a, scr)
    project(nc, a, scr)
    attend(nc, a, scr, out)
    r = run(nc, [arrays], core_ids=[0])
    return r.results[0]["out"]
```

```python
import concourse.bass as bass
from concourse import mybir
from contextlib import ExitStack

FP32 = mybir.dt.float32
BF16 = mybir.dt.bfloat16
FP32R = mybir.dt.float32r
ALU = mybir.AluOpType
ACT = mybir.ActivationFunctionType
AX = mybir.AxisListType

P = 128
B, T, D = 16, 1024, 256
NH, HD = 16, 16
DC = D // P
E0 = 16
RT = B * E0 // P
BPT = P // E0
HPC = P // HD
MS = 512
TPM = MS // P
STEPS = B * T // MS
GH = 4
NG = NH // GH
QT = T // P
VW = HD + 1
VPAD = GH * VW + 32 - VW
NPOS = 3
NSLOT = 6
KA = NPOS + NSLOT * HD
KB = KA + 3
Q_PART = [0, 0, 0, 1, 1, 2]
K_PART = [0, 1, 2, 0, 1, 0]
EPS = 1e-5
BIG = -1e30
LEAD = 5


class Chain:

    def __init__(self, eng, sem, base=0):
        self.eng, self.sem, self.base, self.n = eng, sem, base, 0

    def __call__(self, ins):
        self.n += 1
        ins.then_inc(self.sem, 1)
        self.eng.wait_ge(self.sem, self.base + self.n)


def prepare(nc, a, scr):
    ctx = ExitStack()
    with ctx:
        def sb(name, shape, dt=FP32):
            return ctx.enter_context(nc.sbuf_tensor(name, shape, dt))

        def pb(name, shape, dt=FP32):
            return ctx.enter_context(nc.psum_tensor(name, shape, dt))

        def sem(name):
            return ctx.enter_context(nc.semaphore(name))

        ident = sb("p_ident", [P, P])
        ones = sb("p_ones", [P, P])
        ldT = sb("p_ldT", [100, 4])
        da = sb("p_da", [100, D])
        luT = sb("p_luT", [4, 50])
        uaT = sb("p_uaT", [50, D])
        t1 = sb("p_t1", [4, D])
        t2 = sb("p_t2", [50, D])
        wt = sb("p_wt", [P, DC, D])
        x = sb("p_x", [P, RT, D])
        xn = sb("p_xn", [P, RT, D])
        lna = sb("p_lna", [P, D])
        stats = sb("p_stats", [P, RT, 6])
        mv = sb("p_mv", [P, RT, 2])
        ve = sb("p_ve", [P, 32])
        rstd = sb("p_rstd", [P, 32])
        neghalf = sb("p_neghalf", [P, 32])
        xT = sb("p_xT", [P, DC, RT * P])
        wqkv = sb("p_wqkv", [P, 3, DC, D])
        wo = sb("p_wo", [P, DC, D])
        bqv = sb("p_bqv", [P, 2, D])
        bd = sb("p_bd", [P, 3, P])
        bl = sb("p_bl", [P, 3, HD])
        lnw = sb("p_lnw", [P, 2, HD])
        cur = [sb(f"p_cur{i}", [P, RT, D]) for i in range(3)]
        curT = [sb(f"p_curT{i}", [P, DC, RT * P]) for i in range(3)]
        lat = [sb(f"p_lat{i}", [P, RT, D]) for i in range(3)]
        nrm = [sb(f"p_nrm{i}", [P, RT, D]) for i in range(2)]
        nrmT = [sb(f"p_nrmT{i}", [P, DC, RT * P]) for i in range(2)]
        sq = sb("p_sq", [P, RT, D])
        mean = sb("p_mean", [P, RT * NH])
        hmask = sb("p_hmask", [P, HPC])
        bmask = sb("p_bmask", [P, P])
        kx = sb("p_kx", [P, 2, HPC, P])
        s = sb("p_s", [P, 2, HPC, P])
        smax = sb("p_smax", [P, 2, HPC])
        ssum = sb("p_ssum", [P, 2, HPC])
        pT = sb("p_pT", [P, 2, HPC, P])
        ai = [sb(f"p_ai{i}", [P, RT, D]) for i in range(3)]
        dsum = sb("p_dsum", [P, 8])
        sc = sb("p_sc", [P, 3])
        tsc = sb("p_tsc", [P, 4])
        pbank = [pb(f"p_b{i}", [P, 1024]) for i in range(4)]

        s_in = sem("p_loaded")
        s_const = sem("p_const")
        s_lora_pe = sem("p_lora_pe")
        s_lora = sem("p_lora")
        s_var = sem("p_var")
        s_rstd = sem("p_rstd")
        s_xn = sem("p_xn")
        s_xT_pe = sem("p_xT_pe")
        s_xT = sem("p_xT")
        s_qkv_pe = sem("p_qkv_pe")
        s_cur = sem("p_cur")
        s_curT_pe = sem("p_curT_pe")
        s_curT = sem("p_curT")
        s_lat_pe = sem("p_lat_pe")
        s_nrm = sem("p_nrm")
        s_nrmT_pe = sem("p_nrmT_pe")
        s_nrmT = sem("p_nrmT")
        s_kx = sem("p_kx")
        s_sc_pe = sem("p_scores_pe")
        s_sub = sem("p_sub")
        s_exp = sem("p_exp")
        s_turn_pe = sem("p_turn_pe")
        s_pT = sem("p_pT")
        s_pv_pe = sem("p_pv_pe")
        s_ai = sem("p_ai")
        s_dif = sem("p_dif")
        s_dif_pe = sem("p_dif_pe")
        s_sel = sem("p_sel")
        s_oT_pe = sem("p_oT_pe")
        s_oT = sem("p_oT")
        s_o_pe = sem("p_o_pe")
        s_o = sem("p_o")
        s_out = sem("p_stored")
        s_link = sem("p_dve_link")

        UN = DC * RT
        flat = lambda t: t.rearrange("p h n -> p (h n)")
        heads = lambda t: t[:, :, :].rearrange("p r (h d) -> p (r h) d", d=HD)
        whole = lambda bank: bank[:, 0:RT * D].rearrange("p (r n) -> p r n", r=RT)
        col = lambda t: t.rearrange("p (h o) -> p h o", o=1)

        block = ctx.enter_context(nc.Block())
        lo = [(ident[:, :], a["ident"]), (ldT[:, :], a["ldT"]), (da[:, :], a["down_aux"]),
              (luT[:, :], a["luT"]), (uaT[:, :], a["uaT"]),
              (wt[:, :, :], a["W0T"].rearrange("(k p) n -> p k n", p=P)),
              (lna[:, :], a["lna_w"].partition_broadcast(P)),
              (wo[:, :, :], a["WoT"].rearrange("(k p) n -> p k n", p=P)),
              (bqv[:, 0, :], a["bq"].partition_broadcast(P)),
              (bqv[:, 1, :], a["bv"].partition_broadcast(P)),
              (lnw[:, 0, :], a["lnc_w"].partition_broadcast(P)),
              (lnw[:, 1, :], a["lnd_w"].partition_broadcast(P)),
              (hmask[:, :], a["headmask"]), (bmask[:, :], a["batchmask"]),
              (sc[:, 0:1], a["temp"].partition_broadcast(P)),
              (sc[:, 1:2], a["threshold"].partition_broadcast(P)),
              (sc[:, 2:3], a["factor"].partition_broadcast(P))]
        for n, w in enumerate(("WqT", "WkT", "WvT")):
            lo.append((wqkv[:, n, :, :], a[w].rearrange("(k p) n -> p k n", p=P)))
        for n, w in enumerate(("blq", "blk", "blv")):
            lo.append((bl[:, n, :], a[w].partition_broadcast(P)))
        for b in range(B):
            at = b % BPT * E0
            lo.append((x[at:at + E0, b // BPT, :], a["x"][b, 0:E0, :]))
        n_loads = 16 * (len(lo) + 3 * HPC)

        @block.sync
        def _(sp):
            for dst, src in lo:
                sp.dma_start(dst, src).then_inc(s_in, 16)
            sp.wait_ge(s_const, 3)
            for n, w in enumerate(("WlqT", "WlkT", "WlvT")):
                for h in range(HPC):
                    sp.dma_start(bd[h * HD:(h + 1) * HD, n, h * HD:(h + 1) * HD], a[w]).then_inc(s_in, 16)
            sp.wait_ge(s_lora, 3)
            sp.dma_start(scr["w0"].rearrange("(k p) n -> p k n", p=P), wt[:, :, :]).then_inc(s_out, 16)
            sp.wait_ge(s_o, 1)
            sp.dma_start(scr["attn0"].rearrange("(r p) n -> p r n", p=P), xn[:, :, :]).then_inc(s_out, 16)
            sp.wait_ge(s_out, 32)

        @block.gpsimd
        def _(pool):
            pool.memset(ones[:, :], 1.0).then_inc(s_const, 1)
            pool.memset(bd[:, :, :], 0.0).then_inc(s_const, 1)
            pool.memset(neghalf[:, :], -0.5).then_inc(s_const, 1)
            pool.wait_ge(s_const, 3)
            for n in range(2):
                pool.wait_ge(s_var, n + 1)
                pool.tensor_tensor(rstd[:, 0:RT], ve[:, 0:RT], neghalf[:, 0:RT], ALU.pow).then_inc(s_rstd, 1)
            for it in range(3):
                pool.wait_ge(s_var, 3 * it + 3)
                pool.tensor_tensor(tsc[:, 0:1], tsc[:, 3:4], neghalf[:, 0:1], ALU.pow).then_inc(s_rstd, 1)
                for n in range(2):
                    pool.wait_ge(s_var, 3 * it + 4 + n)
                    pool.tensor_tensor(rstd[:, :], ve[:, :], neghalf[:, :], ALU.pow).then_inc(s_rstd, 1)

        @block.tensor
        def _(pe):
            def turn_rows(bank, src):
                for k in range(DC):
                    for r in range(RT):
                        at = (k * RT + r) * P
                        mm = pe.transpose(bank[:, at:at + P], src[:, r, k * P:(k + 1) * P], ident[:, :])
                return mm

            pe.wait_ge(s_in, n_loads)
            pe.wait_ge(s_const, 3)
            pe.matmul(pbank[0][0:4, 0:D], ldT[:, :], da[:, :], start=True, stop=True).then_inc(s_lora_pe, 1)
            pe.wait_ge(s_lora, 1)
            pe.matmul(pbank[0][0:50, 0:D], luT[:, :], t1[:, :], start=True, stop=True).then_inc(s_lora_pe, 1)
            pe.wait_ge(s_lora, 2)
            for k in range(DC):
                mm = pe.matmul(pbank[0][:, k * D:(k + 1) * D], t2[:, k * P:(k + 1) * P], uaT[:, :],
                               start=True, stop=True)
            mm.then_inc(s_lora_pe, 1)
            pe.wait_ge(s_xn, 1)
            turn_rows(pbank[1], xn).then_inc(s_xT_pe, 1)
            pe.wait_ge(s_xT, 1)
            pe.wait_ge(s_lora, 3)
            for n in range(3):
                for r in range(RT):
                    for k in range(DC):
                        mm = pe.matmul(pbank[n][:, r * D:(r + 1) * D], xT[:, k, r * P:(r + 1) * P],
                                       wqkv[:, n, k, :], start=(k == 0), stop=(k == DC - 1))
                mm.then_inc(s_qkv_pe, 1)
            for it in range(3):
                pe.wait_ge(s_cur, it + 1)
                for n in range(3):
                    src = cur[n] if n == 0 or it == 0 else lat[n]
                    turn_rows(pbank[n], src).then_inc(s_curT_pe, 1)
                for n in range(3):
                    pe.wait_ge(s_curT, 3 * it + n + 1)
                    for r in range(RT):
                        for k in range(DC):
                            at = r * D + k * P
                            mm = pe.matmul(pbank[n][:, at:at + P], curT[n][:, k, r * P:(r + 1) * P],
                                           bd[:, n, :], start=True, stop=True)
                    mm.then_inc(s_lat_pe, 1)
                for n in range(2):
                    pe.wait_ge(s_nrm, 2 * it + n + 1)
                    turn_rows(pbank[n], nrm[n]).then_inc(s_nrmT_pe, 1)
                pe.wait_ge(s_nrmT, 2 * it + 2)

                def scores(u):
                    g, k, r, z = UN * it + u, u // RT, u % RT, u % 2
                    pe.wait_ge(s_kx, g + 1)
                    if g >= 2:
                        pe.wait_ge(s_pT, g - 1)
                    for c in range(2):
                        mm = pe.matmul(pbank[2 + z][:, c * 512:(c + 1) * 512], nrmT[0][:, k, r * P:(r + 1) * P],
                                       flat(kx[:, z, c * 4:(c + 1) * 4, :]), start=True, stop=True)
                    mm.then_inc(s_sc_pe, 1)

                def weigh(u):
                    g, k, r, z = UN * it + u, u // RT, u % RT, u % 2
                    pe.wait_ge(s_exp, g + 1)
                    for h in range(HPC):
                        mm = pe.transpose(pbank[2 + z][:, h * P:(h + 1) * P], s[:, z, h, :], ident[:, :])
                    mm.then_inc(s_turn_pe, 1)
                    pe.wait_ge(s_pT, g + 1)
                    if g >= 2:
                        pe.wait_ge(s_ai, g - 1)
                    for h in range(HPC):
                        at = k * P + h * HD
                        mm = pe.matmul(pbank[z][:, h * HD:(h + 1) * HD], pT[:, z, h, :],
                                       lat[2][:, r, at:at + HD], start=True, stop=True)
                    mm.then_inc(s_pv_pe, 1)

                scores(0)
                for u in range(1, UN):
                    scores(u)
                    weigh(u - 1)
                weigh(UN - 1)
                if it == 1:
                    pe.wait_ge(s_dif, 1)
                    pe.matmul(pbank[0][:, 512:513], ones[:, :], dsum[:, 0:1], start=True, stop=True).then_inc(s_dif_pe, 1)
            pe.wait_ge(s_sel, 1)
            turn_rows(pbank[0], ai[2]).then_inc(s_oT_pe, 1)
            pe.wait_ge(s_oT, 1)
            for r in range(RT):
                for k in range(DC):
                    mm = pe.matmul(pbank[1][:, r * D:(r + 1) * D], xT[:, k, r * P:(r + 1) * P], wo[:, k, :],
                                   start=(k == 0), stop=(k == DC - 1))
            mm.then_inc(s_o_pe, 1)

        @block.scalar
        def _(act):
            for it in range(3):
                for n in range(3):
                    act.wait_ge(s_curT_pe, 3 * it + n + 1)
                    nc.scalar.copy(curT[n][:, :, :], whole(pbank[n])).then_inc(s_curT, 1)
                for n in range(2):
                    act.wait_ge(s_nrmT_pe, 2 * it + n + 1)
                    nc.scalar.copy(nrmT[n][:, :, :], whole(pbank[n])).then_inc(s_nrmT, 1)

                def exps(u):
                    g, z = UN * it + u, u % 2
                    act.wait_ge(s_sub, g + 1)
                    nc.scalar.activation(flat(s[:, z, :, :]), flat(s[:, z, :, :]), ACT.Exp).then_inc(s_exp, 1)

                def copies(u):
                    g, z = UN * it + u, u % 2
                    act.wait_ge(s_turn_pe, g + 1)
                    if g >= 2:
                        act.wait_ge(s_pv_pe, g - 1)
                    nc.scalar.copy(flat(pT[:, z, :, :]), pbank[2 + z][:, :]).then_inc(s_pT, 1)

                exps(0)
                for u in range(1, UN):
                    copies(u - 1)
                    exps(u)
                copies(UN - 1)

        @block.vector
        def _(dve):
            V = nc.vector
            link = Chain(dve, s_link)
            dve.wait_ge(s_in, n_loads)
            dve.wait_ge(s_const, 3)
            dve.wait_ge(s_lora_pe, 1)
            V.tensor_copy(t1[:, :], pbank[0][0:4, 0:D]).then_inc(s_lora, 1)
            dve.wait_ge(s_lora_pe, 2)
            V.tensor_copy(t2[:, :], pbank[0][0:50, 0:D]).then_inc(s_lora, 1)
            dve.wait_ge(s_lora_pe, 3)
            V.tensor_tensor(wt[:, :, :], wt[:, :, :], pbank[0][:, 0:DC * D].rearrange("p (k n) -> p k n", k=DC),
                            ALU.add).then_inc(s_lora, 1)
            for n in range(2):
                src = x if n == 0 else xn
                for r in range(RT):
                    link(V.bn_stats(stats[:, r, :], src[:, r, :]))
                    link(V.bn_aggr(mv[:, r, :], stats[:, r, :]))
                V.tensor_scalar(ve[:, 0:RT], mv[:, :, 1], EPS, None, ALU.add).then_inc(s_var, 1)
                dve.wait_ge(s_rstd, n + 1)
                for r in range(RT):
                    link(V.tensor_scalar(xn[:, r, :], src[:, r, :], mv[:, r, 0:1], rstd[:, r:r + 1],
                                         ALU.subtract, ALU.mult))
            V.tensor_tensor(xn[:, :, :], xn[:, :, :],
                            lna[:, :].rearrange("p (o n) -> p o n", o=1).to_broadcast([P, RT, D]),
                            ALU.mult).then_inc(s_xn, 1)
            dve.wait_ge(s_xT_pe, 1)
            V.tensor_copy(xT[:, :, :], whole(pbank[1])).then_inc(s_xT, 1)
            scale = HD ** -0.25
            dve.wait_ge(s_qkv_pe, 1)
            link(V.tensor_tensor(cur[0][:, :, :], whole(pbank[0]), bqv[:, 0:1, :].to_broadcast([P, RT, D]), ALU.add))
            link(V.tensor_scalar(cur[0][:, :, :], cur[0][:, :, :], scale, None, ALU.mult))
            dve.wait_ge(s_qkv_pe, 2)
            link(V.tensor_scalar(cur[1][:, :, :], whole(pbank[1]), scale, None, ALU.mult))
            dve.wait_ge(s_qkv_pe, 3)
            V.tensor_tensor(cur[2][:, :, :], whole(pbank[2]), bqv[:, 1:2, :].to_broadcast([P, RT, D]),
                            ALU.add).then_inc(s_cur, 1)
            for it in range(3):
                for n in range(3):
                    dve.wait_ge(s_lat_pe, 3 * it + n + 1)
                    link(V.tensor_tensor(heads(lat[n]), pbank[n][:, 0:RT * D].rearrange("p (h d) -> p h d", d=HD),
                                         bl[:, n:n + 1, :].to_broadcast([P, RT * NH, HD]), ALU.add))
                link(V.tensor_scalar(tsc[:, 1:2], sc[:, 0:1], 0.005 * it, None, ALU.add))
                link(V.tensor_scalar(tsc[:, 2:3], tsc[:, 1:2], 0.0, None, ALU.is_gt))
                link(V.tensor_scalar(tsc[:, 1:2], tsc[:, 1:2], tsc[:, 2:3], None, ALU.mult))
                link(V.tensor_scalar(tsc[:, 2:3], tsc[:, 2:3], -1.0, 1.0, ALU.mult, ALU.add))
                V.tensor_tensor(tsc[:, 3:4], tsc[:, 1:2], tsc[:, 2:3], ALU.add).then_inc(s_var, 1)
                for n in range(2):
                    link(V.tensor_reduce(mean[:, :], heads(lat[n]), AX.X, ALU.add))
                    link(V.tensor_scalar(mean[:, :], mean[:, :], 1.0 / HD, None, ALU.mult))
                    link(V.tensor_tensor(heads(nrm[n]), heads(lat[n]),
                                         col(mean[:, :]).to_broadcast([P, RT * NH, HD]), ALU.subtract))
                    link(V.tensor_tensor(sq[:, :, :], nrm[n][:, :, :], nrm[n][:, :, :], ALU.mult))
                    link(V.tensor_reduce(ve[:, :], heads(sq), AX.X, ALU.add))
                    V.tensor_scalar(ve[:, :], ve[:, :], 1.0 / HD, EPS, ALU.mult, ALU.add).then_inc(s_var, 1)
                    link(V.tensor_tensor(heads(nrm[n]), heads(nrm[n]),
                                         lnw[:, n:n + 1, :].to_broadcast([P, RT * NH, HD]), ALU.mult))
                    dve.wait_ge(s_rstd, 3 * it + 4 + n)
                    norm = V.tensor_tensor(heads(nrm[n]), heads(nrm[n]),
                                           col(rstd[:, :]).to_broadcast([P, RT * NH, HD]), ALU.mult)
                    if n == 1:
                        norm.then_inc(s_nrm, 1)
                    else:
                        link(norm)
                        V.tensor_scalar(nrm[0][:, :, :], nrm[0][:, :, :], tsc[:, 0:1], None,
                                        ALU.mult).then_inc(s_nrm, 1)
                dve.wait_ge(s_nrmT, 2 * it + 2)

                def keys(u):
                    g, k, r, z = UN * it + u, u // RT, u % RT, u % 2
                    if g >= 2:
                        dve.wait_ge(s_sc_pe, g - 1)
                    V.tensor_tensor(kx[:, z, :, :],
                                    nrmT[1][:, k:k + 1, r * P:(r + 1) * P].to_broadcast([P, HPC, P]),
                                    col(hmask[:, :]).to_broadcast([P, HPC, P]), ALU.mult).then_inc(s_kx, 1)

                def shifted(u):
                    g, z = UN * it + u, u % 2
                    dve.wait_ge(s_sc_pe, g + 1)
                    if g >= 2:
                        dve.wait_ge(s_turn_pe, g - 1)
                    link(V.scalar_tensor_tensor(
                        s[:, z, :, :], pbank[2 + z][:, :].rearrange("p (h n) -> p h n", n=P), HD ** -0.5,
                        bmask[:, :].rearrange("p (o n) -> p o n", o=1).to_broadcast([P, HPC, P]),
                        ALU.mult, ALU.add))
                    link(V.tensor_reduce(smax[:, z, :], s[:, z, :, :], AX.X, ALU.max))
                    V.tensor_tensor(s[:, z, :, :], s[:, z, :, :], col(smax[:, z, :]).to_broadcast([P, HPC, P]),
                                    ALU.subtract).then_inc(s_sub, 1)

                def result(u):
                    g, k, r, z = UN * it + u, u // RT, u % RT, u % 2
                    dve.wait_ge(s_exp, g + 1)
                    link(V.tensor_reduce(ssum[:, z, :], s[:, z, :, :], AX.X, ALU.add))
                    link(V.reciprocal(ssum[:, z, :], ssum[:, z, :]))
                    dve.wait_ge(s_pv_pe, g + 1)
                    V.tensor_tensor(ai[it][:, r, k * P:(k + 1) * P].rearrange("p (h d) -> p h d", d=HD),
                                    pbank[z][:, 0:P].rearrange("p (h d) -> p h d", d=HD),
                                    col(ssum[:, z, :]).to_broadcast([P, HPC, HD]), ALU.mult).then_inc(s_ai, 1)

                keys(0)
                keys(1)
                shifted(0)
                for u in range(1, UN):
                    shifted(u)
                    if u + 1 < UN:
                        keys(u + 1)
                    result(u - 1)
                result(UN - 1)
                dve.wait_ge(s_ai, UN * (it + 1))
                if it == 1:
                    link(V.tensor_tensor(sq[:, :, :], ai[1][:, :, :], ai[0][:, :, :], ALU.subtract))
                    V.tensor_reduce(dsum[:, 0:1], sq[:, :, :], AX.XY, ALU.add,
                                    apply_absolute_value=True).then_inc(s_dif, 1)
                    dve.wait_ge(s_dif_pe, 1)
                    link(V.tensor_scalar(dsum[:, 1:2], pbank[0][:, 512:513], 1.0 / (B * T * D), None, ALU.mult))
                    link(V.tensor_scalar(dsum[:, 2:3], dsum[:, 1:2], sc[:, 2:3], sc[:, 1:2], ALU.mult, ALU.add))
                    link(V.tensor_tensor(dsum[:, 3:4], dsum[:, 1:2], dsum[:, 2:3], ALU.is_lt))
                    link(V.tensor_scalar(dsum[:, 4:5], dsum[:, 3:4], -1.0, 1.0, ALU.mult, ALU.add))
                if it < 2:
                    V.tensor_tensor(cur[0][:, :, :], cur[0][:, :, :], ai[it][:, :, :], ALU.add).then_inc(s_cur, 1)
            link(V.tensor_scalar(ai[1][:, :, :], ai[1][:, :, :], dsum[:, 3:4], None, ALU.mult))
            V.scalar_tensor_tensor(flat(ai[2][:, :, :]), flat(ai[2][:, :, :]), dsum[:, 4:5], flat(ai[1][:, :, :]),
                                   ALU.mult, ALU.add).then_inc(s_sel, 1)
            dve.wait_ge(s_oT_pe, 1)
            V.tensor_copy(xT[:, :, :], whole(pbank[0])).then_inc(s_oT, 1)
            dve.wait_ge(s_o_pe, 1)
            V.tensor_copy(xn[:, :, :], whole(pbank[1])).then_inc(s_o, 1)


def project(nc, a, scr):
    ctx = ExitStack()
    with ctx:
        def sb(name, shape, dt=FP32):
            return ctx.enter_context(nc.sbuf_tensor(name, shape, dt))

        def sem(name):
            return ctx.enter_context(nc.semaphore(name))

        ident = sb("j_ident", [P, P])
        names = ("w0", "wq", "wk", "wv", "wr", "wkk", "wvv")
        w_hi = sb("j_w_hi", [P, len(names), DC, D], FP32R)
        w_lo = sb("j_w_lo", [P, len(names), DC, D], FP32R)
        w = {n: (w_hi[:, i, :, :], w_lo[:, i, :, :]) for i, n in enumerate(names)}
        bias0 = sb("j_bias0", [P, 2, D])
        vbias = sb("j_vbias", [P, D])
        obias = sb("j_obias", [P, D])
        qbias = sb("j_qbias", [P, DC])
        kbias = sb("j_kbias", [P, DC])
        mu = sb("j_mu", [P, 2, DC])
        omu = sb("j_omu", [P, 2, DC])
        neghalf = sb("j_neghalf", [P, TPM])
        x = sb("j_x", [P, 2, TPM, D])
        att = sb("j_att", [E0, D])
        xn = sb("j_xn", [P, TPM, D])
        xT = [sb(f"j_xT{i}", [P, DC, MS], FP32R) for i in range(2)]
        x1 = sb("j_x1", [P, 2, TPM, D])
        x1n = sb("j_x1n", [P, TPM, D])
        x1T = sb("j_x1T", [P, 2, DC, MS + 1])
        stats = sb("j_stats", [P, 2, TPM, 6])
        mv = sb("j_mv", [P, 2, TPM, 2])
        ve = sb("j_ve", [P, 2, TPM])
        hold = sb("j_hold", [P, 1])
        rstd = sb("j_rstd", [P, 2, TPM])
        x1s = [sb(f"j_x1s{i}", [P, DC, MS], FP32R) for i in range(2)]
        mix = sb("j_mix", [P, 2, DC, MS])
        mixs = [sb(f"j_mixs{i}", [P, 2, DC, MS], FP32R) for i in range(2)]
        full = sb("j_full", [P, 2, DC, MS])
        rest = sb("j_rest", [P, 2, DC, MS])
        part = sb("j_part", [P, 3, 3, DC, MS], BF16)
        v = sb("j_v", [P, 2, TPM, NH, VW])
        kact = sb("j_kact", [P, DC, MS])
        kfull = sb("j_kfull", [P, DC, MS])
        ksq = [sb(f"j_ksq{i}", [P, DC, MS], FP32R) for i in range(2)]
        gate = sb("j_gate", [P, TPM, D])
        ffn = sb("j_ffn", [P, TPM, D])
        res = sb("j_res", [P, 2, TPM, D])
        bank = [ctx.enter_context(nc.psum_tensor(f"j_b{i}", [P, 2 * 512], FP32)) for i in range(4)]

        s_w = sem("j_weights")
        s_set = sem("j_set")
        s_x = [sem(f"j_x_in{i}") for i in range(2)]
        s_att = sem("j_att_in")
        s_var0, s_rs0, s_xn = sem("j_var0"), sem("j_rs0"), sem("j_xn_ready")
        s_var1, s_rs1, s_x1n = sem("j_var1"), sem("j_rs1"), sem("j_x1n_ready")
        s_t1, s_xT = sem("j_t1_pe"), sem("j_xT_ready")
        s_f0, s_xb, s_x1 = sem("j_f0_pe"), sem("j_xb_ready"), sem("j_x1_ready")
        s_t2, s_x1T = sem("j_t2_pe"), sem("j_x1T_ready")
        s_xTl, s_x1l = sem("j_xT_lo"), sem("j_x1T_lo")
        s_xmu, s_mix = sem("j_xmu_ready"), [sem("j_mixr_ready"), sem("j_mixk_ready")]
        s_mixh, s_mixl = [sem("j_mixr_hi"), sem("j_mixk_hi")], [sem("j_mixr_lo"), sem("j_mixk_lo")]
        s_ksh, s_ksl = sem("j_ksq_hi"), sem("j_ksq_lo")
        s_wh = sem("j_w_hi_done")
        s_neg = sem("j_neghalf_set")
        s_q, s_full = sem("j_q_pe"), [sem("j_q_full"), sem("j_k_full")]
        s_k = sem("j_k_pe")
        s_hi, s_res1 = [sem("j_q_hi"), sem("j_k_hi")], [sem("j_q_res1"), sem("j_k_res1")]
        s_mid, s_lo = [sem("j_q_mid"), sem("j_k_mid")], [sem("j_q_lo"), sem("j_k_lo")]
        s_v, s_vb = sem("j_v_pe"), sem("j_v_ready")
        s_kk, s_relu, s_ksq = sem("j_kk_pe"), sem("j_relu"), sem("j_ksq")
        s_r, s_tanh = sem("j_r_pe"), sem("j_tanh")
        s_kv, s_ffn, s_xo, s_res = sem("j_kv_pe"), sem("j_ffn_ready"), sem("j_xo_ready"), sem("j_res_ready")
        s_q_out, s_k_out = sem("j_q_stored"), [sem(f"j_k_stored{i}") for i in range(2)]
        s_v_out = [sem(f"j_v_stored{i}") for i in range(2)]
        s_res_out = [sem(f"j_res_stored{i}") for i in range(2)]
        s_link = sem("j_dve_link")
        s_xbias = sem("j_xbias")

        xt = a["x"].rearrange("b (h t p) c -> (b h) p t c", p=P, t=TPM)
        res_d = scr["res"].rearrange("b (h t p) c -> (b h) p t c", p=P, t=TPM)
        v_d = scr["v"].rearrange("b (h t p) c -> (b h) p t c", p=P, t=TPM)
        part_d = [scr[n].rearrange("s b (k p) t -> b s p k t", p=P) for n in ("qs", "ks")]
        att_d = scr["attn0"].rearrange("(b t) n -> b t n", t=E0)
        rows = lambda bk: bk[:, :].rearrange("p (t n) -> p t n", t=TPM)
        chunks = lambda bk: bk[:, :].rearrange("p (k n) -> p k n", k=DC)
        every = lambda t, n=TPM: t.rearrange("p (o n) -> p o n", o=1).to_broadcast([P, n, D])

        block = ctx.enter_context(nc.Block())
        lo = [(ident[:, :], a["ident"])]
        stage = [full[:, i // DC, i % DC, :].rearrange("p (k n) -> p k n", k=DC) for i in range(4)]
        stage += [rest[:, i // DC, i % DC, :].rearrange("p (k n) -> p k n", k=DC) for i in range(3)]
        lo += [(stage[i], src.rearrange("(k p) n -> p k n", p=P)) for i, src in enumerate(
            (scr["w0"], a["q_w"], a["kv_w"][:, 0:D], a["kv_w"][:, D:2 * D], a["WrT"], a["WkkT"], a["WvvT"]))]
        lo += [(bias0[:, 0, :], a["b0"].partition_broadcast(P)), (bias0[:, 1, :], a["bo"].partition_broadcast(P)),
               (vbias[:, :], a["kv_b"][D:2 * D].partition_broadcast(P)),
               (obias[:, :], a["o_b"].partition_broadcast(P)),
               (mu[:, 0, :], a["mu_r_col"]), (mu[:, 1, :], a["mu_k_col"]),
               (qbias[:, :], a["q_b_col"]), (kbias[:, :], a["k_b_col"])]
        n_w = 16 * len(lo)
        N_SET = 8

        @block.sync
        def _(sp):
            sp.dma_start(x[:, 0, :, :], xt[0]).then_inc(s_x[0], 16)
            for dst, src in lo[1::2]:
                sp.dma_start(dst, src).then_inc(s_w, 16)
            sp.dma_start(x[:, 1, :, :], xt[1]).then_inc(s_x[1], 16)
            sp.dma_start(att[:, :], att_d[0]).then_inc(s_att, 16)

            def store_parts(n, slot, b, half, done, s_out):
                sp.wait_ge(s_lo[n], done)
                for s in range(3):
                    sp.dma_start(part_d[n][b, s][:, :, half * MS:(half + 1) * MS], part[:, slot, s, :, :]).then_inc(s_out, 16)

            def store_late(m, b, half):
                store_parts(1, 1 + half, b, half, m + 1, s_k_out[half])
                sp.wait_ge(s_res, m + 1)
                sp.dma_start(res_d[m], res[:, half, :, :]).then_inc(s_res_out[half], 16)

            def step(b, half, first, more):
                m = 2 * b + half
                if half == 0 and more:
                    sp.wait_ge(s_xb, 2 * b + 1)
                    sp.dma_start(att[:, :], att_d[b + 1]).then_inc(s_att, 16)
                if more:
                    sp.wait_ge(s_x1, m + 1)
                    sp.dma_start(x[:, half, :, :], xt[m + 2]).then_inc(s_x[half], 16)
                if not first:
                    store_late(m - 1, b - 1 + half, 1 - half)
                sp.wait_ge(s_vb, m + 1)
                sp.dma_start(v_d[m], v[:, half, :, :, :].rearrange("p t h d -> p t (h d)")).then_inc(s_v_out[half], 16)
                store_parts(0, 0, b, half, m + 1, s_q_out)

            step(0, 0, True, True)
            step(0, 1, False, True)
            with sp.Fori(1, B - 1) as b:
                for half in range(2):
                    step(b, half, False, True)
            for half in range(2):
                step(B - 1, half, False, False)
            store_late(STEPS - 1, B - 1, 1)
            sp.wait_ge(s_q_out, 48 * STEPS)
            for n in range(2):
                sp.wait_ge(s_k_out[n], 48 * B)
                sp.wait_ge(s_v_out[n], 16 * B)
                sp.wait_ge(s_res_out[n], 16 * B)

        @block.tensor
        def _(pe):
            def turn(bk, src):
                for k in range(DC):
                    for t in range(TPM):
                        at = k * MS + t * P
                        mm = pe.transpose(bk[:, at:at + P], src[:, t, k * P:(k + 1) * P], ident[:, :])
                return mm

            TERMS = [(k, x, y) for k in range(DC) for x, y in ((0, 0), (0, 1), (1, 0))]

            def by_token(bk, src, weight):
                for t in range(TPM):
                    for n, (k, x, y) in enumerate(TERMS):
                        mm = pe.matmul(bk[:, t * D:(t + 1) * D], src[x][:, k, t * P:(t + 1) * P], weight[y][:, k, :],
                                       start=(n == 0), stop=(n == len(TERMS) - 1))
                return mm

            def by_dim(bk, src, weight):
                for c in range(DC):
                    for n, (k, y, x) in enumerate(TERMS):
                        mm = pe.matmul(bk[:, c * MS:(c + 1) * MS], weight[y][:, k, c * P:(c + 1) * P], src[x][:, k, :],
                                       start=(n == 0), stop=(n == len(TERMS) - 1))
                return mm

            mixed = [[t[:, i, :, :] for t in mixs] for i in range(2)]

            def step(m, half, first, more):
                own, other = bank[2 + half], bank[3 - half]
                pe.wait_ge(s_x1n, m + 1)
                if not first:
                    pe.wait_ge(s_full[1], m)
                turn(bank[0], x1n).then_inc(s_t2, 1)
                if more:
                    pe.wait_ge(s_xn, m + 2)
                    if not first:
                        pe.wait_ge(s_vb, m)
                    turn(bank[1], xn).then_inc(s_t1, 1)
                if not first:
                    pe.wait_ge(s_ksl, m)
                    by_token(other, ksq, w["wvv"]).then_inc(s_kv, 1)
                pe.wait_ge(s_x1l, m + 1)
                if not first:
                    pe.wait_ge(s_tanh, m)
                by_dim(own, x1s, w["wq"]).then_inc(s_q, 1)
                if more:
                    pe.wait_ge(s_xTl, m + 2)
                    if not first:
                        pe.wait_ge(s_ffn, m)
                    by_token(other, xT, w["w0"]).then_inc(s_f0, 1)
                by_dim(bank[0], x1s, w["wk"]).then_inc(s_k, 1)
                if not more:
                    pe.wait_ge(s_vb, m)
                by_token(bank[1], x1s, w["wv"]).then_inc(s_v, 1)
                pe.wait_ge(s_mixl[1], m + 1)
                pe.wait_ge(s_full[0], m + 1)
                by_dim(own, mixed[1], w["wkk"]).then_inc(s_kk, 1)
                pe.wait_ge(s_mixl[0], m + 1)
                if more:
                    pe.wait_ge(s_x1, m + 2)
                else:
                    pe.wait_ge(s_ffn, m)
                by_token(other, mixed[0], w["wr"]).then_inc(s_r, 1)

            pe.wait_ge(s_w, n_w)
            pe.wait_ge(s_set, N_SET)
            pe.wait_ge(s_xn, 1)
            turn(bank[1], xn).then_inc(s_t1, 1)
            pe.wait_ge(s_xTl, 1)
            by_token(bank[2], xT, w["w0"]).then_inc(s_f0, 1)
            pe.wait_ge(s_x1, 1)
            step(0, 0, True, True)
            step(1, 1, False, True)
            with pe.Fori(1, B - 1) as b:
                for half in range(2):
                    step(2 * b + half, half, False, True)
            step(STEPS - 2, 0, False, True)
            step(STEPS - 1, 1, False, False)
            pe.wait_ge(s_ksl, STEPS)
            by_token(bank[3], ksq, w["wvv"]).then_inc(s_kv, 1)

        @block.scalar
        def _(act):
            def high_part(n, slot):
                nc.scalar.copy(part[:, slot, 0, :, :], full[:, n, :, :]).then_inc(s_hi[n], 1)

            def middle_part(n, slot, m):
                act.wait_ge(s_res1[n], m + 1)
                nc.scalar.copy(part[:, slot, 1, :, :], rest[:, n, :, :]).then_inc(s_mid[n], 1)

            def mix_high(i, m, first):
                act.wait_ge(s_mix[i], m + 1)
                if not first:
                    act.wait_ge(s_kk if i == 1 else s_r, m)
                nc.scalar.copy(mixs[0][:, i, :, :], mix[:, i, :, :]).then_inc(s_mixh[i], 1)

            def step(m, b, half, first, more):
                own, other = bank[2 + half], bank[3 - half]
                act.wait_ge(s_t2, m + 1)
                nc.scalar.copy(x1s[0][:, :, :], chunks(bank[0]))
                nc.scalar.copy(x1T[:, half, :, 1:MS + 1], chunks(bank[0])).then_inc(s_x1T, 1)
                if more:
                    act.wait_ge(s_t1, m + 2)
                    act.wait_ge(s_f0, m + 1)
                    nc.scalar.copy(xT[0][:, :, :], chunks(bank[1])).then_inc(s_xT, 1)
                act.wait_ge(s_x1T, m + 1)
                if half == 1:
                    nc.scalar.copy(x1T[:, 1, :, 0:1], x1T[:, 0, :, MS:MS + 1]).then_inc(s_xmu, 1)
                for i in (1, 0):
                    if not first:
                        act.wait_ge(s_mixl[i], m)
                    for k in range(DC):
                        nc.scalar.activation(mix[:, i, k, :], x1T[:, half, k, 1:MS + 1], ACT.Copy,
                                             scale=mu[:, i, k:k + 1]).then_inc(s_xmu, 1)
                if not first:
                    middle_part(1, 2 - half, m - 1)
                mix_high(1, m, first)
                act.wait_ge(s_q, m + 1)
                if not first:
                    act.wait_ge(s_res1[0], m)
                    act.wait_ge(s_hi[0], m)
                for k in range(DC):
                    i = nc.scalar.activation(full[:, 0, k, :], own[:, k * MS:(k + 1) * MS], ACT.Identity,
                                             bias=qbias[:, k:k + 1], scale=HD ** -0.5)
                i.then_inc(s_full[0], 1)
                mix_high(0, m, first)
                act.wait_ge(s_full[0], m + 1)
                if not first:
                    act.wait_ge(s_q_out, 48 * m)
                high_part(0, 0)
                act.wait_ge(s_k, m + 1)
                if not first:
                    act.wait_ge(s_res1[1], m)
                    act.wait_ge(s_hi[1], m)
                for k in range(DC):
                    i = nc.scalar.activation(full[:, 1, k, :], bank[0][:, k * MS:(k + 1) * MS], ACT.Identity,
                                             bias=kbias[:, k:k + 1])
                i.then_inc(s_full[1], 1)
                middle_part(0, 0, m)
                act.wait_ge(s_full[1], m + 1)
                if not (isinstance(b, int) and b == 0):
                    act.wait_ge(s_k_out[half], 48 * b)
                high_part(1, 1 + half)
                act.wait_ge(s_kk, m + 1)
                if not first:
                    act.wait_ge(s_ksq, m)
                    act.wait_ge(s_kv, m)
                    act.wait_ge(s_ksl, m)
                nc.scalar.activation(kact[:, :, :], chunks(own), ACT.Relu).then_inc(s_relu, 1)
                act.wait_ge(s_relu, m + 1)
                nc.scalar.activation(ksq[0][:, :, :], kact[:, :, :], ACT.Square)
                nc.scalar.activation(kfull[:, :, :], kact[:, :, :], ACT.Square).then_inc(s_ksq, 1)
                act.wait_ge(s_r, m + 1)
                if not first:
                    act.wait_ge(s_ffn, m)
                nc.scalar.activation(gate[:, :, :], rows(other), ACT.Tanh, scale=0.5).then_inc(s_tanh, 1)

            for dst, src in lo[0::2]:
                act.dma_start(dst, src).then_inc(s_w, 16)
            act.wait_ge(s_w, n_w)
            flat4 = lambda t: t.rearrange("p a k n -> p (a k n)")
            nc.scalar.copy(flat4(w_hi[:, 0:4, :, :]), flat4(full[:, :, :, :])).then_inc(s_wh, 1)
            nc.scalar.copy(flat4(w_hi[:, 4:6, :, :]), flat4(rest[:, :, :, :])[:, 0:2 * DC * D]).then_inc(s_wh, 1)
            nc.scalar.activation(w_hi[:, 6, :, :].rearrange("p k n -> p (k n)"),
                                 flat4(rest[:, :, :, :])[:, 2 * DC * D:3 * DC * D], ACT.Copy, scale=0.5).then_inc(s_wh, 1)
            act.wait_ge(s_set, N_SET)
            act.wait_ge(s_t1, 1)
            nc.scalar.copy(xT[0][:, :, :], chunks(bank[1])).then_inc(s_xT, 1)
            step(0, 0, 0, True, True)
            step(1, 0, 1, False, True)
            with act.Fori(1, B - 1) as b:
                for half in range(2):
                    step(2 * b + half, b, half, False, True)
            step(STEPS - 2, B - 1, 0, False, True)
            step(STEPS - 1, B - 1, 1, False, False)
            middle_part(1, 2, STEPS - 1)

        @block.vector
        def _(dve):
            V = nc.vector
            STEP_LINKS, PRO_LINKS = 4, 6

            def norm_stats(z, src, link, s_var):
                for t in range(TPM):
                    i = V.bn_stats(stats[:, z, t, :], src[:, t, :])
                link(i)
                V.memset(hold[:, :], 0.0)
                for t in range(TPM):
                    i = V.bn_aggr(mv[:, z, t, :], stats[:, z, t, :])
                link(i)
                V.tensor_scalar(ve[:, z, :], mv[:, z, :, 1], EPS, None, ALU.add).then_inc(s_var, 1)

            def normalise(z, src, dst, s_done):
                for t in range(TPM):
                    i = V.tensor_scalar(dst[:, t, :], src[:, t, :], mv[:, z, t, 0:1], rstd[:, z, t:t + 1],
                                        ALU.subtract, ALU.mult)
                i.then_inc(s_done, 1)

            def layer0(m, half, link, first=False, meanwhile=None):
                dve.wait_ge(s_f0, m + 1)
                dve.wait_ge(s_xb, m + 1)
                if not first:
                    dve.wait_ge(s_xo, m - 1)
                V.tensor_tensor(x1[:, half, :, :], rows(bank[2 + half]), x[:, half, :, :], ALU.add).then_inc(s_x1, 1)
                dve.wait_ge(s_x1, m + 1)
                norm_stats(1, x1[:, half, :, :], link, s_var1)
                if meanwhile:
                    meanwhile()
                dve.wait_ge(s_rs1, m + 1)
                if not first:
                    dve.wait_ge(s_t2, m)
                normalise(1, x1[:, half, :, :], x1n, s_x1n)

            def norm0(m, half, count, link, first=False, meanwhile=None):
                dve.wait_ge(s_x[half], 16 * count)
                norm_stats(0, x[:, half, :, :], link, s_var0)
                if meanwhile:
                    meanwhile()
                dve.wait_ge(s_rs0, m + 1)
                if not first:
                    dve.wait_ge(s_t1, m)
                normalise(0, x[:, half, :, :], xn, s_xn)

            def low(dst, src, high, s_done):
                V.tensor_tensor(dst, src, high.bitcast(FP32), ALU.subtract).then_inc(s_done, 1)

            def gated(m, half, first):
                dve.wait_ge(s_tanh, m + 1)
                dve.wait_ge(s_kv, m + 1)
                if not first:
                    dve.wait_ge(s_res, m)
                V.scalar_tensor_tensor(ffn[:, :, :], gate[:, :, :], 1.0, rows(bank[2 + half]),
                                       ALU.add, ALU.mult).then_inc(s_ffn, 1)

            def step(m, b, half, base, more, norm):
                static = isinstance(m, int)
                first = static and m == 0
                link = Chain(dve, s_link, base)

                def mix_low(i):
                    dve.wait_ge(s_mixh[i], m + 1)
                    low(mixs[1][:, i, :, :], mix[:, i, :, :], mixs[0][:, i, :, :], s_mixl[i])

                def add_v_bias():
                    dve.wait_ge(s_v, m + 1)
                    if not (isinstance(b, int) and b == 0):
                        dve.wait_ge(s_v_out[half], 16 * b)
                    for t in range(TPM):
                        i = V.tensor_tensor(v[:, half, t, :, 0:HD],
                                            bank[1][:, t * D:(t + 1) * D].rearrange("p (h d) -> p h d", d=HD),
                                            vbias[:, :].rearrange("p (h d) -> p h d", d=HD), ALU.add)
                    i.then_inc(s_vb, 1)

                dve.wait_ge(s_x1T, m + 1)
                low(x1s[1][:, :, :], chunks(bank[0]), x1s[0][:, :, :], s_x1l)
                if more:
                    dve.wait_ge(s_xT, m + 2)
                    low(xT[1][:, :, :], chunks(bank[1]), xT[0][:, :, :], s_xTl)
                if not first:
                    gated(m - 1, 1 - half, static and m == 1)
                for i in (1, 0):
                    dve.wait_ge(s_xmu, 4 * m + (b + half) + (4 if i == 0 else 2))
                    for k in range(DC):
                        j = V.scalar_tensor_tensor(mix[:, i, k, :], x1T[:, half, k, 0:MS], omu[:, i, k:k + 1],
                                                   mix[:, i, k, :], ALU.mult, ALU.add)
                    j.then_inc(s_mix[i], 1)
                mix_low(1)
                if more:
                    layer0(m + 1, 1 - half, link, meanwhile=lambda: mix_low(0))
                else:
                    mix_low(0)
                if norm:
                    norm0(m + 2, half, b + 2, link, meanwhile=add_v_bias)
                else:
                    add_v_bias()
                dve.wait_ge(s_ksq, m + 1)
                if not first:
                    dve.wait_ge(s_kv, m)
                low(ksq[1][:, :, :], kfull[:, :, :], ksq[0][:, :, :], s_ksl)

            pro = Chain(dve, s_link)
            norm0(0, 0, 1, pro, True)
            dve.wait_ge(s_w, n_w)
            dve.wait_ge(s_wh, 3)
            flat4 = lambda t: t.rearrange("p a k n -> p (a k n)")
            V.tensor_tensor(flat4(w_lo[:, 0:4, :, :]), flat4(full[:, :, :, :]),
                            flat4(w_hi[:, 0:4, :, :]).bitcast(FP32), ALU.subtract).then_inc(s_set, 1)
            V.tensor_tensor(flat4(w_lo[:, 4:6, :, :]), flat4(rest[:, :, :, :])[:, 0:2 * DC * D],
                            flat4(w_hi[:, 4:6, :, :]).bitcast(FP32), ALU.subtract).then_inc(s_set, 1)
            V.scalar_tensor_tensor(w_lo[:, 6, :, :].rearrange("p k n -> p (k n)"),
                                   flat4(rest[:, :, :, :])[:, 2 * DC * D:3 * DC * D], 0.5,
                                   w_hi[:, 6, :, :].rearrange("p k n -> p (k n)").bitcast(FP32),
                                   ALU.mult, ALU.subtract).then_inc(s_set, 1)
            V.tensor_scalar(qbias[:, :], qbias[:, :], HD ** -0.5, None, ALU.mult).then_inc(s_set, 1)
            V.tensor_scalar(omu[:, :, :], mu[:, :, :], -1.0, 1.0, ALU.mult, ALU.add).then_inc(s_set, 1)
            V.tensor_tensor(bias0[:, 0, :], bias0[:, 0, :], bias0[:, 1, :], ALU.add).then_inc(s_set, 1)
            dve.wait_ge(s_set, N_SET)
            dve.wait_ge(s_xT, 1)
            V.tensor_tensor(xT[1][:, :, :], chunks(bank[1]), xT[0][:, :, :].bitcast(FP32),
                            ALU.subtract).then_inc(s_xTl, 1)
            norm0(1, 1, 1, pro)
            layer0(0, 0, pro, True)
            assert pro.n == PRO_LINKS
            step(0, 0, 0, PRO_LINKS, True, True)
            step(1, 0, 1, PRO_LINKS + STEP_LINKS, True, True)
            with dve.Fori(1, B - 1) as b:
                for half in range(2):
                    step(2 * b + half, b, half, PRO_LINKS + STEP_LINKS * (2 * b + half), True, True)
            step(STEPS - 2, B - 1, 0, PRO_LINKS + STEP_LINKS * (STEPS - 2), True, False)
            step(STEPS - 1, B - 1, 1, PRO_LINKS + STEP_LINKS * (STEPS - 2) + 2, False, False)
            gated(STEPS - 1, 1, False)

        @block.gpsimd
        def _(pool):
            pool.memset(neghalf[:, :], -0.5).then_inc(s_neg, 1)
            pool.memset(v[:, :, :, :, HD:VW], 1.0).then_inc(s_set, 1)
            pool.memset(x1T[:, 0, :, 0:1], 0.0).then_inc(s_set, 1)

            def rs0(m):
                pool.wait_ge(s_var0, m + 1)
                pool.tensor_tensor(rstd[:, 0, :], ve[:, 0, :], neghalf[:, :], ALU.pow).then_inc(s_rs0, 1)

            def rs1(m):
                pool.wait_ge(s_var1, m + 1)
                pool.tensor_tensor(rstd[:, 1, :], ve[:, 1, :], neghalf[:, :], ALU.pow).then_inc(s_rs1, 1)

            def with_bias(m, b, half):
                pool.wait_ge(s_xn, m + 1)
                if half == 0:
                    pool.tensor_tensor(x[:, half, :, :], x[:, half, :, :], every(bias0[:, 0, :]), ALU.add).then_inc(s_xbias, 1)
                    pool.wait_ge(s_xbias, b + 1)
                    pool.wait_ge(s_att, 16 * (b + 1))
                    pool.tensor_tensor(x[0:E0, half, 0, :], x[0:E0, half, 0, :], att[:, :], ALU.add).then_inc(s_xb, 1)
                else:
                    pool.tensor_tensor(x[:, half, :, :], x[:, half, :, :], every(bias0[:, 0, :]), ALU.add).then_inc(s_xb, 1)

            def remainder(n, slot, m):
                pool.wait_ge(s_hi[n], m + 1)
                pool.tensor_tensor(rest[:, n, :, :], full[:, n, :, :], part[:, slot, 0, :, :],
                                   ALU.subtract).then_inc(s_res1[n], 1)

            def low_part(n, slot, m):
                pool.wait_ge(s_mid[n], m + 1)
                pool.tensor_tensor(part[:, slot, 2, :, :], rest[:, n, :, :], part[:, slot, 1, :, :],
                                   ALU.subtract).then_inc(s_lo[n], 1)

            def add_ffn(m, half):
                pool.wait_ge(s_xo, m + 1)
                pool.wait_ge(s_ffn, m + 1)
                pool.tensor_tensor(res[:, half, :, :], res[:, half, :, :], ffn[:, :, :], ALU.add).then_inc(s_res, 1)

            def step(m, b, half, first, more, norm):
                remainder(0, 0, m)
                if more:
                    rs1(m + 1)
                if not first:
                    low_part(1, 2 - half, m - 1)
                if not first:
                    add_ffn(m - 1, 1 - half)
                if norm:
                    rs0(m + 2)
                low_part(0, 0, m)
                if not first:
                    pool.wait_ge(s_lo[1], m)
                remainder(1, 1 + half, m)
                if not (isinstance(b, int) and b == 0):
                    pool.wait_ge(s_res_out[half], 16 * b)
                pool.tensor_tensor(res[:, half, :, :], x1[:, half, :, :], every(obias[:, :]), ALU.add).then_inc(s_xo, 1)
                if norm:
                    with_bias(m + 2, b + 1, half)

            pool.wait_ge(s_neg, 1)
            rs0(0)
            pool.wait_ge(s_set, N_SET)
            with_bias(0, 0, 0)
            rs0(1)
            with_bias(1, 0, 1)
            rs1(0)
            step(0, 0, 0, True, True, True)
            step(1, 0, 1, False, True, True)
            with pool.Fori(1, B - 1) as b:
                for half in range(2):
                    step(2 * b + half, b, half, False, True, True)
            step(STEPS - 2, B - 1, 0, False, True, False)
            step(STEPS - 1, B - 1, 1, False, False, False)
            low_part(1, 2, STEPS - 1)
            add_ffn(STEPS - 1, 1)


def quads():
    half = T // 2
    key_side = [(j, 0, P * j, half - P * j) for j in range(QT // 2)]
    key_side += [(j, 1, max(half, P * j), T - max(half, P * j)) for j in range(QT)]
    query_side = [(i, 0, P * (i + 1)) for i in reversed(range(QT // 2))]
    query_side += [(i, 0, half) for i in range(QT // 2, QT)]
    query_side += [(i, half, P * (i + 1) - half) for i in reversed(range(QT // 2, QT))]
    assert [q[3] for q in key_side] == [q[2] for q in query_side]
    return key_side, query_side


KEY_QUADS, QUERY_QUADS = quads()
NQ = len(KEY_QUADS)


def per_bank(n):
    return 512 // n if n in (128, 256) else 1


def body_units(kind):
    at = {}
    for g in range(NG):
        for r in range(NQ):
            todo = []
            ahead, q = divmod(r + LEAD, NQ)
            to = g + 1 + ahead
            if not (kind == "last" and to >= NG):
                for h in range(0, GH, per_bank(QUERY_QUADS[q][2])):
                    todo.append(("max", to, (q, h)))
            if r == 2 and not (kind == "first" and g == 0):
                todo.append(("norm", g - 1, 1))
            if r == 6:
                todo.append(("norm", g, 0))
            if r == 8 and not (kind == "last" and g == NG - 1):
                todo.append(("rows", g + 1, None))
            if g == 0 and kind != "first":
                if r in (4, 5):
                    todo += [("turn", -1, 2 * (r - 4) + u) for u in range(2)]
                if r in (7, 8):
                    todo += [("out", -1, 2 * (r - 7) + u) for u in range(2)]
            at[g, r] = todo
    return at


def attend(nc, a, scr, out):
    ctx = ExitStack()
    with ctx:
        def sb(name, shape, dt=FP32):
            return ctx.enter_context(nc.sbuf_tensor(name, shape, dt))

        def sem(name):
            return ctx.enter_context(nc.semaphore(name))

        ident = sb("t_ident", [P, P])
        identb = sb("t_identb", [P, P], BF16)
        amask = sb("t_amask", [P, P], BF16)
        bmask = sb("t_bmask", [P, P], BF16)
        ow = sb("t_ow", [P, DC, D])
        q_op = [sb(f"t_q{g}", [P, GH, T], BF16) for g in range(NG)]
        k_op = [sb(f"t_k{g}", [P, GH, T], BF16) for g in range(NG)]
        v = [sb(f"t_v{g}", [P, QT, VPAD], FP32) for g in range(NG)]
        prob = sb("t_prob", [P, 2, GH, 512])
        mx = sb("t_mx", [P, 2, GH, QT])
        mx2 = sb("t_mx2", [P, 2, 2, GH, QT // 2])
        mrest = sb("t_mrest", [P, GH * QT])
        mpart = sb("t_mpart", [P, 3, GH * QT], BF16)
        mrows = sb("t_mrows", [3 * GH * QT, P], BF16)
        yu = sb("t_yu", [P, 2, 512])
        rec = sb("t_rec", [P, 2, GH, GH])
        y = sb("t_y", [P, QT, D])
        yT = sb("t_yT", [P, DC, T])
        res = sb("t_res", [P, QT, D])
        o = sb("t_o", [P, QT, D])
        abank = [ctx.enter_context(nc.psum_tensor(f"t_a{i}", [P, 512], FP32)) for i in range(3)]
        abf = [t[:, :].bitcast(BF16) for t in abank]
        bbank = [ctx.enter_context(nc.psum_tensor(f"t_b{i}", [P, 512], FP32)) for i in range(3)]
        ybank = [ctx.enter_context(nc.psum_tensor(f"t_y{i}", [P, 512], FP32)) for i in range(2)]

        s_c0 = sem("t_const_in")
        s_c = [sem(f"t_const_in{g}") for g in range(NG)]
        s_set = sem("t_set")
        s_qk = [sem(f"t_qk_in{g}") for g in range(NG)]
        s_vin = [sem(f"t_v_in{g}") for g in range(NG)]
        s_a = sem("t_a_pe")
        s_au = sem("t_a_used")
        s_b = sem("t_b_pe")
        s_e = sem("t_exp")
        s_pv = sem("t_pv_pe")
        s_yu = sem("t_yu_copied")
        s_mp = sem("t_mpart_ready")
        s_mw = sem("t_mrows_written")
        s_m = [sem(f"t_m_in{g}") for g in range(NG)]
        s_res = sem("t_res_in")
        s_out = sem("t_out_stored")
        s_link = sem("t_dve_link")

        kinds = {k: body_units(k) for k in ("first", "mid", "last")}
        count = {k: sum(map(len, at.values())) for k, at in kinds.items()}
        PRO = [("max", 0, (q, h)) for q in range(NQ) for h in range(0, GH, per_bank(QUERY_QUADS[q][2]))]
        PRO += [("rows", 0, None)]
        PRO += [("max", 1, (q, h)) for q in range(LEAD) for h in range(0, GH, per_bank(QUERY_QUADS[q][2]))]
        TAIL = [("norm", -1, 1)] + [("turn", -1, u) for u in range(4)] + [("out", -1, u) for u in range(4)]
        B_UNITS = NG * sum(GH // per_bank(q[3]) for q in KEY_QUADS)

        def base(kind, b):
            if kind == "first":
                return len(PRO)
            return len(PRO) + count["first"] + count["mid"] * (b - 1)

        TAIL_BASE = len(PRO) + count["first"] + count["mid"] * (B - 2) + count["last"]
        LOADS = 2 * NSLOT

        qs = scr["qs"].rearrange("s b (h d) t -> s b d h t", d=HD)
        ks = scr["ks"].rearrange("s b (h d) t -> s b d h t", d=HD)
        vs = scr["v"].rearrange("b (j p) (g c) -> b g p j c", p=P, g=NG)
        resd = scr["res"].rearrange("b (t p) c -> b p t c", p=P)
        outd = out.rearrange("b (t p) c -> b p t c", p=P)

        def load_q(eng, b, g):
            for s in range(NSLOT):
                at = NPOS + s * HD
                eng.dma_start(q_op[g][at:at + HD, :, :],
                              qs[Q_PART[s], b][:, g * GH:(g + 1) * GH, :]).then_inc(s_qk[g], 16)

        def load_k(eng, b, g):
            for s in range(NSLOT):
                at = NPOS + s * HD
                eng.dma_start(k_op[g][at:at + HD, :, :],
                              ks[K_PART[s], b][:, g * GH:(g + 1) * GH, :]).then_inc(s_qk[g], 16)

        block = ctx.enter_context(nc.Block())

        @block.sync
        def _(sp):
            def load(b, g):
                load_q(sp, b, g)
                load_k(sp, b, g)
                load_v(b, g)

            def load_v(b, g):
                sp.dma_start(v[g][:, :, 0:GH * VW], vs[b, g]).then_inc(s_vin[g], 16)

            def rows(b, g):
                t = NG * b + g
                if isinstance(b, int) and b == 0 and g == 0:
                    sp.wait_ge(s_au, PRO.index(("rows", 0, None)) + 1)
                sp.dma_start(scr["m"][g], mrows[:, :]).then_inc(s_mw, 16)
                sp.wait_ge(s_mw, 16 * (t + 1))
                sp.dma_start(q_op[g][KA:KB, :, :].rearrange("p h t -> p (h t)"),
                             scr["m"][g].rearrange("(s n) q -> s (n q)", s=3)).then_inc(s_m[g], 16)

            def body(kind, b):
                seen = base(kind, b)
                for g in range(NG):
                    for r in range(NQ):
                        for what, to, detail in kinds[kind][g, r]:
                            seen = seen + 1
                            if what == "rows":
                                sp.wait_ge(s_au, seen)
                                rows(b + to // NG, to % NG)
                        if r == 1 and not (kind == "first" and g == 0):
                            done = NG * NQ * b + NQ * g
                            if g > 0 and kind != "last":
                                sp.wait_ge(s_pv, done)
                                load(b + 1, g - 1)
                            if g == 0:
                                sp.wait_ge(s_pv, done)
                                load(b, NG - 1)

            for g in range(NG):
                sp.dma_start(q_op[g][0:NPOS, :, :], a["q_pos"][:, g * GH:(g + 1) * GH, :]).then_inc(s_c[g], 16)
                load_q(sp, 0, g)
                if g == 0:
                    sp.dma_start(identb[:, :], a["identb"]).then_inc(s_c0, 16)
            for g in range(NG):
                load_v(0, g)
            rows(0, 0)
            body("first", 0)
            with sp.Fori(1, B - 1) as b:
                body("mid", b)
            body("last", B - 1)

        @block.tensor
        def _(pe):
            def a_unit(what, to, detail, n, seen, b, seen_norm):
                bk = abank[n]
                if what == "max":
                    g = to % NG
                    q, h0 = detail
                    i, k0, w = QUERY_QUADS[q]
                    for s in range(per_bank(w)):
                        h = h0 + s
                        piece = bk[:, s * w:(s + 1) * w]
                        diagonal = k0 + w == (i + 1) * P
                        mm = pe.matmul(piece, q_op[g][0:KA, h, i * P:(i + 1) * P], k_op[g][0:KA, h, k0:k0 + w],
                                       start=True, stop=not diagonal)
                        if diagonal:
                            mm = pe.matmul(piece[:, w - P:w], identb[:, :], amask[:, :], start=False, stop=True)
                elif what == "rows":
                    pe.wait_ge(s_mp, NG * b + to + 1)
                    mm = pe.transpose(abf[n][0:3 * GH * QT, 0:P], mpart[:, :, :].rearrange("p s n -> p (s n)"), identb[:, :])
                elif what == "norm":
                    pe.wait_ge(s_yu, 2 * (NG * b + to) + detail + 1)
                    for t in range(4):
                        mm = pe.transpose(bk[:, t * P:(t + 1) * P], yu[:, detail, t * P:(t + 1) * P], ident[:, :])
                elif what == "turn":
                    pe.wait_ge(s_au, seen_norm)
                    k, half = divmod(detail, 2)
                    for t in range(4):
                        mm = pe.transpose(bk[:, t * P:(t + 1) * P], y[:, half * 4 + t, k * P:(k + 1) * P], ident[:, :])
                else:
                    pe.wait_ge(s_au, seen_norm)
                    for s in range(2):
                        t = 2 * detail + s
                        for k in range(DC):
                            mm = pe.matmul(bk[:, s * D:(s + 1) * D], yT[:, k, t * P:(t + 1) * P], ow[:, k, :],
                                           start=(k == 0), stop=(k == DC - 1))
                mm.then_inc(s_a, 1)

            def run(units, start, n0, b, last_of):
                for n, (what, to, detail) in enumerate(units, n0):
                    pe.wait_ge(s_au, start + max(n - 2, 0))
                    if what == "max" and detail == (0, 0):
                        if isinstance(b, int) and b == 0 and to < NG:
                            pe.wait_ge(s_c[to], 16 * 3)
                        pe.wait_ge(s_qk[to % NG], 16 * LOADS * (b + to // NG + 1))
                    if what == "norm":
                        last_of["norm"] = start + n + 1
                    if what == "turn":
                        last_of["turn"] = start + n + 1
                    a_unit(what, to, detail, n % 3, start + n, b,
                           last_of.get("norm" if what == "turn" else "turn"))

            def body(kind, b):
                at, start, n0, u0, last_of = kinds[kind], base(kind, b), 0, 0, {}
                for g in range(NG):
                    t = NG * b + g
                    for r in range(NQ):
                        j, c, q0, w = KEY_QUADS[r]
                        todo = list(at[g, r])
                        maxes = [u for u in todo if u[0] == "max"]
                        if r == 0:
                            pe.wait_ge(s_m[g], 16 * (b + 1))
                            pe.wait_ge(s_vin[g], 16 * (b + 1))
                        pieces = list(range(0, GH, per_bank(w)))
                        for x, h0 in enumerate(pieces):
                            if maxes:
                                run([maxes.pop(0)], start, n0, b, last_of)
                                n0 += 1
                            pe.wait_ge(s_e, B_UNITS * b + max(u0 - 2, 0))
                            for s in range(per_bank(w)):
                                h = h0 + s
                                piece = bbank[u0 % 3][:, s * w:(s + 1) * w]
                                diagonal = q0 == j * P
                                mm = pe.matmul(piece, k_op[g][0:KB, h, j * P:(j + 1) * P], q_op[g][0:KB, h, q0:q0 + w],
                                               start=True, stop=not diagonal)
                                if diagonal:
                                    mm = pe.matmul(piece[:, 0:P], identb[:, :], bmask[:, :], start=False, stop=True)
                            mm.then_inc(s_b, 1)
                            u0 += 1
                            if x == min(2, len(pieces) - 1):
                                weigh(kind, b, g, r - 1, u0 - x - 1)
                        rest = maxes + [u for u in todo if u[0] != "max"]
                        run(rest, start, n0, b, last_of)
                        n0 += len(rest)
                if kind == "last":
                    weigh(kind, b, NG, -1, u0)
                assert n0 == count[kind] and u0 == B_UNITS

            def weigh(kind, b, g, r, units):
                if r < 0:
                    if kind == "first" and g == 0:
                        return
                    r, g = NQ - 1, g - 1
                j, c, q0, w = KEY_QUADS[r]
                pe.wait_ge(s_e, B_UNITS * b + units)
                if j == 0 and not (kind == "first" and g == 0):
                    pe.wait_ge(s_yu, 2 * (NG * b + g - 1) + c + 1)
                for h in range(GH):
                    mm = pe.matmul(ybank[c][32 * h:32 * h + 32, q0 - 512 * c:q0 - 512 * c + w],
                                   v[g % NG][:, j, h * VW:h * VW + 32], prob[:, r % 2, h, 0:w],
                                   start=(j == 0), stop=(j == (QT // 2 if c == 0 else QT) - 1))
                mm.then_inc(s_pv, 1)

            pe.wait_ge(s_c0, 16 * 5)
            pe.wait_ge(s_set, 1)
            run(PRO, 0, 0, 0, {})
            body("first", 0)
            with pe.Fori(1, B - 1) as b:
                body("mid", b)
            body("last", B - 1)
            run(TAIL, TAIL_BASE, 0, B, {})

        @block.scalar
        def _(act):
            LAST_OUT = {k: 1 + max(n for n, u in enumerate(u for g in range(NG) for r in range(NQ) for u in at[g, r])
                                   if u[0] == "out") for k, at in kinds.items() if k != "first"}

            def copy_y(b, g, c):
                t = NG * b + g
                act.wait_ge(s_pv, NQ * t + (4 if c == 0 else NQ))
                nc.scalar.copy(yu[:, c, :], ybank[c][:, :]).then_inc(s_yu, 1)

            def body(kind, b):
                seen, u0 = base(kind, b), 0
                used = {} if kind == "first" else {0: seen, 1: seen}
                for g in range(NG):
                    if g == 0 and kind != "first":
                        act.wait_ge(s_au, base(kind, b))
                        act.dma_start(res[:, :, :], resd[b - 1]).then_inc(s_res, 16)
                    if g == 1 and kind != "first":
                        act.wait_ge(s_au, base(kind, b) + LAST_OUT[kind])
                        act.dma_start(outd[b - 1], o[:, :, :]).then_inc(s_out, 16)
                    for r in range(NQ):
                        j, c, q0, w = KEY_QUADS[r]
                        if not (kind == "first" and g == 0 and r < 2):
                            act.wait_ge(s_pv, NG * NQ * b + NQ * g + r - 1)
                        for h0 in range(0, GH, per_bank(w)):
                            act.wait_ge(s_b, B_UNITS * b + u0 + 1)
                            m = per_bank(w)
                            nc.scalar.activation(prob[:, r % 2, h0:h0 + m, 0:w],
                                                 bbank[u0 % 3][:, 0:m * w].rearrange("p (h n) -> p h n", h=m),
                                                 ACT.Exp).then_inc(s_e, 1)
                            u0 += 1
                        for what, to, detail in kinds[kind][g, r]:
                            seen = seen + 1
                            if what == "norm":
                                used[detail] = seen
                        if r == 0 and not (kind == "first" and g == 0):
                            if used.get(1) is not None:
                                act.wait_ge(s_au, used[1])
                            copy_y(b, g - 1, 1)
                        if r == 4:
                            if used.get(0) is not None:
                                act.wait_ge(s_au, used[0])
                            copy_y(b, g, 0)

            for g in range(NG):
                act.dma_start(k_op[g][0:NPOS, :, :], a["k_pos"]).then_inc(s_c[g], 16)
                load_k(act, 0, g)
                if g == 0:
                    act.dma_start(amask[:, :], a["amask"]).then_inc(s_c0, 16)
                    act.dma_start(bmask[:, :], a["bmask"]).then_inc(s_c0, 16)
                    act.dma_start(ident[:, :], a["ident"]).then_inc(s_c0, 16)
                    act.dma_start(ow[:, :, :], a["o_w"].rearrange("(k p) n -> p k n", p=P)).then_inc(s_c0, 16)
                act.dma_start(k_op[g][KA:KB, :, :], a["k_one"]).then_inc(s_c[g], 16)
            act.wait_ge(s_set, 1)
            body("first", 0)
            with act.Fori(1, B - 1) as b:
                body("mid", b)
            body("last", B - 1)
            act.wait_ge(s_au, TAIL_BASE)
            act.dma_start(res[:, :, :], resd[B - 1]).then_inc(s_res, 16)
            copy_y(B - 1, NG - 1, 1)
            act.wait_ge(s_au, TAIL_BASE + len(TAIL))
            act.dma_start(outd[B - 1], o[:, :, :]).then_inc(s_out, 16)
            act.wait_ge(s_out, 16 * B)

        @block.vector
        def _(dve):
            V = nc.vector

            def unit(what, to, detail, n, seen, b, link):
                bk = abank[n]
                dve.wait_ge(s_a, seen + 1)
                if what == "max":
                    z = to % 2
                    q, h0 = detail
                    i, k0, w = QUERY_QUADS[q]
                    m = per_bank(w)
                    dst = mx[:, z, h0:h0 + m, i] if i < QT // 2 else mx2[:, z, k0 // 512, h0:h0 + m, i - QT // 2]
                    V.tensor_reduce(dst, bk[:, 0:m * w].rearrange("p (h n) -> p h n", h=m), AX.X,
                                    ALU.max).then_inc(s_au, 1)
                    if q == NQ - 1 and h0 + m == GH:
                        parts(to, seen + 1, link, b)
                elif what == "rows":
                    if not (isinstance(b, int) and b == 0 and to == 0):
                        dve.wait_ge(s_mw, 16 * (NG * b + to))
                    V.tensor_copy(mrows[:, :], abf[n][0:3 * GH * QT, 0:P]).then_inc(s_au, 1)
                elif what == "norm":
                    piece = bk[:, :].rearrange("p (t h n) -> p t h n", t=4, h=GH)
                    link(V.reciprocal(rec[:, detail, :, :], piece[:, :, :, HD]))
                    g = to % NG
                    for t in range(4):
                        i = V.tensor_tensor(
                            y[:, 4 * detail + t, g * GH * HD:(g + 1) * GH * HD].rearrange("p (h d) -> p h d", d=HD),
                            piece[:, t, :, 0:HD],
                            rec[:, detail, t, :].rearrange("p (h o) -> p h o", o=1).to_broadcast([P, GH, HD]), ALU.mult)
                    i.then_inc(s_au, 1)
                elif what == "turn":
                    k, half = divmod(detail, 2)
                    V.tensor_copy(yT[:, k, half * 512:(half + 1) * 512], bk[:, :]).then_inc(s_au, 1)
                else:
                    if detail == 0:
                        dve.wait_ge(s_res, 16 * b)
                        if not (isinstance(b, int) and b == 1):
                            dve.wait_ge(s_out, 16 * (b - 1))
                    V.tensor_tensor(o[:, 2 * detail:2 * detail + 2, :], bk[:, :].rearrange("p (t n) -> p t n", t=2),
                                    res[:, 2 * detail:2 * detail + 2, :], ALU.add).then_inc(s_au, 1)

            def parts(to, seen, link, b):
                z = to % 2
                dve.wait_ge(s_au, seen)
                link(V.tensor_tensor(mx[:, z, :, QT // 2:QT], mx2[:, z, 0, :, :], mx2[:, z, 1, :, :], ALU.max))
                flat = mx[:, z, :, :].rearrange("p h i -> p (h i)")
                link(V.tensor_scalar(mpart[:, 0, :], flat, -1.0, None, ALU.mult))
                link(V.scalar_tensor_tensor(mrest[:, :], flat, -1.0, mpart[:, 0, :], ALU.mult, ALU.subtract))
                link(V.tensor_copy(mpart[:, 1, :], mrest[:, :]))
                V.tensor_tensor(mpart[:, 2, :], mrest[:, :], mpart[:, 1, :], ALU.subtract).then_inc(s_mp, 1)

            def links_of(units):
                return sum(4 if (w == "max" and d[0] == NQ - 1 and d[1] + per_bank(QUERY_QUADS[d[0]][2]) == GH)
                           else 1 if w == "norm" else 0 for w, _, d in units)

            in_body = {k: [u for g in range(NG) for r in range(NQ) for u in at[g, r]] for k, at in kinds.items()}
            n_links = {k: links_of(u) for k, u in in_body.items()}

            def body(kind, b):
                start = base(kind, b)
                lb = links_of(PRO) if kind == "first" else links_of(PRO) + n_links["first"] + n_links["mid"] * (b - 1)
                link = Chain(dve, s_link, lb)
                for n, (what, to, detail) in enumerate(in_body[kind]):
                    unit(what, to, detail, n % 3, start + n, b, link)
                assert link.n == n_links[kind]

            for g in range(NG):
                i = V.memset(v[g][:, :, GH * VW:VPAD], 0.0)
            i.then_inc(s_set, 1)
            dve.wait_ge(s_set, 1)
            pro = Chain(dve, s_link)
            for n, (what, to, detail) in enumerate(PRO):
                unit(what, to, detail, n % 3, n, 0, pro)
            body("first", 0)
            with dve.Fori(1, B - 1) as b:
                body("mid", b)
            body("last", B - 1)
            link = Chain(dve, s_link, links_of(PRO) + n_links["first"] + n_links["mid"] * (B - 2) + n_links["last"])
            for n, (what, to, detail) in enumerate(TAIL):
                unit(what, to, detail, n % 3, TAIL_BASE + n, B, link)


def kernel(**inputs):
    import numpy as np
    import concourse.bacc as bacc
    from concourse.bass_utils import run_bass_kernel_spmd as run

    nc = bacc.Bacc("TRN2", target_bir_lowering=False, num_devices=1)
    arrays, a = {}, {}

    def give(name, array):
        array = np.ascontiguousarray(array)
        arrays[f"in_{name}"] = array
        a[name] = nc.dram_tensor(f"in_{name}", array.shape, mybir.dt.from_np(array.dtype), kind="ExternalInput").ap()

    turned = {"WqT": "L0_attn_Wq", "WkT": "L0_attn_Wk", "WvT": "L0_attn_Wv", "WoT": "L0_attn_Wo",
              "WlqT": "L0_attn_Wlq", "WlkT": "L0_attn_Wlk", "WlvT": "L0_attn_Wlv", "W0T": "L0_ffn_W",
              "ldT": "L0_ffn_lora_down", "luT": "L0_ffn_lora_up", "uaT": "L0_ffn_up_aux",
              "WrT": "L1_ffn_W_r", "WkkT": "L1_ffn_W_k", "WvvT": "L1_ffn_W_v"}
    plain = {"x": "L0_attn_x", "bq": "L0_attn_bq", "bv": "L0_attn_bv", "bo": "L0_attn_bo",
             "lna_w": "L0_attn_lna_w", "lnc_w": "L0_attn_lnc_w", "lnd_w": "L0_attn_lnd_w",
             "blq": "L0_attn_blq", "blk": "L0_attn_blk", "blv": "L0_attn_blv",
             "down_aux": "L0_ffn_down_aux", "b0": "L0_ffn_b", "q_w": "L1_attn_q_w",
             "kv_w": "L1_attn_kv_w", "kv_b": "L1_attn_kv_b", "o_w": "L1_attn_o_w", "o_b": "L1_attn_o_b"}
    for name, of in turned.items():
        give(name, np.asarray(inputs[of]).T)
    for name, of in plain.items():
        give(name, inputs[of])
    for name in ("temp", "threshold", "factor"):
        give(name, np.asarray(inputs["L0_attn_" + name]).reshape(1))

    for name, vec in (("mu_r_col", inputs["L1_ffn_mu_r"]), ("mu_k_col", inputs["L1_ffn_mu_k"]),
                      ("q_b_col", inputs["L1_attn_q_b"]), ("k_b_col", np.asarray(inputs["L1_attn_kv_b"])[0:D])):
        give(name, np.asarray(vec).reshape(DC, P).T)

    bf16 = np.dtype("bfloat16")
    p = np.arange(P)
    t = np.arange(T)
    head = np.arange(1, NH + 1)
    later = np.where(p[None, :] > p[:, None], BIG, 0.0)
    give("ident", np.eye(P, dtype=np.float32))
    give("identb", np.eye(P).astype(bf16))
    give("amask", later.astype(bf16))
    give("bmask", later.T.astype(bf16))
    give("headmask", (p[:, None] // HD == np.arange(HPC)[None, :]).astype(np.float32))
    give("batchmask", np.where(p[:, None] // E0 == p[None, :] // E0, 0.0, BIG).astype(np.float32))
    k_pos = np.stack([t - t % 8, t % 8, np.full(T, 8)]).astype(bf16)
    slope = np.broadcast_to(head[:, None] / NH, (NH, T))
    q_pos = np.stack([slope, slope, -head[:, None] * (t // P)[None, :]]).astype(bf16)
    give("k_pos", np.broadcast_to(k_pos[:, None, :], (NPOS, GH, T)))
    give("k_one", np.ones((3, GH, T)).astype(bf16))
    give("q_pos", q_pos)

    def scratch(name, shape, dt=FP32):
        return nc.dram_tensor(name, shape, dt, kind="Internal").ap()

    scr = {"w0": scratch("scr_w0", (D, D)), "attn0": scratch("scr_attn0", (B * E0, D)),
           "qs": scratch("scr_q", (3, B, D, T), BF16), "ks": scratch("scr_k", (3, B, D, T), BF16),
           "v": scratch("scr_v", (B, T, NH * VW)), "res": scratch("scr_res", (B, T, D)),
           "m": scratch("scr_m", (NG, 3 * GH * QT, P), BF16)}
    out = nc.dram_tensor("out", (B, T, D), FP32, kind="ExternalOutput").ap()
    prepare(nc, a, scr)
    project(nc, a, scr)
    attend(nc, a, scr, out)
    r = run(nc, [arrays], core_ids=[0])
    return r.results[0]["out"]
```

```python
import concourse.bass as bass
from concourse import mybir
from contextlib import ExitStack

FP32 = mybir.dt.float32
BF16 = mybir.dt.bfloat16
FP32R = mybir.dt.float32r
ALU = mybir.AluOpType
ACT = mybir.ActivationFunctionType
AX = mybir.AxisListType

P = 128
B, T, D = 16, 1024, 256
NH, HD = 16, 16
DC = D // P
E0 = 16
RT = B * E0 // P
BPT = P // E0
HPC = P // HD
MS = 512
TPM = MS // P
STEPS = B * T // MS
GH = 4
NG = NH // GH
QT = T // P
VW = HD + 1
VPAD = GH * VW + 32 - VW
NPOS = 3
NSLOT = 6
KA = NPOS + NSLOT * HD
KB = KA + 3
Q_PART = [0, 0, 0, 1, 1, 2]
K_PART = [0, 1, 2, 0, 1, 0]
EPS = 1e-5
BIG = -1e30
LEAD = 12


class Chain:

    def __init__(self, eng, sem, base=0):
        self.eng, self.sem, self.base, self.n = eng, sem, base, 0

    def __call__(self, ins):
        self.n += 1
        ins.then_inc(self.sem, 1)
        self.eng.wait_ge(self.sem, self.base + self.n)


def prepare(nc, a, scr):
    ctx = ExitStack()
    with ctx:
        def sb(name, shape, dt=FP32):
            return ctx.enter_context(nc.sbuf_tensor(name, shape, dt))

        def sem(name):
            return ctx.enter_context(nc.semaphore(name))

        NC = B * DC
        W = NC * E0
        ROUNDS = 3
        ident = sb("p_ident", [P, P])
        ones = sb("p_ones", [P, P])
        ldT = sb("p_ldT", [100, 4])
        da = sb("p_da", [100, D])
        luT = sb("p_luT", [4, 50])
        uaT = sb("p_uaT", [50, D])
        t1 = sb("p_t1", [4, D])
        t2 = sb("p_t2", [50, D])
        wt = sb("p_wt", [P, DC, D])
        x = sb("p_x", [P, RT, D])
        xn = sb("p_xn", [P, RT, D])
        lna = sb("p_lna", [P, D])
        stats = sb("p_stats", [P, RT, 6])
        mv = sb("p_mv", [P, RT, 2])
        ve0 = sb("p_row_ve", [P, RT])
        rstd0 = sb("p_row_rstd", [P, RT])
        xT = sb("p_xT", [P, DC, RT * P])
        wqkv = sb("p_wqkv", [P, 3, DC, D])
        wo = sb("p_wo", [P, DC, D])
        bq = sb("p_bq", [P, DC])
        bv = sb("p_bv", [P, DC])
        neghalf = sb("p_neghalf", [P, W // P, HPC])
        hmask = sb("p_hmask", [P, HPC])
        avg = sb("p_avg", [P, HPC, HD])
        wl = sb("p_wl", [P, 3, HD])
        bd = sb("p_bd", [P, 3, HPC, HD])
        bl = sb("p_bl", [P, 3])
        lnw = sb("p_lnw", [P, 2])
        qw = sb("p_qw", [P, ROUNDS])
        tsc = sb("p_tsc", [P, 3, ROUNDS])
        sc = sb("p_sc", [P, 3])
        cur = [sb(f"p_cur{i}", [P, W]) for i in range(3)]
        lat = [sb(f"p_lat{i}", [P, W]) for i in range(3)]
        cen = [sb(f"p_cen{i}", [P, W]) for i in range(2)]
        sq = [sb(f"p_sq{i}", [P, W]) for i in range(2)]
        ve = [sb(f"p_ve{i}", [P, W // P, HPC]) for i in range(2)]
        rstd = [sb(f"p_rstd{i}", [P, W // P, HPC]) for i in range(2)]
        wide = [sb(f"p_wide{i}", [P, W // P, HPC, HD]) for i in range(2)]
        avgh = sb("p_avgh", [P, HPC])
        qn = sb("p_qn", [P, W])
        kn = sb("p_kn", [P, 2, W + E0])
        vt = sb("p_vt", [P, 2, W + E0])
        raw = sb("p_raw", [P, 2, 512])
        qbd = sb("p_qbd", [P, NC, HPC, E0])
        pbd = sb("p_pbd", [P, NC, HPC, E0])
        s = sb("p_s", [P, W])
        pt = sb("p_pt", [P, W])
        smax = sb("p_smax", [P, NC])
        ssum = sb("p_ssum", [P, NC])
        ai = [sb(f"p_ai{i}", [P, W]) for i in range(ROUNDS)]
        dif = sb("p_dif", [P, W])
        dsum = sb("p_dsum", [P, 8])
        pair = [ctx.enter_context(nc.psum_tensor(f"p_b{i}", [P, 1024], FP32)) for i in range(4)]
        bank = [pair[i // 2][:, i % 2 * 512:(i % 2 + 1) * 512] for i in range(8)]
        b_lora, b_x, b_lat, b_mean, b_var = bank[0], bank[1], bank[2:5], bank[5:7], bank[0:2]
        b_raw, b_turned, b_dif, b_o = pair[1], pair[2], bank[5], bank[1]
        b_dev = b_mean

        s_xin, s_in, s_late = sem("p_x_in"), sem("p_loaded"), sem("p_loaded_late")
        s_const = sem("p_const")
        s_lora_pe = sem("p_lora_pe")
        s_lora = sem("p_lora")
        s_var = sem("p_var")
        s_rs0 = sem("p_rs0")
        s_xn, s_xT_pe, s_xT = sem("p_xn"), sem("p_xT_pe"), sem("p_xT")
        s_qkv_pe = [sem(f"p_{n}_pe") for n in "qkv"]
        s_cur = [sem(f"p_{n}_ready") for n in "qkv"]
        s_lat_pe = [sem(f"p_lat{n}_pe") for n in "qkv"]
        s_lat = [sem(f"p_lat{n}") for n in "qkv"]
        s_mean_pe, s_cen, s_sq, s_var_pe, s_ve, s_rstd, s_wide, s_dev_pe, s_nrm = (
            [sem(f"p_{w}_{n}") for n in "qk"]
            for w in ("mean_pe", "cen", "sq", "var_pe", "ve", "rstd", "wide", "dev_pe", "nrm"))
        s_vt = sem("p_vt_ready")
        s_qbd = [sem("p_qbd_dve"), sem("p_qbd_act")]
        s_pbd = [sem("p_pbd_dve"), sem("p_pbd_act")]
        s_sc_pe, s_sub, s_exp, s_pt, s_pv_pe = (sem(f"p_{n}") for n in ("scores_pe", "sub", "exp", "pt", "pv_pe"))
        s_raw_pe = sem("p_raw_pe")
        s_raw = [sem("p_raw_dve"), sem("p_raw_act")]
        s_dif, s_dif_pe, s_conv, s_sel = (sem(f"p_{n}") for n in ("dif_ready", "dif_pe", "conv", "sel"))
        s_o_pe, s_o, s_out = sem("p_o_pe"), sem("p_o"), sem("p_stored")
        s_link = sem("p_dve_link")

        groups = lambda t: t.rearrange("p (c n) -> p c n", n=E0)
        turned = b_turned[:, :].rearrange("p (c n) -> p c n", n=2 * E0)[:, :, 0:E0]
        col = lambda t: t.rearrange("p (h o) -> p h o", o=1)
        whole = lambda bk: bk[:, 0:RT * D].rearrange("p (r n) -> p r n", r=RT)
        chunk = lambda t, k: t.rearrange("p (b k n) -> p k b n", k=DC, n=E0)[:, k, :, :]
        by_batch = lambda t: t.rearrange("p (b n) -> p b n", n=E0)

        block = ctx.enter_context(nc.Block())
        rows_k = lambda t: t.rearrange("(k p) n -> p k n", p=P)
        first_sp = [(wqkv[:, 1, :, :], rows_k(a["WkT"])), (wqkv[:, 0, :, :], rows_k(a["WqT"])),
                    (wqkv[:, 2, :, :], rows_k(a["WvT"])), (bq[:, :], a["bq_col"]), (bv[:, :], a["bv_col"])]
        first_act = [(ident[:, :], a["ident"]), (lna[:, :], a["lna_w"].partition_broadcast(P)),
                     (hmask[:, :], a["headmask"]), (wl[:, :, :], a["wl_rep"]), (bl[:, :], a["bl_rep"]),
                     (lnw[:, :], a["lnw_rep"]),
                     (sc[:, 0:1], a["temp"].partition_broadcast(P)),
                     (sc[:, 1:2], a["threshold"].partition_broadcast(P)),
                     (sc[:, 2:3], a["factor"].partition_broadcast(P))]
        late = [(ldT[:, :], a["ldT"]), (da[:, :], a["down_aux"]), (luT[:, :], a["luT"]), (uaT[:, :], a["uaT"]),
                (wt[:, :, :], rows_k(a["W0T"])), (wo[:, :, :], rows_k(a["WoT"]))]
        n_in, n_late = 16 * (len(first_sp) + len(first_act)), 16 * len(late)

        @block.sync
        def _(sp):
            for b in range(B):
                at = b % BPT * E0
                if b % 2 == 0:
                    sp.dma_start(x[at:at + E0, b // BPT, :], a["x"][b, 0:E0, :]).then_inc(s_xin, 16)
            for dst, src in first_sp:
                sp.dma_start(dst, src).then_inc(s_in, 16)
            for dst, src in late:
                sp.dma_start(dst, src).then_inc(s_late, 16)
            sp.wait_ge(s_lora, 3)
            sp.dma_start(scr["w0"].rearrange("(k p) n -> p k n", p=P), wt[:, :, :]).then_inc(s_out, 16)
            sp.wait_ge(s_o, 1)
            sp.dma_start(scr["attn0"].rearrange("(r p) n -> p r n", p=P), xn[:, :, :]).then_inc(s_out, 16)
            sp.wait_ge(s_out, 32)

        @block.gpsimd
        def _(pool):
            pool.memset(ones[:, :], 1.0).then_inc(s_const, 1)
            pool.memset(neghalf[:, :, :], -0.5).then_inc(s_const, 1)
            pool.memset(kn[:, :, W:W + E0], 0.0).then_inc(s_const, 1)
            pool.memset(vt[:, :, W:W + E0], 0.0).then_inc(s_const, 1)
            pool.wait_ge(s_const, 4)
            for n in range(2):
                pool.wait_ge(s_var, n + 1)
                pool.tensor_tensor(rstd0[:, :], ve0[:, :], neghalf[:, 0, 0:RT], ALU.pow).then_inc(s_rs0, 1)
            pool.wait_ge(s_var, 3)
            pool.tensor_tensor(tsc[:, 2, :], tsc[:, 2, :], neghalf[:, 0, 0:ROUNDS], ALU.pow).then_inc(s_rs0, 1)

            def power(n, it):
                pool.wait_ge(s_ve[n], it + 1)
                if it > 0:
                    pool.wait_ge(s_wide[n], it)
                pool.tensor_tensor(rstd[n][:, :, :], ve[n][:, :, :], neghalf[:, :, :], ALU.pow).then_inc(s_rstd[n], 1)

            power(1, 0)
            for it in range(ROUNDS):
                power(0, it)
                if it + 1 < ROUNDS:
                    power(1, it + 1)

        @block.tensor
        def _(pe):
            bdm = bd[:, :, :, :].rearrange("p n h d -> p n (h d)")
            avgm = avg[:, :, :].rearrange("p h d -> p (h d)")

            def latent(n, it):
                if n == 0:
                    pe.wait_ge(s_cur[0], it + 1)
                elif it == 0:
                    pe.wait_ge(s_cur[n], 1)
                else:
                    pe.wait_ge(s_lat[n], it)
                src = cur[n] if n == 0 or it == 0 else lat[n]
                pe.matmul(b_lat[n][:, :], bdm[:, n, :], src[:, :], start=True, stop=True).then_inc(s_lat_pe[n], 1)

            def mean(n, it):
                pe.wait_ge(s_lat[n], it + 1)
                pe.matmul(b_mean[n][:, :], avgm, lat[n][:, :], start=True, stop=True).then_inc(s_mean_pe[n], 1)

            def variance(n, it):
                pe.wait_ge(s_sq[n], it + 1)
                for c in range(W // P):
                    mm = pe.matmul(b_var[n][:, c * HPC:(c + 1) * HPC], sq[n][:, c * P:(c + 1) * P], avgh[:, :],
                                   start=True, stop=True)
                mm.then_inc(s_var_pe[n], 1)

            def deviation(n, it):
                pe.wait_ge(s_wide[n], it + 1)
                for c in range(W // P):
                    mm = pe.transpose(b_dev[n][:, c * P:(c + 1) * P],
                                      wide[n][:, c, :, :].rearrange("p h d -> p (h d)"), ident[:, :])
                mm.then_inc(s_dev_pe[n], 1)

            def products(rows, spread):
                for c in range(NC):
                    at = 32 * (c % 4)
                    mm = pe.matmul(b_raw[at:at + 32, c // 4 * P:(c // 4 + 1) * P], rows[:, c * E0:c * E0 + 2 * E0],
                                   spread[:, c, :, :].rearrange("p h n -> p (h n)"), start=True, stop=True)
                return mm

            def turn_back(copied):
                for half in range(2):
                    pe.wait_ge(s_raw[half], copied)
                for c in range(NC // 4):
                    mm = pe.transpose(b_turned[:, c * P:(c + 1) * P], raw[:, c // 4, c % 4 * P:(c % 4 + 1) * P], ident[:, :])
                return mm

            pe.wait_ge(s_in, n_in)
            pe.wait_ge(s_xn, 1)
            for k in range(DC):
                for r in range(RT):
                    at = (k * RT + r) * P
                    mm = pe.transpose(b_x[:, at:at + P], xn[:, r, k * P:(k + 1) * P], ident[:, :])
            mm.then_inc(s_xT_pe, 1)
            pe.wait_ge(s_late, n_late)
            pe.matmul(b_lora[0:4, 0:D], ldT[:, :], da[:, :], start=True, stop=True).then_inc(s_lora_pe, 1)
            pe.wait_ge(s_xT, 1)
            for n in (1, 0, 2):
                for k in range(DC):
                    for c in range(DC):
                        mm = pe.matmul(b_lat[n][:, k * RT * P:(k + 1) * RT * P], wqkv[:, n, c, k * P:(k + 1) * P],
                                       xT[:, c, :], start=(c == 0), stop=(c == DC - 1))
                mm.then_inc(s_qkv_pe[n], 1)
            pe.wait_ge(s_lora, 1)
            pe.matmul(b_lora[0:50, 0:D], luT[:, :], t1[:, :], start=True, stop=True).then_inc(s_lora_pe, 1)
            latent(1, 0)
            latent(2, 0)
            pe.wait_ge(s_lora, 2)
            for k in range(DC):
                mm = pe.matmul(b_lora[:, k * D:(k + 1) * D], t2[:, k * P:(k + 1) * P], uaT[:, :],
                               start=True, stop=True)
            mm.then_inc(s_lora_pe, 1)
            mean(1, 0)
            variance(1, 0)
            deviation(1, 0)
            for it in range(ROUNDS):
                more = it + 1 < ROUNDS
                latent(0, it)
                if more:
                    latent(1, it + 1)
                mean(0, it)
                if more:
                    latent(2, it + 1)
                if it == 0:
                    pe.wait_ge(s_lora, 3)
                variance(0, it)
                if more:
                    pe.wait_ge(s_nrm[1], it + 1)
                    mean(1, it + 1)
                    variance(1, it + 1)
                deviation(0, it)
                pe.wait_ge(s_nrm[1], it + 1)
                for half in range(2):
                    pe.wait_ge(s_qbd[half], it + 1)
                pe.wait_ge(s_lat[2], min(it + 2, ROUNDS))
                products(kn[:, it % 2, :], qbd).then_inc(s_raw_pe, 1)
                turn_back(2 * it + 1).then_inc(s_sc_pe, 1)
                if more:
                    deviation(1, it + 1)
                for half in range(2):
                    pe.wait_ge(s_pbd[half], it + 1)
                products(vt[:, it % 2, :], pbd).then_inc(s_raw_pe, 1)
                turn_back(2 * it + 2).then_inc(s_pv_pe, 1)
                if it == 1:
                    pe.wait_ge(s_dif, 1)
                    pe.matmul(b_dif[:, 0:1], ones[:, :], dsum[:, 0:1], start=True, stop=True).then_inc(s_dif_pe, 1)
                    pe.wait_ge(s_conv, 1)
            pe.wait_ge(s_sel, 1)
            for r in range(RT):
                for k in range(DC):
                    mm = pe.matmul(b_o[:, r * D:(r + 1) * D], xT[:, k, r * P:(r + 1) * P], wo[:, k, :],
                                   start=(k == 0), stop=(k == DC - 1))
            mm.then_inc(s_o_pe, 1)

        @block.scalar
        def _(act):
            for b in range(1, B, 2):
                at = b % BPT * E0
                act.dma_start(x[at:at + E0, b // BPT, :], a["x"][b, 0:E0, :]).then_inc(s_xin, 16)
            for dst, src in first_act:
                act.dma_start(dst, src).then_inc(s_in, 16)

            def latent(n, it):
                act.wait_ge(s_lat_pe[n], it + 1)
                if n == 2 and it > 0:
                    act.wait_ge(s_vt, it)
                if n == 0 and it > 0:
                    act.wait_ge(s_cen[0], it)
                nc.scalar.activation(lat[n][:, :], b_lat[n][:, :], ACT.Identity, bias=bl[:, n:n + 1]).then_inc(s_lat[n], 1)

            def square(n, it):
                act.wait_ge(s_cen[n], it + 1)
                if it > 0:
                    act.wait_ge(s_var_pe[n], it)
                nc.scalar.activation(sq[n][:, :], cen[n][:, :], ACT.Square).then_inc(s_sq[n], 1)

            def spread(dst, src, s_done):
                for h in range(HPC // 2, HPC):
                    i = nc.scalar.activation(dst[:, :, h, :], groups(src[:, :]), ACT.Copy, scale=hmask[:, h:h + 1])
                i.then_inc(s_done, 1)

            def copy_raw(n):
                act.wait_ge(s_raw_pe, n)
                nc.scalar.copy(raw[:, 1, :], b_raw[:, 512:1024]).then_inc(s_raw[1], 1)

            act.wait_ge(s_in, n_in)
            act.wait_ge(s_lora_pe, 1)
            nc.scalar.copy(t1[:, :], b_lora[0:4, 0:D]).then_inc(s_lora, 1)
            act.wait_ge(s_qkv_pe[1], 1)
            for k in range(DC):
                i = nc.scalar.activation(chunk(cur[1][:, :], k), by_batch(b_lat[1][:, k * RT * P:(k + 1) * RT * P]),
                                         ACT.Copy, scale=HD ** -0.25)
            i.then_inc(s_cur[1], 1)
            act.wait_ge(s_qkv_pe[2], 1)
            for k in range(DC):
                i = nc.scalar.activation(chunk(cur[2][:, :], k), by_batch(b_lat[2][:, k * RT * P:(k + 1) * RT * P]),
                                         ACT.Identity, bias=bv[:, k:k + 1])
            i.then_inc(s_cur[2], 1)
            act.wait_ge(s_lora_pe, 2)
            nc.scalar.copy(t2[:, :], b_lora[0:50, 0:D]).then_inc(s_lora, 1)
            latent(1, 0)
            latent(2, 0)
            square(1, 0)
            for it in range(ROUNDS):
                more = it + 1 < ROUNDS
                latent(0, it)
                if more:
                    latent(1, it + 1)
                square(0, it)
                if more:
                    latent(2, it + 1)
                    square(1, it + 1)
                act.wait_ge(s_nrm[0], it + 1)
                if it > 0:
                    act.wait_ge(s_sc_pe, it)
                spread(qbd, qn, s_qbd[1])
                copy_raw(2 * it + 1)
                act.wait_ge(s_sub, it + 1)
                nc.scalar.activation(s[:, :], s[:, :], ACT.Exp).then_inc(s_exp, 1)
                act.wait_ge(s_pt, it + 1)
                if it > 0:
                    act.wait_ge(s_pv_pe, it)
                spread(pbd, pt, s_pbd[1])
                copy_raw(2 * it + 2)

        @block.vector
        def _(dve):
            V = nc.vector
            link = Chain(dve, s_link)

            def centre(n, it):
                dve.wait_ge(s_mean_pe[n], it + 1)
                if it > 0:
                    dve.wait_ge(s_nrm[n], it)
                    dve.wait_ge(s_sq[n], it)
                V.tensor_tensor(cen[n][:, :], lat[n][:, :], b_mean[n][:, :], ALU.subtract).then_inc(s_cen[n], 1)

            def eps(n, it):
                dve.wait_ge(s_var_pe[n], it + 1)
                if it > 0:
                    dve.wait_ge(s_rstd[n], it)
                V.tensor_scalar(ve[n][:, :, :].rearrange("p c h -> p (c h)"), b_var[n][:, 0:NC], EPS, None,
                                ALU.add).then_inc(s_ve[n], 1)

            def widen(n, it):
                dve.wait_ge(s_rstd[n], it + 1)
                if it > 0:
                    dve.wait_ge(s_dev_pe[n], it)
                V.tensor_copy(wide[n][:, :, :, :].rearrange("p c h d -> p (c h) d"),
                              col(rstd[n][:, :, :].rearrange("p c h -> p (c h)")).to_broadcast([P, NC, HD])
                              ).then_inc(s_wide[n], 1)

            def norm(n, it):
                dve.wait_ge(s_dev_pe[n], it + 1)
                if n == 0 and it > 0:
                    for half in range(2):
                        dve.wait_ge(s_qbd[half], it)
                if n == 1 and it > 1:
                    dve.wait_ge(s_sc_pe, it - 1)
                dst, weight = (qn[:, :], qw[:, it:it + 1]) if n == 0 else (kn[:, it % 2, 0:W], lnw[:, 1:2])
                V.scalar_tensor_tensor(dst, cen[n][:, :], weight, b_dev[n][:, :], ALU.mult, ALU.mult).then_inc(s_nrm[n], 1)

            def swap_v(it):
                dve.wait_ge(s_lat[2], it + 1)
                if it > 1:
                    dve.wait_ge(s_pv_pe, it - 1)
                V.transpose(vt[:, it % 2, 0:W], lat[2][:, :]).then_inc(s_vt, 1)

            def spread(dst, src, s_done):
                for h in range(HPC // 2):
                    i = V.tensor_scalar(dst[:, :, h, :], groups(src[:, :]), hmask[:, h:h + 1], None, ALU.mult)
                i.then_inc(s_done, 1)

            def copy_raw(n):
                dve.wait_ge(s_raw_pe, n)
                V.tensor_copy(raw[:, 0, :], b_raw[:, 0:512]).then_inc(s_raw[0], 1)

            dve.wait_ge(s_xin, 16 * B)
            dve.wait_ge(s_const, 4)
            for n in range(2):
                src = x if n == 0 else xn
                for r in range(RT):
                    link(V.bn_stats(stats[:, r, :], src[:, r, :]))
                    link(V.bn_aggr(mv[:, r, :], stats[:, r, :]))
                V.tensor_scalar(ve0[:, :], mv[:, :, 1], EPS, None, ALU.add).then_inc(s_var, 1)
                dve.wait_ge(s_rs0, n + 1)
                for r in range(RT):
                    link(V.tensor_scalar(xn[:, r, :], src[:, r, :], mv[:, r, 0:1], rstd0[:, r:r + 1],
                                         ALU.subtract, ALU.mult))
            dve.wait_ge(s_in, n_in)
            V.tensor_tensor(xn[:, :, :], xn[:, :, :],
                            lna[:, :].rearrange("p (o n) -> p o n", o=1).to_broadcast([P, RT, D]),
                            ALU.mult).then_inc(s_xn, 1)
            for h in range(HPC):
                V.tensor_scalar(bd[:, :, h, :], wl[:, :, :], hmask[:, h:h + 1], None, ALU.mult)
            V.tensor_scalar(avgh[:, :], hmask[:, :], 1.0 / HD, None, ALU.mult)
            V.tensor_scalar(avg[:, :, :], col(hmask[:, :]).to_broadcast([P, HPC, HD]), 1.0 / HD, None, ALU.mult)
            dve.wait_ge(s_xT_pe, 1)
            V.tensor_copy(xT[:, :, :], whole(b_x)).then_inc(s_xT, 1)
            for it in range(ROUNDS):
                i = V.tensor_scalar(tsc[:, 0, it:it + 1], sc[:, 0:1], 0.005 * it, None, ALU.add)
            link(i)
            link(V.tensor_scalar(tsc[:, 1, :], tsc[:, 0, :], 0.0, None, ALU.is_gt))
            link(V.tensor_tensor(tsc[:, 0, :], tsc[:, 0, :], tsc[:, 1, :], ALU.mult))
            link(V.tensor_scalar(tsc[:, 1, :], tsc[:, 1, :], -1.0, 1.0, ALU.mult, ALU.add))
            V.tensor_tensor(tsc[:, 2, :], tsc[:, 0, :], tsc[:, 1, :], ALU.add).then_inc(s_var, 1)
            dve.wait_ge(s_qkv_pe[0], 1)
            for k in range(DC):
                i = V.tensor_scalar(chunk(cur[0][:, :], k), by_batch(b_lat[0][:, k * RT * P:(k + 1) * RT * P]),
                                    bq[:, k:k + 1], HD ** -0.25, ALU.add, ALU.mult)
            i.then_inc(s_cur[0], 1)
            dve.wait_ge(s_rs0, 3)
            link(V.tensor_scalar(qw[:, :], tsc[:, 2, :], lnw[:, 0:1], HD ** -0.5, ALU.mult, ALU.mult))
            centre(1, 0)
            dve.wait_ge(s_lora_pe, 3)
            V.tensor_tensor(wt[:, :, :], wt[:, :, :], b_lora[:, :].rearrange("p (k n) -> p k n", k=DC),
                            ALU.add).then_inc(s_lora, 1)
            eps(1, 0)
            swap_v(0)
            widen(1, 0)
            norm(1, 0)
            for it in range(ROUNDS):
                more = it + 1 < ROUNDS
                centre(0, it)
                eps(0, it)
                if more:
                    centre(1, it + 1)
                    eps(1, it + 1)
                widen(0, it)
                norm(0, it)
                dve.wait_ge(s_nrm[0], it + 1)
                if it > 0:
                    dve.wait_ge(s_sc_pe, it)
                spread(qbd, qn, s_qbd[0])
                if more:
                    swap_v(it + 1)
                copy_raw(2 * it + 1)
                dve.wait_ge(s_sc_pe, it + 1)
                link(V.tensor_reduce(smax[:, :], turned, AX.X, ALU.max))
                V.tensor_tensor(groups(s[:, :]), turned, col(smax[:, :]).to_broadcast([P, NC, E0]),
                                ALU.subtract).then_inc(s_sub, 1)
                if more:
                    widen(1, it + 1)
                dve.wait_ge(s_exp, it + 1)
                link(V.tensor_reduce(ssum[:, :], groups(s[:, :]), AX.X, ALU.add))
                link(V.reciprocal(ssum[:, :], ssum[:, :]))
                link(V.tensor_tensor(groups(s[:, :]), groups(s[:, :]), col(ssum[:, :]).to_broadcast([P, NC, E0]), ALU.mult))
                if it > 0:
                    for half in range(2):
                        dve.wait_ge(s_pbd[half], it)
                V.transpose(pt[:, :], s[:, :]).then_inc(s_pt, 1)
                dve.wait_ge(s_pt, it + 1)
                if it > 0:
                    dve.wait_ge(s_pv_pe, it)
                spread(pbd, pt, s_pbd[0])
                if more:
                    norm(1, it + 1)
                copy_raw(2 * it + 2)
                dve.wait_ge(s_pv_pe, it + 1)
                link(V.transpose(ai[it][:, :], turned))
                if more:
                    V.tensor_tensor(cur[0][:, :], cur[0][:, :], ai[it][:, :], ALU.add).then_inc(s_cur[0], 1)
                if it == 1:
                    link(V.tensor_tensor(dif[:, :], ai[1][:, :], ai[0][:, :], ALU.subtract))
                    V.tensor_reduce(dsum[:, 0:1], dif[:, :], AX.X, ALU.add, apply_absolute_value=True).then_inc(s_dif, 1)
                    dve.wait_ge(s_dif_pe, 1)
                    V.tensor_scalar(dsum[:, 1:2], b_dif[:, 0:1], 1.0 / (B * T * D), None, ALU.mult).then_inc(s_conv, 1)
                    dve.wait_ge(s_conv, 1)
                    link(V.tensor_scalar(dsum[:, 2:3], dsum[:, 1:2], sc[:, 2:3], sc[:, 1:2], ALU.mult, ALU.add))
                    link(V.tensor_tensor(dsum[:, 3:4], dsum[:, 1:2], dsum[:, 2:3], ALU.is_lt))
                    link(V.tensor_scalar(dsum[:, 4:5], dsum[:, 3:4], -1.0, 1.0, ALU.mult, ALU.add))
            link(V.tensor_scalar(ai[1][:, :], ai[1][:, :], dsum[:, 3:4], None, ALU.mult))
            for k in range(DC):
                i = V.scalar_tensor_tensor(by_batch(xT[:, k, :]), chunk(ai[2][:, :], k), dsum[:, 4:5],
                                           chunk(ai[1][:, :], k), ALU.mult, ALU.add)
            i.then_inc(s_sel, 1)
            dve.wait_ge(s_o_pe, 1)
            V.tensor_copy(xn[:, :, :], whole(b_o)).then_inc(s_o, 1)


def project(nc, a, scr):
    ctx = ExitStack()
    with ctx:
        def sb(name, shape, dt=FP32):
            return ctx.enter_context(nc.sbuf_tensor(name, shape, dt))

        def sem(name):
            return ctx.enter_context(nc.semaphore(name))

        ident = sb("j_ident", [P, P])
        names = ("w0", "wq", "wk", "wv", "wr", "wkk", "wvv")
        w_hi = sb("j_w_hi", [P, len(names), DC, D], FP32R)
        w_lo = sb("j_w_lo", [P, len(names), DC, D], FP32R)
        w = {n: (w_hi[:, i, :, :], w_lo[:, i, :, :]) for i, n in enumerate(names)}
        bias0 = sb("j_bias0", [P, 2, D])
        vbias = sb("j_vbias", [P, D])
        obias = sb("j_obias", [P, D])
        qbias = sb("j_qbias", [P, DC])
        kbias = sb("j_kbias", [P, DC])
        mu = sb("j_mu", [P, 2, DC])
        omu = sb("j_omu", [P, 2, DC])
        neghalf = sb("j_neghalf", [P, TPM])
        x = sb("j_x", [P, 2, TPM, D])
        att = sb("j_att", [E0, D])
        xn = sb("j_xn", [P, TPM, D])
        xT = [sb(f"j_xT{i}", [P, DC, MS], FP32R) for i in range(2)]
        x1 = sb("j_x1", [P, 2, TPM, D])
        x1n = sb("j_x1n", [P, TPM, D])
        x1T = sb("j_x1T", [P, 2, DC, MS + 1])
        stats = sb("j_stats", [P, 2, TPM, 6])
        mv = sb("j_mv", [P, 2, TPM, 2])
        ve = sb("j_ve", [P, 2, TPM])
        hold = sb("j_hold", [P, 1])
        rstd = sb("j_rstd", [P, 2, TPM])
        x1s = [sb(f"j_x1s{i}", [P, DC, MS], FP32R) for i in range(2)]
        mix = sb("j_mix", [P, 2, DC, MS])
        mixs = [sb(f"j_mixs{i}", [P, 2, DC, MS], FP32R) for i in range(2)]
        full = sb("j_full", [P, 2, DC, MS])
        rest = sb("j_rest", [P, 2, DC, MS])
        part = sb("j_part", [P, 3, 3, DC, MS], BF16)
        v = sb("j_v", [P, 2, TPM, NH, VW])
        kact = sb("j_kact", [P, DC, MS])
        kfull = sb("j_kfull", [P, DC, MS])
        ksq = [sb(f"j_ksq{i}", [P, DC, MS], FP32R) for i in range(2)]
        gate = sb("j_gate", [P, TPM, D])
        ffn = sb("j_ffn", [P, TPM, D])
        res = sb("j_res", [P, 2, TPM, D])
        bank = [ctx.enter_context(nc.psum_tensor(f"j_b{i}", [P, 2 * 512], FP32)) for i in range(4)]

        s_w = sem("j_weights")
        s_set = sem("j_set")
        s_x = [sem(f"j_x_in{i}") for i in range(2)]
        s_att = sem("j_att_in")
        s_var0, s_rs0, s_xn = sem("j_var0"), sem("j_rs0"), sem("j_xn_ready")
        s_var1, s_rs1, s_x1n = sem("j_var1"), sem("j_rs1"), sem("j_x1n_ready")
        s_t1, s_xT = sem("j_t1_pe"), sem("j_xT_ready")
        s_f0, s_xb, s_x1 = sem("j_f0_pe"), sem("j_xb_ready"), sem("j_x1_ready")
        s_t2, s_x1T = sem("j_t2_pe"), sem("j_x1T_ready")
        s_xTl, s_x1l = sem("j_xT_lo"), sem("j_x1T_lo")
        s_xmu, s_mix = sem("j_xmu_ready"), [sem("j_mixr_ready"), sem("j_mixk_ready")]
        s_mixh, s_mixl = [sem("j_mixr_hi"), sem("j_mixk_hi")], [sem("j_mixr_lo"), sem("j_mixk_lo")]
        s_ksh, s_ksl = sem("j_ksq_hi"), sem("j_ksq_lo")
        s_wh = sem("j_w_hi_done")
        s_neg = sem("j_neghalf_set")
        s_q, s_full = sem("j_q_pe"), [sem("j_q_full"), sem("j_k_full")]
        s_k = sem("j_k_pe")
        s_hi, s_res1 = [sem("j_q_hi"), sem("j_k_hi")], [sem("j_q_res1"), sem("j_k_res1")]
        s_mid, s_lo = [sem("j_q_mid"), sem("j_k_mid")], [sem("j_q_lo"), sem("j_k_lo")]
        s_v, s_vb = sem("j_v_pe"), sem("j_v_ready")
        s_kk, s_relu, s_ksq = sem("j_kk_pe"), sem("j_relu"), sem("j_ksq")
        s_r, s_tanh = sem("j_r_pe"), sem("j_tanh")
        s_kv, s_ffn, s_xo, s_res = sem("j_kv_pe"), sem("j_ffn_ready"), sem("j_xo_ready"), sem("j_res_ready")
        s_q_out, s_k_out = sem("j_q_stored"), [sem(f"j_k_stored{i}") for i in range(2)]
        s_v_out = [sem(f"j_v_stored{i}") for i in range(2)]
        s_res_out = [sem(f"j_res_stored{i}") for i in range(2)]
        s_link = sem("j_dve_link")
        s_xbias = sem("j_xbias")

        xt = a["x"].rearrange("b (h t p) c -> (b h) p t c", p=P, t=TPM)
        res_d = scr["res"].rearrange("b (h t p) c -> (b h) p t c", p=P, t=TPM)
        v_d = scr["v"].rearrange("b (h t p) c -> (b h) p t c", p=P, t=TPM)
        part_d = [scr[n].rearrange("s b (k p) t -> b s p k t", p=P) for n in ("qs", "ks")]
        att_d = scr["attn0"].rearrange("(b t) n -> b t n", t=E0)
        rows = lambda bk: bk[:, :].rearrange("p (t n) -> p t n", t=TPM)
        chunks = lambda bk: bk[:, :].rearrange("p (k n) -> p k n", k=DC)
        every = lambda t, n=TPM: t.rearrange("p (o n) -> p o n", o=1).to_broadcast([P, n, D])

        block = ctx.enter_context(nc.Block())
        lo = [(ident[:, :], a["ident"])]
        stage = [full[:, i // DC, i % DC, :].rearrange("p (k n) -> p k n", k=DC) for i in range(4)]
        stage += [rest[:, i // DC, i % DC, :].rearrange("p (k n) -> p k n", k=DC) for i in range(3)]
        lo += [(stage[i], src.rearrange("(k p) n -> p k n", p=P)) for i, src in enumerate(
            (scr["w0"], a["q_w"], a["kv_w"][:, 0:D], a["kv_w"][:, D:2 * D], a["WrT"], a["WkkT"], a["WvvT"]))]
        lo += [(bias0[:, 0, :], a["b0"].partition_broadcast(P)), (bias0[:, 1, :], a["bo"].partition_broadcast(P)),
               (vbias[:, :], a["kv_b"][D:2 * D].partition_broadcast(P)),
               (obias[:, :], a["o_b"].partition_broadcast(P)),
               (mu[:, 0, :], a["mu_r_col"]), (mu[:, 1, :], a["mu_k_col"]),
               (qbias[:, :], a["q_b_col"]), (kbias[:, :], a["k_b_col"])]
        n_w = 16 * len(lo)
        N_SET = 8

        @block.sync
        def _(sp):
            sp.dma_start(x[:, 0, :, :], xt[0]).then_inc(s_x[0], 16)
            for dst, src in lo[1::2]:
                sp.dma_start(dst, src).then_inc(s_w, 16)
            sp.dma_start(x[:, 1, :, :], xt[1]).then_inc(s_x[1], 16)
            sp.dma_start(att[:, :], att_d[0]).then_inc(s_att, 16)

            def store_parts(n, slot, b, half, done, s_out):
                sp.wait_ge(s_lo[n], done)
                for s in range(3):
                    sp.dma_start(part_d[n][b, s][:, :, half * MS:(half + 1) * MS], part[:, slot, s, :, :]).then_inc(s_out, 16)

            def store_late(m, b, half):
                store_parts(1, 1 + half, b, half, m + 1, s_k_out[half])
                sp.wait_ge(s_res, m + 1)
                sp.dma_start(res_d[m], res[:, half, :, :]).then_inc(s_res_out[half], 16)

            def step(b, half, first, more):
                m = 2 * b + half
                if half == 0 and more:
                    sp.wait_ge(s_xb, 2 * b + 1)
                    sp.dma_start(att[:, :], att_d[b + 1]).then_inc(s_att, 16)
                if more:
                    sp.wait_ge(s_x1, m + 1)
                    sp.dma_start(x[:, half, :, :], xt[m + 2]).then_inc(s_x[half], 16)
                if not first:
                    store_late(m - 1, b - 1 + half, 1 - half)
                sp.wait_ge(s_vb, m + 1)
                sp.dma_start(v_d[m], v[:, half, :, :, :].rearrange("p t h d -> p t (h d)")).then_inc(s_v_out[half], 16)
                store_parts(0, 0, b, half, m + 1, s_q_out)

            step(0, 0, True, True)
            step(0, 1, False, True)
            with sp.Fori(1, B - 1) as b:
                for half in range(2):
                    step(b, half, False, True)
            for half in range(2):
                step(B - 1, half, False, False)
            store_late(STEPS - 1, B - 1, 1)
            sp.wait_ge(s_q_out, 48 * STEPS)
            for n in range(2):
                sp.wait_ge(s_k_out[n], 48 * B)
                sp.wait_ge(s_v_out[n], 16 * B)
                sp.wait_ge(s_res_out[n], 16 * B)

        @block.tensor
        def _(pe):
            def turn(bk, src):
                for k in range(DC):
                    for t in range(TPM):
                        at = k * MS + t * P
                        mm = pe.transpose(bk[:, at:at + P], src[:, t, k * P:(k + 1) * P], ident[:, :])
                return mm

            TERMS = [(k, x, y) for k in range(DC) for x, y in ((0, 0), (0, 1), (1, 0))]

            def by_token(bk, src, weight):
                for t in range(TPM):
                    for n, (k, x, y) in enumerate(TERMS):
                        mm = pe.matmul(bk[:, t * D:(t + 1) * D], src[x][:, k, t * P:(t + 1) * P], weight[y][:, k, :],
                                       start=(n == 0), stop=(n == len(TERMS) - 1))
                return mm

            def by_dim(bk, src, weight):
                for c in range(DC):
                    for n, (k, y, x) in enumerate(TERMS):
                        mm = pe.matmul(bk[:, c * MS:(c + 1) * MS], weight[y][:, k, c * P:(c + 1) * P], src[x][:, k, :],
                                       start=(n == 0), stop=(n == len(TERMS) - 1))
                return mm

            mixed = [[t[:, i, :, :] for t in mixs] for i in range(2)]

            def step(m, half, first, more):
                own, other = bank[2 + half], bank[3 - half]
                pe.wait_ge(s_x1n, m + 1)
                if not first:
                    pe.wait_ge(s_full[1], m)
                turn(bank[0], x1n).then_inc(s_t2, 1)
                if more:
                    pe.wait_ge(s_xn, m + 2)
                    if not first:
                        pe.wait_ge(s_vb, m)
                    turn(bank[1], xn).then_inc(s_t1, 1)
                if not first:
                    pe.wait_ge(s_ksl, m)
                    by_token(other, ksq, w["wvv"]).then_inc(s_kv, 1)
                pe.wait_ge(s_x1l, m + 1)
                if not first:
                    pe.wait_ge(s_tanh, m)
                by_dim(own, x1s, w["wq"]).then_inc(s_q, 1)
                if more:
                    pe.wait_ge(s_xTl, m + 2)
                    if not first:
                        pe.wait_ge(s_ffn, m)
                    by_token(other, xT, w["w0"]).then_inc(s_f0, 1)
                by_dim(bank[0], x1s, w["wk"]).then_inc(s_k, 1)
                if not more:
                    pe.wait_ge(s_vb, m)
                by_token(bank[1], x1s, w["wv"]).then_inc(s_v, 1)
                pe.wait_ge(s_mixl[1], m + 1)
                pe.wait_ge(s_full[0], m + 1)
                by_dim(own, mixed[1], w["wkk"]).then_inc(s_kk, 1)
                pe.wait_ge(s_mixl[0], m + 1)
                if more:
                    pe.wait_ge(s_x1, m + 2)
                else:
                    pe.wait_ge(s_ffn, m)
                by_token(other, mixed[0], w["wr"]).then_inc(s_r, 1)

            pe.wait_ge(s_w, n_w)
            pe.wait_ge(s_set, N_SET)
            pe.wait_ge(s_xn, 1)
            turn(bank[1], xn).then_inc(s_t1, 1)
            pe.wait_ge(s_xTl, 1)
            by_token(bank[2], xT, w["w0"]).then_inc(s_f0, 1)
            pe.wait_ge(s_x1, 1)
            step(0, 0, True, True)
            step(1, 1, False, True)
            with pe.Fori(1, B - 1) as b:
                for half in range(2):
                    step(2 * b + half, half, False, True)
            step(STEPS - 2, 0, False, True)
            step(STEPS - 1, 1, False, False)
            pe.wait_ge(s_ksl, STEPS)
            by_token(bank[3], ksq, w["wvv"]).then_inc(s_kv, 1)

        @block.scalar
        def _(act):
            def high_part(n, slot):
                nc.scalar.copy(part[:, slot, 0, :, :], full[:, n, :, :]).then_inc(s_hi[n], 1)

            def middle_part(n, slot, m):
                act.wait_ge(s_res1[n], m + 1)
                nc.scalar.copy(part[:, slot, 1, :, :], rest[:, n, :, :]).then_inc(s_mid[n], 1)

            def mix_high(i, m, first):
                act.wait_ge(s_mix[i], m + 1)
                if not first:
                    act.wait_ge(s_kk if i == 1 else s_r, m)
                nc.scalar.copy(mixs[0][:, i, :, :], mix[:, i, :, :]).then_inc(s_mixh[i], 1)

            def step(m, b, half, first, more):
                own, other = bank[2 + half], bank[3 - half]
                act.wait_ge(s_t2, m + 1)
                nc.scalar.copy(x1s[0][:, :, :], chunks(bank[0]))
                nc.scalar.copy(x1T[:, half, :, 1:MS + 1], chunks(bank[0])).then_inc(s_x1T, 1)
                if more:
                    act.wait_ge(s_t1, m + 2)
                    act.wait_ge(s_f0, m + 1)
                    nc.scalar.copy(xT[0][:, :, :], chunks(bank[1])).then_inc(s_xT, 1)
                act.wait_ge(s_x1T, m + 1)
                if half == 1:
                    nc.scalar.copy(x1T[:, 1, :, 0:1], x1T[:, 0, :, MS:MS + 1]).then_inc(s_xmu, 1)
                for i in (1, 0):
                    if not first:
                        act.wait_ge(s_mixl[i], m)
                    for k in range(DC):
                        nc.scalar.activation(mix[:, i, k, :], x1T[:, half, k, 1:MS + 1], ACT.Copy,
                                             scale=mu[:, i, k:k + 1]).then_inc(s_xmu, 1)
                if not first:
                    middle_part(1, 2 - half, m - 1)
                mix_high(1, m, first)
                act.wait_ge(s_q, m + 1)
                if not first:
                    act.wait_ge(s_res1[0], m)
                    act.wait_ge(s_hi[0], m)
                for k in range(DC):
                    i = nc.scalar.activation(full[:, 0, k, :], own[:, k * MS:(k + 1) * MS], ACT.Identity,
                                             bias=qbias[:, k:k + 1], scale=HD ** -0.5)
                i.then_inc(s_full[0], 1)
                mix_high(0, m, first)
                act.wait_ge(s_full[0], m + 1)
                if not first:
                    act.wait_ge(s_q_out, 48 * m)
                high_part(0, 0)
                act.wait_ge(s_k, m + 1)
                if not first:
                    act.wait_ge(s_res1[1], m)
                    act.wait_ge(s_hi[1], m)
                for k in range(DC):
                    i = nc.scalar.activation(full[:, 1, k, :], bank[0][:, k * MS:(k + 1) * MS], ACT.Identity,
                                             bias=kbias[:, k:k + 1])
                i.then_inc(s_full[1], 1)
                middle_part(0, 0, m)
                act.wait_ge(s_full[1], m + 1)
                if not (isinstance(b, int) and b == 0):
                    act.wait_ge(s_k_out[half], 48 * b)
                high_part(1, 1 + half)
                act.wait_ge(s_kk, m + 1)
                if not first:
                    act.wait_ge(s_ksq, m)
                    act.wait_ge(s_kv, m)
                    act.wait_ge(s_ksl, m)
                nc.scalar.activation(kact[:, :, :], chunks(own), ACT.Relu).then_inc(s_relu, 1)
                act.wait_ge(s_relu, m + 1)
                nc.scalar.activation(ksq[0][:, :, :], kact[:, :, :], ACT.Square)
                nc.scalar.activation(kfull[:, :, :], kact[:, :, :], ACT.Square).then_inc(s_ksq, 1)
                act.wait_ge(s_r, m + 1)
                if not first:
                    act.wait_ge(s_ffn, m)
                nc.scalar.activation(gate[:, :, :], rows(other), ACT.Tanh, scale=0.5).then_inc(s_tanh, 1)

            for dst, src in lo[0::2]:
                act.dma_start(dst, src).then_inc(s_w, 16)
            act.wait_ge(s_w, n_w)
            flat4 = lambda t: t.rearrange("p a k n -> p (a k n)")
            nc.scalar.copy(flat4(w_hi[:, 0:4, :, :]), flat4(full[:, :, :, :])).then_inc(s_wh, 1)
            nc.scalar.copy(flat4(w_hi[:, 4:6, :, :]), flat4(rest[:, :, :, :])[:, 0:2 * DC * D]).then_inc(s_wh, 1)
            nc.scalar.activation(w_hi[:, 6, :, :].rearrange("p k n -> p (k n)"),
                                 flat4(rest[:, :, :, :])[:, 2 * DC * D:3 * DC * D], ACT.Copy, scale=0.5).then_inc(s_wh, 1)
            act.wait_ge(s_set, N_SET)
            act.wait_ge(s_t1, 1)
            nc.scalar.copy(xT[0][:, :, :], chunks(bank[1])).then_inc(s_xT, 1)
            step(0, 0, 0, True, True)
            step(1, 0, 1, False, True)
            with act.Fori(1, B - 1) as b:
                for half in range(2):
                    step(2 * b + half, b, half, False, True)
            step(STEPS - 2, B - 1, 0, False, True)
            step(STEPS - 1, B - 1, 1, False, False)
            middle_part(1, 2, STEPS - 1)

        @block.vector
        def _(dve):
            V = nc.vector
            STEP_LINKS, PRO_LINKS = 4, 6

            def norm_stats(z, src, link, s_var):
                for t in range(TPM):
                    i = V.bn_stats(stats[:, z, t, :], src[:, t, :])
                link(i)
                V.memset(hold[:, :], 0.0)
                for t in range(TPM):
                    i = V.bn_aggr(mv[:, z, t, :], stats[:, z, t, :])
                link(i)
                V.tensor_scalar(ve[:, z, :], mv[:, z, :, 1], EPS, None, ALU.add).then_inc(s_var, 1)

            def normalise(z, src, dst, s_done):
                for t in range(TPM):
                    i = V.tensor_scalar(dst[:, t, :], src[:, t, :], mv[:, z, t, 0:1], rstd[:, z, t:t + 1],
                                        ALU.subtract, ALU.mult)
                i.then_inc(s_done, 1)

            def layer0(m, half, link, first=False, meanwhile=None):
                dve.wait_ge(s_f0, m + 1)
                dve.wait_ge(s_xb, m + 1)
                if not first:
                    dve.wait_ge(s_xo, m - 1)
                V.tensor_tensor(x1[:, half, :, :], rows(bank[2 + half]), x[:, half, :, :], ALU.add).then_inc(s_x1, 1)
                dve.wait_ge(s_x1, m + 1)
                norm_stats(1, x1[:, half, :, :], link, s_var1)
                if meanwhile:
                    meanwhile()
                dve.wait_ge(s_rs1, m + 1)
                if not first:
                    dve.wait_ge(s_t2, m)
                normalise(1, x1[:, half, :, :], x1n, s_x1n)

            def norm0(m, half, count, link, first=False, meanwhile=None):
                dve.wait_ge(s_x[half], 16 * count)
                norm_stats(0, x[:, half, :, :], link, s_var0)
                if meanwhile:
                    meanwhile()
                dve.wait_ge(s_rs0, m + 1)
                if not first:
                    dve.wait_ge(s_t1, m)
                normalise(0, x[:, half, :, :], xn, s_xn)

            def low(dst, src, high, s_done):
                V.tensor_tensor(dst, src, high.bitcast(FP32), ALU.subtract).then_inc(s_done, 1)

            def gated(m, half, first):
                dve.wait_ge(s_tanh, m + 1)
                dve.wait_ge(s_kv, m + 1)
                if not first:
                    dve.wait_ge(s_res, m)
                V.scalar_tensor_tensor(ffn[:, :, :], gate[:, :, :], 1.0, rows(bank[2 + half]),
                                       ALU.add, ALU.mult).then_inc(s_ffn, 1)

            def step(m, b, half, base, more, norm):
                static = isinstance(m, int)
                first = static and m == 0
                link = Chain(dve, s_link, base)

                def mix_low(i):
                    dve.wait_ge(s_mixh[i], m + 1)
                    low(mixs[1][:, i, :, :], mix[:, i, :, :], mixs[0][:, i, :, :], s_mixl[i])

                def add_v_bias():
                    dve.wait_ge(s_v, m + 1)
                    if not (isinstance(b, int) and b == 0):
                        dve.wait_ge(s_v_out[half], 16 * b)
                    for t in range(TPM):
                        i = V.tensor_tensor(v[:, half, t, :, 0:HD],
                                            bank[1][:, t * D:(t + 1) * D].rearrange("p (h d) -> p h d", d=HD),
                                            vbias[:, :].rearrange("p (h d) -> p h d", d=HD), ALU.add)
                    i.then_inc(s_vb, 1)

                dve.wait_ge(s_x1T, m + 1)
                low(x1s[1][:, :, :], chunks(bank[0]), x1s[0][:, :, :], s_x1l)
                if more:
                    dve.wait_ge(s_xT, m + 2)
                    low(xT[1][:, :, :], chunks(bank[1]), xT[0][:, :, :], s_xTl)
                if not first:
                    gated(m - 1, 1 - half, static and m == 1)
                for i in (1, 0):
                    dve.wait_ge(s_xmu, 4 * m + (b + half) + (4 if i == 0 else 2))
                    for k in range(DC):
                        j = V.scalar_tensor_tensor(mix[:, i, k, :], x1T[:, half, k, 0:MS], omu[:, i, k:k + 1],
                                                   mix[:, i, k, :], ALU.mult, ALU.add)
                    j.then_inc(s_mix[i], 1)
                mix_low(1)
                if more:
                    layer0(m + 1, 1 - half, link, meanwhile=lambda: mix_low(0))
                else:
                    mix_low(0)
                if norm:
                    norm0(m + 2, half, b + 2, link, meanwhile=add_v_bias)
                else:
                    add_v_bias()
                dve.wait_ge(s_ksq, m + 1)
                if not first:
                    dve.wait_ge(s_kv, m)
                low(ksq[1][:, :, :], kfull[:, :, :], ksq[0][:, :, :], s_ksl)

            pro = Chain(dve, s_link)
            norm0(0, 0, 1, pro, True)
            dve.wait_ge(s_w, n_w)
            dve.wait_ge(s_wh, 3)
            flat4 = lambda t: t.rearrange("p a k n -> p (a k n)")
            V.tensor_tensor(flat4(w_lo[:, 0:4, :, :]), flat4(full[:, :, :, :]),
                            flat4(w_hi[:, 0:4, :, :]).bitcast(FP32), ALU.subtract).then_inc(s_set, 1)
            V.tensor_tensor(flat4(w_lo[:, 4:6, :, :]), flat4(rest[:, :, :, :])[:, 0:2 * DC * D],
                            flat4(w_hi[:, 4:6, :, :]).bitcast(FP32), ALU.subtract).then_inc(s_set, 1)
            V.scalar_tensor_tensor(w_lo[:, 6, :, :].rearrange("p k n -> p (k n)"),
                                   flat4(rest[:, :, :, :])[:, 2 * DC * D:3 * DC * D], 0.5,
                                   w_hi[:, 6, :, :].rearrange("p k n -> p (k n)").bitcast(FP32),
                                   ALU.mult, ALU.subtract).then_inc(s_set, 1)
            V.tensor_scalar(qbias[:, :], qbias[:, :], HD ** -0.5, None, ALU.mult).then_inc(s_set, 1)
            V.tensor_scalar(omu[:, :, :], mu[:, :, :], -1.0, 1.0, ALU.mult, ALU.add).then_inc(s_set, 1)
            V.tensor_tensor(bias0[:, 0, :], bias0[:, 0, :], bias0[:, 1, :], ALU.add).then_inc(s_set, 1)
            dve.wait_ge(s_set, N_SET)
            dve.wait_ge(s_xT, 1)
            V.tensor_tensor(xT[1][:, :, :], chunks(bank[1]), xT[0][:, :, :].bitcast(FP32),
                            ALU.subtract).then_inc(s_xTl, 1)
            norm0(1, 1, 1, pro)
            layer0(0, 0, pro, True)
            assert pro.n == PRO_LINKS
            step(0, 0, 0, PRO_LINKS, True, True)
            step(1, 0, 1, PRO_LINKS + STEP_LINKS, True, True)
            with dve.Fori(1, B - 1) as b:
                for half in range(2):
                    step(2 * b + half, b, half, PRO_LINKS + STEP_LINKS * (2 * b + half), True, True)
            step(STEPS - 2, B - 1, 0, PRO_LINKS + STEP_LINKS * (STEPS - 2), True, False)
            step(STEPS - 1, B - 1, 1, PRO_LINKS + STEP_LINKS * (STEPS - 2) + 2, False, False)
            gated(STEPS - 1, 1, False)

        @block.gpsimd
        def _(pool):
            pool.memset(neghalf[:, :], -0.5).then_inc(s_neg, 1)
            pool.memset(v[:, :, :, :, HD:VW], 1.0).then_inc(s_set, 1)
            pool.memset(x1T[:, 0, :, 0:1], 0.0).then_inc(s_set, 1)

            def rs0(m):
                pool.wait_ge(s_var0, m + 1)
                pool.tensor_tensor(rstd[:, 0, :], ve[:, 0, :], neghalf[:, :], ALU.pow).then_inc(s_rs0, 1)

            def rs1(m):
                pool.wait_ge(s_var1, m + 1)
                pool.tensor_tensor(rstd[:, 1, :], ve[:, 1, :], neghalf[:, :], ALU.pow).then_inc(s_rs1, 1)

            def with_bias(m, b, half):
                pool.wait_ge(s_xn, m + 1)
                if half == 0:
                    pool.tensor_tensor(x[:, half, :, :], x[:, half, :, :], every(bias0[:, 0, :]), ALU.add).then_inc(s_xbias, 1)
                    pool.wait_ge(s_xbias, b + 1)
                    pool.wait_ge(s_att, 16 * (b + 1))
                    pool.tensor_tensor(x[0:E0, half, 0, :], x[0:E0, half, 0, :], att[:, :], ALU.add).then_inc(s_xb, 1)
                else:
                    pool.tensor_tensor(x[:, half, :, :], x[:, half, :, :], every(bias0[:, 0, :]), ALU.add).then_inc(s_xb, 1)

            def remainder(n, slot, m):
                pool.wait_ge(s_hi[n], m + 1)
                pool.tensor_tensor(rest[:, n, :, :], full[:, n, :, :], part[:, slot, 0, :, :],
                                   ALU.subtract).then_inc(s_res1[n], 1)

            def low_part(n, slot, m):
                pool.wait_ge(s_mid[n], m + 1)
                pool.tensor_tensor(part[:, slot, 2, :, :], rest[:, n, :, :], part[:, slot, 1, :, :],
                                   ALU.subtract).then_inc(s_lo[n], 1)

            def add_ffn(m, half):
                pool.wait_ge(s_xo, m + 1)
                pool.wait_ge(s_ffn, m + 1)
                pool.tensor_tensor(res[:, half, :, :], res[:, half, :, :], ffn[:, :, :], ALU.add).then_inc(s_res, 1)

            def step(m, b, half, first, more, norm):
                remainder(0, 0, m)
                if more:
                    rs1(m + 1)
                if not first:
                    low_part(1, 2 - half, m - 1)
                if not first:
                    add_ffn(m - 1, 1 - half)
                if norm:
                    rs0(m + 2)
                low_part(0, 0, m)
                if not first:
                    pool.wait_ge(s_lo[1], m)
                remainder(1, 1 + half, m)
                if not (isinstance(b, int) and b == 0):
                    pool.wait_ge(s_res_out[half], 16 * b)
                pool.tensor_tensor(res[:, half, :, :], x1[:, half, :, :], every(obias[:, :]), ALU.add).then_inc(s_xo, 1)
                if norm:
                    with_bias(m + 2, b + 1, half)

            pool.wait_ge(s_neg, 1)
            rs0(0)
            pool.wait_ge(s_set, N_SET)
            with_bias(0, 0, 0)
            rs0(1)
            with_bias(1, 0, 1)
            rs1(0)
            step(0, 0, 0, True, True, True)
            step(1, 0, 1, False, True, True)
            with pool.Fori(1, B - 1) as b:
                for half in range(2):
                    step(2 * b + half, b, half, False, True, True)
            step(STEPS - 2, B - 1, 0, False, True, False)
            step(STEPS - 1, B - 1, 1, False, False, False)
            low_part(1, 2, STEPS - 1)
            add_ffn(STEPS - 1, 1)


def quads():
    half = T // 2
    key_side = [(j, 0, P * j, half - P * j) for j in range(QT // 2)]
    key_side += [(j, 1, max(half, P * j), T - max(half, P * j)) for j in range(QT)]
    query_side = [(i, 0, P * (i + 1)) for i in reversed(range(QT // 2))]
    query_side += [(i, 0, half) for i in range(QT // 2, QT)]
    query_side += [(i, half, P * (i + 1) - half) for i in reversed(range(QT // 2, QT))]
    assert [q[3] for q in key_side] == [q[2] for q in query_side]
    return key_side, query_side


KEY_QUADS, QUERY_QUADS = quads()
NQ = len(KEY_QUADS)


def per_bank(n):
    return 512 // n if n in (128, 256) else 1


def masked_by_vector(q):
    i, k0, w = QUERY_QUADS[q]
    return per_bank(w) == 1 and w > P and k0 + w == (i + 1) * P


def body_units(kind):
    at = {}
    for g in range(NG):
        for r in range(NQ):
            todo = []
            ahead, q = divmod(r + LEAD, NQ)
            to = g + 1 + ahead
            if not (kind == "last" and to >= NG):
                for h in range(0, GH, per_bank(QUERY_QUADS[q][2])):
                    todo.append(("max", to, (q, h)))
            if r == 2 and not (kind == "first" and g == 0):
                todo.append(("norm", g - 1, 1))
            if r == 6:
                todo.append(("norm", g, 0))
            if r == NQ + 1 - LEAD and not (kind == "last" and g == NG - 1):
                todo.append(("rows", g + 1, None))
            if g == 0 and kind != "first":
                if r in (4, 5):
                    todo += [("turn", -1, 2 * (r - 4) + u) for u in range(2)]
                if r in (7, 8):
                    todo += [("out", -1, 2 * (r - 7) + u) for u in range(2)]
            at[g, r] = todo
    return at


def attend(nc, a, scr, out):
    ctx = ExitStack()
    with ctx:
        def sb(name, shape, dt=FP32):
            return ctx.enter_context(nc.sbuf_tensor(name, shape, dt))

        def sem(name):
            return ctx.enter_context(nc.semaphore(name))

        ident = sb("t_ident", [P, P])
        identb = sb("t_identb", [P, P], BF16)
        amask = sb("t_amask", [P, P], BF16)
        bmask = sb("t_bmask", [P, P], BF16)
        maskrow = sb("t_maskrow", [P, 512])
        hold = sb("t_hold", [P, 2, NQ, GH])
        ow = sb("t_ow", [P, DC, D])
        q_op = [sb(f"t_q{g}", [P, GH, T], BF16) for g in range(NG)]
        k_op = [sb(f"t_k{g}", [P, GH, T], BF16) for g in range(NG)]
        v = [sb(f"t_v{g}", [P, QT, VPAD], FP32) for g in range(NG)]
        prob = sb("t_prob", [P, 2, GH, 512])
        mx = sb("t_mx", [P, 2, GH, QT])
        mx2 = sb("t_mx2", [P, 2, 2, GH, QT // 2])
        mrest = sb("t_mrest", [P, GH * QT])
        mpart = sb("t_mpart", [P, 3, GH * QT], BF16)
        mrows = sb("t_mrows", [3 * GH * QT, P], BF16)
        yu = sb("t_yu", [P, 2, 512])
        rec = sb("t_rec", [P, 2, GH, GH])
        y = sb("t_y", [P, QT, D])
        yT = [sb(f"t_yT{i}", [P, DC, T], FP32R) for i in range(2)]
        ows = [sb(f"t_ow{i}", [P, DC, D], FP32R) for i in range(2)]
        res = sb("t_res", [P, QT, D])
        o = sb("t_o", [P, QT, D])
        abank = [ctx.enter_context(nc.psum_tensor(f"t_a{i}", [P, 512], FP32)) for i in range(3)]
        abf = [t[:, :].bitcast(BF16) for t in abank]
        bbank = [ctx.enter_context(nc.psum_tensor(f"t_b{i}", [P, 512], FP32)) for i in range(3)]
        ybank = [ctx.enter_context(nc.psum_tensor(f"t_y{i}", [P, 512], FP32)) for i in range(2)]

        s_c0 = sem("t_const_in")
        s_c = [sem(f"t_const_in{g}") for g in range(NG)]
        s_set = sem("t_set")
        s_qk = [sem(f"t_qk_in{g}") for g in range(NG)]
        s_vin = [sem(f"t_v_in{g}") for g in range(NG)]
        s_a = sem("t_a_pe")
        s_au = sem("t_a_used")
        s_b = sem("t_b_pe")
        s_e = sem("t_exp")
        s_pv = sem("t_pv_pe")
        s_yu = sem("t_yu_copied")
        s_mp = sem("t_mpart_ready")
        s_yh = sem("t_yT_hi")
        s_late, s_ow = sem("t_const_in_late"), sem("t_ow_split")
        s_mw = sem("t_mrows_written")
        s_m = [sem(f"t_m_in{g}") for g in range(NG)]
        s_res = sem("t_res_in")
        s_out = sem("t_out_stored")
        s_link = sem("t_dve_link")

        kinds = {k: body_units(k) for k in ("first", "mid", "last")}
        count = {k: sum(map(len, at.values())) for k, at in kinds.items()}
        PRO = [("max", 0, (q, h)) for q in range(NQ) for h in range(0, GH, per_bank(QUERY_QUADS[q][2]))]
        PRO += [("rows", 0, None)]
        PRO += [("max", 1, (q, h)) for q in range(LEAD) for h in range(0, GH, per_bank(QUERY_QUADS[q][2]))]
        TAIL = [("norm", -1, 1)] + [("turn", -1, u) for u in range(4)] + [("out", -1, u) for u in range(4)]
        B_UNITS = NG * sum(GH // per_bank(q[3]) for q in KEY_QUADS)

        def base(kind, b):
            if kind == "first":
                return len(PRO)
            return len(PRO) + count["first"] + count["mid"] * (b - 1)

        TAIL_BASE = len(PRO) + count["first"] + count["mid"] * (B - 2) + count["last"]
        LOADS = 2 * NSLOT

        qs = scr["qs"].rearrange("s b (h d) t -> s b d h t", d=HD)
        ks = scr["ks"].rearrange("s b (h d) t -> s b d h t", d=HD)
        vs = scr["v"].rearrange("b (j p) (g c) -> b g p j c", p=P, g=NG)
        resd = scr["res"].rearrange("b (t p) c -> b p t c", p=P)
        outd = out.rearrange("b (t p) c -> b p t c", p=P)

        def load_q(eng, b, g):
            for s in range(NSLOT):
                at = NPOS + s * HD
                eng.dma_start(q_op[g][at:at + HD, :, :],
                              qs[Q_PART[s], b][:, g * GH:(g + 1) * GH, :]).then_inc(s_qk[g], 16)

        def load_k(eng, b, g):
            for s in range(NSLOT):
                at = NPOS + s * HD
                eng.dma_start(k_op[g][at:at + HD, :, :],
                              ks[K_PART[s], b][:, g * GH:(g + 1) * GH, :]).then_inc(s_qk[g], 16)

        block = ctx.enter_context(nc.Block())

        @block.sync
        def _(sp):
            def load(b, g):
                load_q(sp, b, g)
                load_k(sp, b, g)
                load_v(b, g)

            def load_v(b, g):
                sp.dma_start(v[g][:, :, 0:GH * VW], vs[b, g]).then_inc(s_vin[g], 16)

            def rows(b, g):
                t = NG * b + g
                if isinstance(b, int) and b == 0 and g == 0:
                    sp.wait_ge(s_au, PRO.index(("rows", 0, None)) + 1)
                sp.dma_start(scr["m"][g], mrows[:, :]).then_inc(s_mw, 16)
                sp.wait_ge(s_mw, 16 * (t + 1))
                sp.dma_start(q_op[g][KA:KB, :, :].rearrange("p h t -> p (h t)"),
                             scr["m"][g].rearrange("(s n) q -> s (n q)", s=3)).then_inc(s_m[g], 16)

            def body(kind, b):
                seen = base(kind, b)
                for g in range(NG):
                    for r in range(NQ):
                        for what, to, detail in kinds[kind][g, r]:
                            seen = seen + 1
                            if what == "rows":
                                sp.wait_ge(s_au, seen)
                                rows(b + to // NG, to % NG)
                        if r == 1 and not (kind == "first" and g == 0):
                            done = NG * NQ * b + NQ * g
                            if g > 0 and kind != "last":
                                sp.wait_ge(s_pv, done)
                                load(b + 1, g - 1)
                            if g == 0:
                                sp.wait_ge(s_pv, done)
                                load(b, NG - 1)

            for g in range(NG):
                sp.dma_start(q_op[g][0:NPOS, :, :], a["q_pos"][:, g * GH:(g + 1) * GH, :]).then_inc(s_c[g], 16)
                load_q(sp, 0, g)
                if g == 0:
                    sp.dma_start(identb[:, :], a["identb"]).then_inc(s_c0, 16)
            for g in range(NG):
                load_v(0, g)
            rows(0, 0)
            body("first", 0)
            with sp.Fori(1, B - 1) as b:
                body("mid", b)
            body("last", B - 1)

        @block.tensor
        def _(pe):
            def a_unit(what, to, detail, n, seen, b, seen_norm):
                bk = abank[n]
                if what == "max":
                    g = to % NG
                    q, h0 = detail
                    i, k0, w = QUERY_QUADS[q]
                    for s in range(per_bank(w)):
                        h = h0 + s
                        piece = bk[:, s * w:(s + 1) * w]
                        diagonal = k0 + w == (i + 1) * P and not masked_by_vector(q)
                        mm = pe.matmul(piece, q_op[g][0:KA, h, i * P:(i + 1) * P], k_op[g][0:KA, h, k0:k0 + w],
                                       start=True, stop=not diagonal)
                        if diagonal:
                            mm = pe.matmul(piece[:, w - P:w], identb[:, :], amask[:, :], start=False, stop=True)
                elif what == "rows":
                    pe.wait_ge(s_mp, NG * b + to + 1)
                    mm = pe.transpose(abf[n][0:3 * GH * QT, 0:P], mpart[:, :, :].rearrange("p s n -> p (s n)"), identb[:, :])
                elif what == "norm":
                    pe.wait_ge(s_yu, 2 * (NG * b + to) + detail + 1)
                    for t in range(4):
                        mm = pe.transpose(bk[:, t * P:(t + 1) * P], yu[:, detail, t * P:(t + 1) * P], ident[:, :])
                elif what == "turn":
                    pe.wait_ge(s_au, seen_norm)
                    k, half = divmod(detail, 2)
                    for t in range(4):
                        mm = pe.transpose(bk[:, t * P:(t + 1) * P], y[:, half * 4 + t, k * P:(k + 1) * P], ident[:, :])
                else:
                    pe.wait_ge(s_au, seen_norm)
                    for s in range(2):
                        t = 2 * detail + s
                        terms = [(k, x, z) for k in range(DC) for x, z in ((0, 0), (0, 1), (1, 0))]
                        for m, (k, x, z) in enumerate(terms):
                            mm = pe.matmul(bk[:, s * D:(s + 1) * D], yT[x][:, k, t * P:(t + 1) * P], ows[z][:, k, :],
                                           start=(m == 0), stop=(m == len(terms) - 1))
                mm.then_inc(s_a, 1)

            def run(units, start, n0, b, last_of):
                for n, (what, to, detail) in enumerate(units, n0):
                    pe.wait_ge(s_au, start + max(n - 2, 0))
                    if what == "max" and detail == (0, 0):
                        if isinstance(b, int) and b == 0 and to < NG:
                            pe.wait_ge(s_c[to], 16 * 3)
                        pe.wait_ge(s_qk[to % NG], 16 * LOADS * (b + to // NG + 1))
                    if what == "norm":
                        last_of["norm"] = start + n + 1
                    if what == "turn":
                        last_of["turn"] = start + n + 1
                    a_unit(what, to, detail, n % 3, start + n, b,
                           last_of.get("norm" if what == "turn" else "turn"))

            def body(kind, b):
                at, start, n0, u0, last_of = kinds[kind], base(kind, b), 0, 0, {}
                for g in range(NG):
                    t = NG * b + g
                    for r in range(NQ):
                        j, c, q0, w = KEY_QUADS[r]
                        todo = list(at[g, r])
                        maxes = [u for u in todo if u[0] == "max"]
                        if r == 0:
                            pe.wait_ge(s_m[g], 16 * (b + 1))
                            pe.wait_ge(s_vin[g], 16 * (b + 1))
                        pieces = list(range(0, GH, per_bank(w)))
                        for x, h0 in enumerate(pieces):
                            if maxes:
                                run([maxes.pop(0)], start, n0, b, last_of)
                                n0 += 1
                            pe.wait_ge(s_e, B_UNITS * b + max(u0 - 2, 0))
                            for s in range(per_bank(w)):
                                h = h0 + s
                                piece = bbank[u0 % 3][:, s * w:(s + 1) * w]
                                diagonal = q0 == j * P
                                mm = pe.matmul(piece, k_op[g][0:KB, h, j * P:(j + 1) * P], q_op[g][0:KB, h, q0:q0 + w],
                                               start=True, stop=not diagonal)
                                if diagonal:
                                    mm = pe.matmul(piece[:, 0:P], identb[:, :], bmask[:, :], start=False, stop=True)
                            mm.then_inc(s_b, 1)
                            u0 += 1
                            if x == min(1, len(pieces) - 1):
                                weigh(kind, b, g, r - 1, u0 - x - 1)
                        rest = maxes + [u for u in todo if u[0] != "max"]
                        run(rest, start, n0, b, last_of)
                        n0 += len(rest)
                if kind == "last":
                    weigh(kind, b, NG, -1, u0)
                assert n0 == count[kind] and u0 == B_UNITS

            def weigh(kind, b, g, r, units):
                if r < 0:
                    if kind == "first" and g == 0:
                        return
                    r, g = NQ - 1, g - 1
                j, c, q0, w = KEY_QUADS[r]
                pe.wait_ge(s_e, B_UNITS * b + units)
                if j == 0 and not (kind == "first" and g == 0):
                    pe.wait_ge(s_yu, 2 * (NG * b + g - 1) + c + 1)
                for h in range(GH):
                    mm = pe.matmul(ybank[c][32 * h:32 * h + 32, q0 - 512 * c:q0 - 512 * c + w],
                                   v[g % NG][:, j, h * VW:h * VW + 32], prob[:, r % 2, h, 0:w],
                                   start=(j == 0), stop=(j == (QT // 2 if c == 0 else QT) - 1))
                mm.then_inc(s_pv, 1)

            pe.wait_ge(s_c0, 16 * 3)
            pe.wait_ge(s_set, 1)
            run(PRO, 0, 0, 0, {})
            pe.wait_ge(s_late, 16 * 3)
            pe.wait_ge(s_ow, 2)
            body("first", 0)
            with pe.Fori(1, B - 1) as b:
                body("mid", b)
            body("last", B - 1)
            run(TAIL, TAIL_BASE, 0, B, {})

        @block.scalar
        def _(act):
            LAST_OUT = {k: 1 + max(n for n, u in enumerate(u for g in range(NG) for r in range(NQ) for u in at[g, r])
                                   if u[0] == "out") for k, at in kinds.items() if k != "first"}

            def turned_high(detail, n, seen):
                k, half = divmod(detail, 2)
                act.wait_ge(s_a, seen)
                nc.scalar.copy(yT[0][:, k, half * 512:(half + 1) * 512], abank[n % 3][:, :]).then_inc(s_yh, 1)

            def copy_y(b, g, c):
                t = NG * b + g
                act.wait_ge(s_pv, NQ * t + (4 if c == 0 else NQ))
                nc.scalar.copy(yu[:, c, :], ybank[c][:, :]).then_inc(s_yu, 1)

            def body(kind, b):
                seen, u0, n = base(kind, b), 0, 0
                used = {} if kind == "first" else {0: seen, 1: seen}
                for g in range(NG):
                    if g == 0 and kind != "first":
                        act.wait_ge(s_au, base(kind, b))
                        act.dma_start(res[:, :, :], resd[b - 1]).then_inc(s_res, 16)
                    if g == 1 and kind != "first":
                        act.wait_ge(s_au, base(kind, b) + LAST_OUT[kind])
                        act.dma_start(outd[b - 1], o[:, :, :]).then_inc(s_out, 16)
                    for r in range(NQ):
                        j, c, q0, w = KEY_QUADS[r]
                        if not (kind == "first" and g == 0 and r < 2):
                            act.wait_ge(s_pv, NG * NQ * b + NQ * g + r - 1)
                        for h0 in range(0, GH, per_bank(w)):
                            act.wait_ge(s_b, B_UNITS * b + u0 + 1)
                            m = per_bank(w)
                            nc.scalar.activation(prob[:, r % 2, h0:h0 + m, 0:w],
                                                 bbank[u0 % 3][:, 0:m * w].rearrange("p (h n) -> p h n", h=m),
                                                 ACT.Exp).then_inc(s_e, 1)
                            u0 += 1
                        for what, to, detail in kinds[kind][g, r]:
                            seen = seen + 1
                            if what == "norm":
                                used[detail] = seen
                            if what == "turn":
                                turned_high(detail, n, seen)
                            n += 1
                        if r == 0 and not (kind == "first" and g == 0):
                            if used.get(1) is not None:
                                act.wait_ge(s_au, used[1])
                            copy_y(b, g - 1, 1)
                        if r == 4:
                            if used.get(0) is not None:
                                act.wait_ge(s_au, used[0])
                            copy_y(b, g, 0)

            for g in range(NG):
                act.dma_start(k_op[g][0:NPOS, :, :], a["k_pos"]).then_inc(s_c[g], 16)
                load_k(act, 0, g)
                if g == 0:
                    act.dma_start(amask[:, :], a["amask"]).then_inc(s_c0, 16)
                    act.dma_start(maskrow[:, :], a["maskrow"]).then_inc(s_c0, 16)
                act.dma_start(k_op[g][KA:KB, :, :], a["k_one"]).then_inc(s_c[g], 16)
            act.dma_start(bmask[:, :], a["bmask"]).then_inc(s_late, 16)
            act.dma_start(ident[:, :], a["ident"]).then_inc(s_late, 16)
            act.dma_start(ow[:, :, :], a["o_w"].rearrange("(k p) n -> p k n", p=P)).then_inc(s_late, 16)
            act.wait_ge(s_late, 16 * 3)
            nc.scalar.copy(ows[0][:, :, :], ow[:, :, :]).then_inc(s_ow, 1)
            act.wait_ge(s_set, 1)
            body("first", 0)
            with act.Fori(1, B - 1) as b:
                body("mid", b)
            body("last", B - 1)
            act.wait_ge(s_au, TAIL_BASE)
            act.dma_start(res[:, :, :], resd[B - 1]).then_inc(s_res, 16)
            copy_y(B - 1, NG - 1, 1)
            for n, (what, to, detail) in enumerate(TAIL):
                if what == "turn":
                    turned_high(detail, n, TAIL_BASE + n + 1)
            act.wait_ge(s_au, TAIL_BASE + len(TAIL))
            act.dma_start(outd[B - 1], o[:, :, :]).then_inc(s_out, 16)
            act.wait_ge(s_out, 16 * B)

        @block.vector
        def _(dve):
            V = nc.vector

            def unit(kind, what, to, detail, n, seen, b, link):
                bk = abank[n]
                dve.wait_ge(s_a, seen + 1)
                if what == "max":
                    z = to % 2
                    q, h0 = detail
                    i, k0, w = QUERY_QUADS[q]
                    m = per_bank(w)
                    dst = mx[:, z, h0:h0 + m, i] if i < QT // 2 else mx2[:, z, k0 // 512, h0:h0 + m, i - QT // 2]
                    if masked_by_vector(q):
                        V.memset(hold[:, z, q, h0:h0 + 1], 0.0)
                        V.tensor_tensor_reduce(out=bk[:, 0:w], in0=bk[:, 0:w], in1=maskrow[:, 512 - w:512], scale=1.0,
                                               scalar=-3.0e38, op0=ALU.add, op1=ALU.max, accum_out=dst).then_inc(s_au, 1)
                    else:
                        V.tensor_reduce(dst, bk[:, 0:m * w].rearrange("p (h n) -> p h n", h=m), AX.X,
                                        ALU.max).then_inc(s_au, 1)
                    if q == NQ - 1 and h0 + m == GH:
                        parts(to, seen + 1, link, b)
                elif what == "rows":
                    if not (isinstance(b, int) and b == 0 and to == 0):
                        dve.wait_ge(s_mw, 16 * (NG * b + to))
                    V.tensor_copy(mrows[:, :], abf[n][0:3 * GH * QT, 0:P]).then_inc(s_au, 1)
                elif what == "norm":
                    piece = bk[:, :].rearrange("p (t h n) -> p t h n", t=4, h=GH)
                    link(V.reciprocal(rec[:, detail, :, :], piece[:, :, :, HD]))
                    g = to % NG
                    for t in range(4):
                        i = V.tensor_tensor(
                            y[:, 4 * detail + t, g * GH * HD:(g + 1) * GH * HD].rearrange("p (h d) -> p h d", d=HD),
                            piece[:, t, :, 0:HD],
                            rec[:, detail, t, :].rearrange("p (h o) -> p h o", o=1).to_broadcast([P, GH, HD]), ALU.mult)
                    i.then_inc(s_au, 1)
                elif what == "turn":
                    k, half = divmod(detail, 2)
                    cols = slice(half * 512, (half + 1) * 512)
                    dve.wait_ge(s_yh, 4 * ((b if kind != "tail" else B) - 1) + detail + 1)
                    V.tensor_tensor(yT[1][:, k, cols], bk[:, :], yT[0][:, k, cols].bitcast(FP32),
                                    ALU.subtract).then_inc(s_au, 1)
                else:
                    if detail == 0:
                        dve.wait_ge(s_res, 16 * b)
                        if not (isinstance(b, int) and b == 1):
                            dve.wait_ge(s_out, 16 * (b - 1))
                    V.tensor_tensor(o[:, 2 * detail:2 * detail + 2, :], bk[:, :].rearrange("p (t n) -> p t n", t=2),
                                    res[:, 2 * detail:2 * detail + 2, :], ALU.add).then_inc(s_au, 1)

            def parts(to, seen, link, b):
                z = to % 2
                dve.wait_ge(s_au, seen)
                link(V.tensor_tensor(mx[:, z, :, QT // 2:QT], mx2[:, z, 0, :, :], mx2[:, z, 1, :, :], ALU.max))
                flat = mx[:, z, :, :].rearrange("p h i -> p (h i)")
                link(V.tensor_scalar(mpart[:, 0, :], flat, -1.0, None, ALU.mult))
                link(V.scalar_tensor_tensor(mrest[:, :], flat, -1.0, mpart[:, 0, :], ALU.mult, ALU.subtract))
                link(V.tensor_copy(mpart[:, 1, :], mrest[:, :]))
                V.tensor_tensor(mpart[:, 2, :], mrest[:, :], mpart[:, 1, :], ALU.subtract).then_inc(s_mp, 1)

            def links_of(units):
                return sum(4 if (w == "max" and d[0] == NQ - 1 and d[1] + per_bank(QUERY_QUADS[d[0]][2]) == GH)
                           else 1 if w == "norm" else 0 for w, _, d in units)

            in_body = {k: [u for g in range(NG) for r in range(NQ) for u in at[g, r]] for k, at in kinds.items()}
            n_links = {k: links_of(u) for k, u in in_body.items()}

            def body(kind, b):
                start = base(kind, b)
                lb = links_of(PRO) if kind == "first" else links_of(PRO) + n_links["first"] + n_links["mid"] * (b - 1)
                link = Chain(dve, s_link, lb)
                for n, (what, to, detail) in enumerate(in_body[kind]):
                    unit(kind, what, to, detail, n % 3, start + n, b, link)
                assert link.n == n_links[kind]

            for g in range(NG):
                i = V.memset(v[g][:, :, GH * VW:VPAD], 0.0)
            i.then_inc(s_set, 1)
            dve.wait_ge(s_set, 1)
            pro = Chain(dve, s_link)
            for n, (what, to, detail) in enumerate(PRO):
                unit("pro", what, to, detail, n % 3, n, 0, pro)
            dve.wait_ge(s_ow, 1)
            V.tensor_tensor(ows[1][:, :, :], ow[:, :, :], ows[0][:, :, :].bitcast(FP32), ALU.subtract).then_inc(s_ow, 1)
            body("first", 0)
            with dve.Fori(1, B - 1) as b:
                body("mid", b)
            body("last", B - 1)
            link = Chain(dve, s_link, links_of(PRO) + n_links["first"] + n_links["mid"] * (B - 2) + n_links["last"])
            for n, (what, to, detail) in enumerate(TAIL):
                unit("tail", what, to, detail, n % 3, TAIL_BASE + n, B, link)


def kernel(**inputs):
    import numpy as np
    import concourse.bacc as bacc
    from concourse.bass_utils import run_bass_kernel_spmd as run

    nc = bacc.Bacc("TRN2", target_bir_lowering=False, num_devices=1)
    arrays, a = {}, {}

    def give(name, array):
        array = np.ascontiguousarray(array)
        arrays[f"in_{name}"] = array
        a[name] = nc.dram_tensor(f"in_{name}", array.shape, mybir.dt.from_np(array.dtype), kind="ExternalInput").ap()

    turned = {"WqT": "L0_attn_Wq", "WkT": "L0_attn_Wk", "WvT": "L0_attn_Wv", "WoT": "L0_attn_Wo",
              "W0T": "L0_ffn_W",
              "ldT": "L0_ffn_lora_down", "luT": "L0_ffn_lora_up", "uaT": "L0_ffn_up_aux",
              "WrT": "L1_ffn_W_r", "WkkT": "L1_ffn_W_k", "WvvT": "L1_ffn_W_v"}
    plain = {"x": "L0_attn_x", "bo": "L0_attn_bo", "lna_w": "L0_attn_lna_w",
             "down_aux": "L0_ffn_down_aux", "b0": "L0_ffn_b", "q_w": "L1_attn_q_w",
             "kv_w": "L1_attn_kv_w", "kv_b": "L1_attn_kv_b", "o_w": "L1_attn_o_w", "o_b": "L1_attn_o_b"}
    for name, of in turned.items():
        give(name, np.asarray(inputs[of]).T)
    for name, of in plain.items():
        give(name, inputs[of])
    for name in ("temp", "threshold", "factor"):
        give(name, np.asarray(inputs["L0_attn_" + name]).reshape(1))

    per_head = lambda names: np.stack([np.tile(np.asarray(inputs["L0_attn_" + n]), HPC) for n in names], axis=1)
    give("wl_rep", np.stack([np.tile(np.asarray(inputs["L0_attn_" + n]).T, (HPC, 1)) for n in ("Wlq", "Wlk", "Wlv")], axis=1))
    give("bl_rep", per_head(("blq", "blk", "blv")))
    give("lnw_rep", per_head(("lnc_w", "lnd_w")))

    for name, vec in (("mu_r_col", inputs["L1_ffn_mu_r"]), ("mu_k_col", inputs["L1_ffn_mu_k"]),
                      ("bq_col", inputs["L0_attn_bq"]), ("bv_col", inputs["L0_attn_bv"]),
                      ("q_b_col", inputs["L1_attn_q_b"]), ("k_b_col", np.asarray(inputs["L1_attn_kv_b"])[0:D])):
        give(name, np.asarray(vec).reshape(DC, P).T)

    bf16 = np.dtype("bfloat16")
    p = np.arange(P)
    t = np.arange(T)
    head = np.arange(1, NH + 1)
    later = np.where(p[None, :] > p[:, None], BIG, 0.0)
    give("ident", np.eye(P, dtype=np.float32))
    give("identb", np.eye(P).astype(bf16))
    give("amask", later.astype(bf16))
    give("bmask", later.T.astype(bf16))
    give("maskrow", np.concatenate([np.zeros((P, 512 - P)), later], axis=1).astype(np.float32))
    give("headmask", (p[:, None] // HD == np.arange(HPC)[None, :]).astype(np.float32))
    k_pos = np.stack([t - t % 8, t % 8, np.full(T, 8)]).astype(bf16)
    slope = np.broadcast_to(head[:, None] / NH, (NH, T))
    q_pos = np.stack([slope, slope, -head[:, None] * (t // P)[None, :]]).astype(bf16)
    give("k_pos", np.broadcast_to(k_pos[:, None, :], (NPOS, GH, T)))
    give("k_one", np.ones((3, GH, T)).astype(bf16))
    give("q_pos", q_pos)

    def scratch(name, shape, dt=FP32):
        return nc.dram_tensor(name, shape, dt, kind="Internal").ap()

    scr = {"w0": scratch("scr_w0", (D, D)), "attn0": scratch("scr_attn0", (B * E0, D)),
           "qs": scratch("scr_q", (3, B, D, T), BF16), "ks": scratch("scr_k", (3, B, D, T), BF16),
           "v": scratch("scr_v", (B, T, NH * VW)), "res": scratch("scr_res", (B, T, D)),
           "m": scratch("scr_m", (NG, 3 * GH * QT, P), BF16)}
    out = nc.dram_tensor("out", (B, T, D), FP32, kind="ExternalOutput").ap()
    prepare(nc, a, scr)
    project(nc, a, scr)
    attend(nc, a, scr, out)
    r = run(nc, [arrays], core_ids=[0])
    return r.results[0]["out"]
```
